# Optimizing a Trainium2 kernel written in Bass

```python
import numpy as np
import jax
import jax.numpy as jnp

def _softmax(x, axis=-1):
    return jax.nn.softmax(x, axis=axis)

def _gelu(x):
    return jax.nn.gelu(x, approximate=True)

def _silu(x):
    return jax.nn.silu(x)

def _sigmoid(x):
    return jax.nn.sigmoid(x)

def _layernorm(x, axis=-1, eps=1e-05):
    m = jnp.mean(x, axis=axis, keepdims=True)
    v = jnp.var(x, axis=axis, keepdims=True)
    return (x - m) / jnp.sqrt(v + eps)

def _scatter_add(tgt, idx, src, axis=0):
    return tgt.at[idx].add(src)

def _segment_sum(src, seg, n):
    return jax.ops.segment_sum(src, seg, n)
kernel_name = 'mk_flamingo_gated_d1_seqx_r4_d37100'

def setup_inputs(seed: int=0):
    np.random.seed(seed)
    _w = jnp.asarray

    def _rec_inputs():
        import jax
        import jax.numpy as jnp
        _rk = jax.random.key(seed)
        x = 7.22e-05 + 1 * jax.random.normal(jax.random.fold_in(_rk, 1), (2, 1024, 256), jnp.float32)
        _lenS = 1024 - jax.random.randint(jax.random.fold_in(_rk, 7), (2,), 0, max(1, 1024 // 4) + 1, jnp.int32)
        _lenS2 = 154 - jax.random.randint(jax.random.fold_in(_rk, 8), (2,), 0, max(1, 154 // 4) + 1, jnp.int32)
        _ctx_1024P = jax.random.normal(jax.random.fold_in(_rk, 11), (2, 16, 256), jnp.float32)
        _ctx_1024c = jax.random.dirichlet(jax.random.fold_in(_rk, 511), 0.3 * jnp.ones((16,), jnp.float32), (2, 154))
        _ctx_1024t = jnp.einsum('bsk,bkd->bsd', _ctx_1024c, _ctx_1024P)
        _ctx_1024t = _ctx_1024t * jax.lax.rsqrt(jnp.mean(jnp.square(_ctx_1024t)) + 1e-12) * 0.953939
        ctx_1024 = 4.13588e-05 + 0.999923 * (_ctx_1024t + 0.3 * jax.random.normal(jax.random.fold_in(_rk, 611), (2, 154, 256), jnp.float32))
        _validS = jnp.arange(1024)[None, :] < _lenS[:, None]
        _validS2 = jnp.arange(154)[None, :] < _lenS2[:, None]
        _causal = jnp.tril(jnp.ones((1024, 1024), dtype=bool))
        mask_BxSxS2_ik1 = jnp.where(jnp.broadcast_to(_validS2[:, None, :], (2, 1024, 154)), 1, 0).astype(jnp.int32)
        _g = jax.random.normal(jax.random.fold_in(_rk, 9001), (2, 1), jnp.float32)
        _g = jnp.sign(_g) * jnp.maximum(jnp.abs(_g), 1.0) + (_g == 0) * 1.0
        g_xattn = _g[0]
        g_ffn = _g[1]
        return (x, ctx_1024, mask_BxSxS2_ik1, g_xattn, g_ffn)
    x, ctx_1024, mask_BxSxS2_ik1, g_xattn, g_ffn = _rec_inputs()

    def _L0_xattn_setup():
        import jax, jax.numpy as jnp
        import numpy as np
        DIM = 256
        NUM_HEADS = 16
        key = jax.random.key(seed)
        ks = jax.random.split(key, 10)
        b, t, s, d = (4, 512, 512, DIM)
        scale = 1.0 / np.sqrt(d)
        return {'q': jax.random.normal(ks[0], (b, t, d), jnp.float32), 'k': jax.random.normal(ks[1], (b, s, d), jnp.float32), 'v': jax.random.normal(ks[2], (b, s, d), jnp.float32), 'attention_mask': jax.random.randint(ks[3], (b, t, s), 0, 2, jnp.int32), 'Wq': jax.random.normal(ks[4], (d, d), jnp.float32) * scale, 'bq': jnp.zeros((d,), jnp.float32), 'Wk': jax.random.normal(ks[5], (d, d), jnp.float32) * scale, 'bk': jnp.zeros((d,), jnp.float32), 'Wv': jax.random.normal(ks[6], (d, d), jnp.float32) * scale, 'bv': jnp.zeros((d,), jnp.float32)}
    _L0_xattn_all = _L0_xattn_setup()
    _L0_xattn_in = {k: v for k, v in _L0_xattn_all.items() if k in ('Wq', 'bq', 'Wk', 'bk', 'Wv', 'bv')}
    del _L0_xattn_all

    def _L0_ffn_setup():
        import jax, jax.numpy as jnp
        import numpy as np
        import math
        N_EMBD = 256
        HIDDEN = 4 * N_EMBD
        N_EXPERTS = 8
        TOP_K = 2
        B, T = (4, 512)

        def new_gelu(x):
            c = math.sqrt(2.0 / math.pi)
            return 0.5 * x * (1.0 + jnp.tanh(c * (x + 0.044715 * x * x * x)))

        def _moe_forward(x, Wfc_s, bfc_s, Wproj_s, bproj_s, Wr, Wfc, bfc, Wproj, bproj):
            Bb, Tt, C = x.shape
            xf = x.reshape(Bb * Tt, C)
            N = Bb * Tt
            shared = new_gelu(xf @ Wfc_s + bfc_s) @ Wproj_s + bproj_s
            logits = xf @ Wr
            probs = jax.nn.softmax(logits, axis=-1)
            topk_p, topk_i = jax.lax.top_k(probs, TOP_K)
            topk_p = topk_p / jnp.sum(topk_p, axis=-1, keepdims=True)
            gate = jnp.zeros((N, N_EXPERTS), dtype=xf.dtype)
            gate = gate.at[jnp.arange(N)[:, None], topk_i].add(topk_p)
            routed = jnp.zeros_like(xf)
            for e in range(N_EXPERTS):
                h = new_gelu(xf @ Wfc[e] + bfc[e]) @ Wproj[e] + bproj[e]
                routed = routed + h * gate[:, e:e + 1]
            return (shared + routed).reshape(Bb, Tt, C)
        key = jax.random.key(seed)
        ks = jax.random.split(key, 10)
        s = 0.02
        return {'x': jax.random.normal(ks[0], (B, T, N_EMBD), dtype=jnp.float32), 'Wfc_s': jax.random.normal(ks[1], (N_EMBD, HIDDEN), dtype=jnp.float32) * s, 'bfc_s': jnp.zeros((HIDDEN,), dtype=jnp.float32), 'Wproj_s': jax.random.normal(ks[2], (HIDDEN, N_EMBD), dtype=jnp.float32) * s, 'bproj_s': jnp.zeros((N_EMBD,), dtype=jnp.float32), 'Wr': jax.random.normal(ks[3], (N_EMBD, N_EXPERTS), dtype=jnp.float32) * s, 'Wfc': jax.random.normal(ks[4], (N_EXPERTS, N_EMBD, HIDDEN), dtype=jnp.float32) * s, 'bfc': jnp.zeros((N_EXPERTS, HIDDEN), dtype=jnp.float32), 'Wproj': jax.random.normal(ks[5], (N_EXPERTS, HIDDEN, N_EMBD), dtype=jnp.float32) * s, 'bproj': jnp.zeros((N_EXPERTS, N_EMBD), dtype=jnp.float32)}
    _L0_ffn_all = _L0_ffn_setup()
    _L0_ffn_in = {k: v for k, v in _L0_ffn_all.items() if k in ('Wfc_s', 'bfc_s', 'Wproj_s', 'bproj_s', 'Wr', 'Wfc', 'bfc', 'Wproj', 'bproj')}
    del _L0_ffn_all
    return {'x': x, 'ctx_1024': ctx_1024, 'mask_BxSxS2_ik1': mask_BxSxS2_ik1, 'g_xattn': g_xattn, 'g_ffn': g_ffn, 'L0_xattn_Wq': _L0_xattn_in['Wq'], 'L0_xattn_bq': _L0_xattn_in['bq'], 'L0_xattn_Wk': _L0_xattn_in['Wk'], 'L0_xattn_bk': _L0_xattn_in['bk'], 'L0_xattn_Wv': _L0_xattn_in['Wv'], 'L0_xattn_bv': _L0_xattn_in['bv'], 'L0_ffn_Wfc_s': _L0_ffn_in['Wfc_s'], 'L0_ffn_bfc_s': _L0_ffn_in['bfc_s'], 'L0_ffn_Wproj_s': _L0_ffn_in['Wproj_s'], 'L0_ffn_bproj_s': _L0_ffn_in['bproj_s'], 'L0_ffn_Wr': _L0_ffn_in['Wr'], 'L0_ffn_Wfc': _L0_ffn_in['Wfc'], 'L0_ffn_bfc': _L0_ffn_in['bfc'], 'L0_ffn_Wproj': _L0_ffn_in['Wproj'], 'L0_ffn_bproj': _L0_ffn_in['bproj']}

def reference(x, ctx_1024, mask_BxSxS2_ik1, g_xattn, g_ffn, L0_xattn_Wq, L0_xattn_bq, L0_xattn_Wk, L0_xattn_bk, L0_xattn_Wv, L0_xattn_bv, L0_ffn_Wfc_s, L0_ffn_bfc_s, L0_ffn_Wproj_s, L0_ffn_bproj_s, L0_ffn_Wr, L0_ffn_Wfc, L0_ffn_bfc, L0_ffn_Wproj, L0_ffn_bproj):
    import jax
    import jax.numpy as jnp

    def _L0_xattn_ref(q, k, v, attention_mask, Wq, bq, Wk, bk, Wv, bv):
        import jax, jax.numpy as jnp
        import numpy as np
        DIM = 256
        NUM_HEADS = 16
        b, t_q, d = q.shape
        _, t_kv, _ = k.shape
        h = NUM_HEADS
        qp = (q @ Wq.T + bq).reshape(b, t_q, h, d // h).transpose(0, 2, 1, 3)
        kp = (k @ Wk.T + bk).reshape(b, t_kv, h, d // h).transpose(0, 2, 1, 3)
        vp = (v @ Wv.T + bv).reshape(b, t_kv, h, d // h).transpose(0, 2, 1, 3)
        scores = jnp.einsum('bhqd,bhkd->bhqk', qp, kp) / jnp.sqrt(jnp.float32(d))
        mask = (attention_mask == 1)[:, None, :, :]
        scores = jnp.where(mask, -jnp.inf, scores)
        attn = jax.nn.softmax(scores, axis=-1)
        out = jnp.einsum('bhqk,bhkd->bhqd', attn, vp)
        return out.transpose(0, 2, 1, 3).reshape(b, t_q, d)

    def _L0_ffn_ref(x, Wfc_s, bfc_s, Wproj_s, bproj_s, Wr, Wfc, bfc, Wproj, bproj):
        import jax, jax.numpy as jnp
        import numpy as np
        import math
        N_EMBD = 256
        HIDDEN = 4 * N_EMBD
        N_EXPERTS = 8
        TOP_K = 2
        B, T = (4, 512)

        def new_gelu(x):
            c = math.sqrt(2.0 / math.pi)
            return 0.5 * x * (1.0 + jnp.tanh(c * (x + 0.044715 * x * x * x)))

        def _moe_forward(x, Wfc_s, bfc_s, Wproj_s, bproj_s, Wr, Wfc, bfc, Wproj, bproj):
            Bb, Tt, C = x.shape
            xf = x.reshape(Bb * Tt, C)
            N = Bb * Tt
            shared = new_gelu(xf @ Wfc_s + bfc_s) @ Wproj_s + bproj_s
            logits = xf @ Wr
            probs = jax.nn.softmax(logits, axis=-1)
            topk_p, topk_i = jax.lax.top_k(probs, TOP_K)
            topk_p = topk_p / jnp.sum(topk_p, axis=-1, keepdims=True)
            gate = jnp.zeros((N, N_EXPERTS), dtype=xf.dtype)
            gate = gate.at[jnp.arange(N)[:, None], topk_i].add(topk_p)
            routed = jnp.zeros_like(xf)
            for e in range(N_EXPERTS):
                h = new_gelu(xf @ Wfc[e] + bfc[e]) @ Wproj[e] + bproj[e]
                routed = routed + h * gate[:, e:e + 1]
            return (shared + routed).reshape(Bb, Tt, C)
        return _moe_forward(x, Wfc_s, bfc_s, Wproj_s, bproj_s, Wr, Wfc, bfc, Wproj, bproj)
    x = x + jnp.tanh(g_xattn[0]) * _L0_xattn_ref(_layernorm(x, axis=-1), ctx_1024, ctx_1024, mask_BxSxS2_ik1, L0_xattn_Wq, L0_xattn_bq, L0_xattn_Wk, L0_xattn_bk, L0_xattn_Wv, L0_xattn_bv)
    x = x + jnp.tanh(g_ffn[0]) * _L0_ffn_ref(_layernorm(x, axis=-1), L0_ffn_Wfc_s, L0_ffn_bfc_s, L0_ffn_Wproj_s, L0_ffn_bproj_s, L0_ffn_Wr, L0_ffn_Wfc, L0_ffn_bfc, L0_ffn_Wproj, L0_ffn_bproj)
    return x

_drawn_inputs = setup_inputs


def setup_inputs(seed=0):
    import zlib

    import numpy as np

    out = dict(_drawn_inputs(seed))
    spreads = {'L0_xattn_bq': (0.0, 0.8),
     'L0_xattn_bk': (0.0, 0.8),
     'L0_xattn_bv': (0.0, 0.1),
     'L0_ffn_bfc_s': (0.0, 0.1),
     'L0_ffn_bproj_s': (0.0, 0.1),
     'L0_ffn_bfc': (0.0, 0.372),
     'L0_ffn_bproj': (0.0, 0.1)}
    factors = {}
    for name, (base, spread) in spreads.items():
        noise = np.random.default_rng([zlib.crc32(name.encode()), seed]).standard_normal(out[name].shape)
        drawn = base * np.exp(spread * noise) if base else spread * noise
        out[name] = jnp.asarray(drawn.astype(out[name].dtype))
    for name, factor in factors.items():
        out[name] = (out[name] * factor).astype(out[name].dtype)
    return out
```

```python
from contextlib import ExitStack

import concourse.bass as bass
from concourse import mybir

FP32 = mybir.dt.float32
FP32R = mybir.dt.float32r
INT32 = mybir.dt.int32
ALU = mybir.AluOpType
ACT = mybir.ActivationFunctionType
AX = mybir.AxisListType

P = 128
B, T, D = 2, 1024, 256
KV = 154
H, HD = 16, 16
NE = 8
TILES = B * T // P
GT = 4
GROUPS = TILES // GT
GN = GT * P
KC = D // P
HALVES = H * HD // P
HH = H // HALVES
HW = HH * KV
HEADS = [(0, 3), (3, 3), (6, 2)]
NCH = -(-HW // P)
CHROWS = [min(P, HW - P * c) for c in range(NCH)]
CHUNKS = [(0, 4), (4, 4), (8, 2)]
STEPS = HALVES * GT
NB = len(HEADS)
KVR = KV - P
MASKED = 1e30
HID = 4 * D
HC = HID // P
PAIRS = HC // 2
TOPK = 2
BT = 2
BN = BT * P
SHARED = TILES // BT
BLOCKS = TILES * TOPK // BT + NE - 1
ROWS = BLOCKS * BN
EPS = 1e-5
SQ = -1.0 / 16.0


def build(nc, x, ctx_kv, mask, g_xattn, g_ffn, wq, bq, wk, bk, wv, bv,
          wfc_s, bfc_s, wproj_s, bproj_s, wr, wfc, bfc, wproj, bproj, out):
    ctx = ExitStack()
    with ctx:
        def sb(name, shape, dt=FP32):
            return ctx.enter_context(nc.sbuf_tensor(name, shape, dt))

        def ps(name):
            return ctx.enter_context(nc.psum_tensor(name, [P, 512], FP32))

        def sem(name):
            return ctx.enter_context(nc.semaphore(name))

        x_rows = nc.dram_tensor("x_rows", [TILES * P, D], FP32, kind="Internal").ap()
        x_sorted = nc.dram_tensor("x_sorted", [ROWS, D], FP32, kind="Internal").ap()
        z_rows = nc.dram_tensor("z_rows", [ROWS, D], FP32, kind="Internal").ap()
        vx = [nc.dram_tensor(f"v_blocks_{n}", [B, HALVES, NCH * P, P], FP32, kind="Internal").ap() for n in ("hi", "lo")]

        X = sb("X", [P, TILES, D])
        bq_col = sb("bq_col", [P, HALVES])
        bk_col = sb("bk_col", [P, HALVES])
        bv_row = sb("bv_row", [P, D])
        gate_x = sb("gate_x", [P, 1])
        tg_x = sb("tg_x", [P, 1])
        wr_raw = sb("wr_raw", [P, KC, NE])
        bq_neg = sb("bq_neg", [P, HALVES])
        wr_hi = sb("wr_hi", [P, KC, P], FP32R)
        wr_lo = sb("wr_lo", [P, KC, P], FP32R)
        ident = sb("ident", [P, P])
        ident_r = sb("ident_r", [P, P], FP32R)
        zeros = sb("zeros", [P, NCH * P])
        head_rows = sb("head_rows", [P, HH])
        neg_half = sb("neg_half", [P, GT])
        negmax = sb("negmax", [P, HALVES, GT, HH])
        psums = sb("psums", [P, HALVES, GT, HH])
        wait_taker = sb("wait_taker", [P, 1])
        stats = sb("stats", [P, GT, 6])
        mv = sb("mv", [P, GT, 2])
        veps = sb("veps", [P, GT])
        rstd = sb("rstd", [P, GT])
        logits = sb("logits", [P, TILES, NE])
        gate_f = sb("gate_f", [P, 1])
        tg_f = sb("tg_f", [P, 1])
        e_const = sb("e_const", [P, TILES])
        iota_e = sb("iota_e", [P, NE])
        iota_b = sb("iota_b", [P, BLOCKS])
        before_e = sb("before_e", [P, NE, NE])
        ones = sb("ones", [P, P])
        before_p = sb("before_p", [P, P])
        b1_rows = sb("b1_rows", [(NE + 1) * HC, P])
        b1_t = sb("b1_t", [P, (NE + 1) * HC])
        b2_all = sb("b2_all", [P, NE + 1, D])
        pos = sb("pos", [P, TOPK, TILES], mybir.dt.uint32)
        gates = sb("gates", [P, TOPK, TILES])
        block_e = sb("block_e", [P, BLOCKS], INT32)

        y2_all = sb("y2_all", [P, TILES, D])

        attention = ExitStack()

        def att_sb(name, shape, dt=FP32):
            return attention.enter_context(nc.sbuf_tensor(name, shape, dt))

        kb_hi = att_sb("kb_hi", [P, B, HALVES, HW], FP32R)
        kb_lo = att_sb("kb_lo", [P, B, HALVES, HW], FP32R)
        mask_big = att_sb("mask_big", [P, TILES, KV], FP32R)
        vs = [att_sb(f"vs_{n}", [P, HALVES, NCH, P], FP32R) for n in ("hi", "lo")]
        y1 = att_sb("y1", [P, GT, D])
        y1t_hi = att_sb("y1t_hi", [P, KC, GN], FP32R)
        y1t_lo = att_sb("y1t_lo", [P, KC, GN], FP32R)
        y2, y2t_hi, y2t_lo = y1, y1t_hi, y1t_lo
        q_hi = att_sb("q_hi", [P, HALVES, GN], FP32R)
        q_lo = att_sb("q_lo", [P, HALVES, GN], FP32R)
        prob = att_sb("prob", [P, 2, HW])
        wq_hi = att_sb("wq_hi", [P, KC, D], FP32R)
        wq_lo = att_sb("wq_lo", [P, KC, D], FP32R)

        early = ExitStack()

        def tmp(name, shape, dt=FP32):
            return early.enter_context(nc.sbuf_tensor(name, shape, dt))

        v_hi = tmp("v_hi", [P, B, D], FP32R)
        v_lo = tmp("v_lo", [P, B, D], FP32R)
        vr_hi = tmp("vr_hi", [KVR, B, D], FP32R)
        vr_lo = tmp("vr_lo", [KVR, B, D], FP32R)
        v_f = tmp("v_f", [P, B, D])
        vr_f = tmp("vr_f", [KVR, B, D])
        w3 = tmp("w3", [P, 3, KC, D])
        ctx_a = tmp("ctx_a", [P, B, D])
        ctx_b = tmp("ctx_b", [KVR, B, D])
        mask_i = tmp("mask_i", [P, TILES, KV], INT32)
        wk_t = tmp("wk_t", [P, KC, D])
        wv_t = tmp("wv_t", [P, KC, D])
        ctx_t = tmp("ctx_t", [P, KC, B, KV])
        k_t = tmp("k_t", [P, HALVES, B, KV])
        kb_f = tmp("kb_f", [P, HH, KV])
        early.close()
        ot = att_sb("ot", [P, HALVES, GN])
        att = att_sb("att", [P, GT, D])
        lt = att_sb("lt", [P, GN])
        rden = att_sb("rden", [P, GT, HH])
        some = att_sb("some", [P, GT])
        pt_hi = att_sb("pt_hi", [P, NCH, GN], FP32R)
        pt_lo = att_sb("pt_lo", [P, NCH, GN], FP32R)
        attention.close()

        raw_fc = sb("raw_fc", [P, 2, KC, HID])
        raw_pj = sb("raw_pj", [P, 2, HC, D])
        fc_hi = sb("fc_hi", [P, KC, HID], FP32R)
        fc_lo = sb("fc_lo", [P, KC, HID], FP32R)
        pj_hi = sb("pj_hi", [P, HC, D], FP32R)
        pj_lo = sb("pj_lo", [P, HC, D], FP32R)
        xr = sb("xr", [P, BT, D])
        xt_hi = sb("xt_hi", [P, KC, BN], FP32R)
        xt_lo = sb("xt_lo", [P, KC, BN], FP32R)
        h_f = sb("h_f", [P, PAIRS, 2, BN])
        b1_now = sb("b1_now", [P, 2, HC])
        ht_hi = sb("ht_hi", [P, HC, BN], FP32R)
        ht_lo = sb("ht_lo", [P, HC, BN], FP32R)
        y_sb = sb("y_sb", [P, 2, BT, D])
        top = sb("top", [P, TILES, NE])
        top_i = sb("top_i", [P, TILES, NE], mybir.dt.uint32)
        top_f = sb("top_f", [P, TOPK, TILES])
        chosen = sb("chosen", [P, TOPK, TILES, NE])
        both = sb("both", [P, TILES, NE])
        in_tile = sb("in_tile", [P, TILES, NE])
        totals = sb("totals", [P, TILES, NE])
        cum = sb("cum", [P, TILES + 1, NE])
        slot = sb("slot", [P, TILES, NE])
        work = sb("work", [P, TOPK, TILES, NE])
        over = sb("over", [P, NE, NE])
        thresholds = sb("thresholds", [P, NE])
        blocks_of = sb("blocks_of", [P, NE])
        start = sb("start", [P, NE])
        end = sb("end", [P, NE])
        passed = sb("passed", [P, BLOCKS, NE])
        block_f = sb("block_f", [P, BLOCKS])
        gap = sb("gap", [P, TILES])
        e_gap = sb("e_gap", [P, TILES])
        pos_f = sb("pos_f", [P, TOPK, TILES])
        none_f = sb("none_f", [P, TOPK, TILES])
        zg = sb("zg", [P, TOPK, TILES, D])


        s_bank = [ps(f"scores_{i}") for i in range(4)]
        t_bank = [ps(f"turned_{i}") for i in range(2)]
        m_bank = [ps(f"misc_{i}") for i in range(2)]

        ld_w = sem("ld_w")
        ld_c = sem("ld_c")
        ld_x = sem("ld_x")
        ld_m = sem("ld_m")
        ld_small = sem("ld_small")
        ld_v = sem("ld_v")
        vx_zero = sem("vx_zero")
        vx_in = sem("vx_in")
        consts = sem("consts")
        c_pool = sem("c_pool")
        prep_full = sem("prep_full")
        prep_done = sem("prep_done")
        kb_ready = sem("kb_ready")
        tanh_ready = sem("tanh_ready")
        veps_ready = sem("veps_ready")
        rstd_ready = sem("rstd_ready")
        y1_ready = sem("y1_ready")
        y2_ready = sem("y2_ready")
        y2_kept = sem("y2_kept")
        s_full = sem("s_full")
        s_max = sem("s_max")
        s_free = sem("s_free")
        p_ready = sem("p_ready")
        p_free = sem("p_free")
        t_full = sem("t_full")
        t_hi = sem("t_hi")
        t_free = sem("t_free")
        pv_done = sem("pv_done")
        m_full = sem("m_full")
        m_hi = sem("m_hi")
        m_free = [sem("m_free_0"), sem("m_free_1")]
        dv = sem("dv")
        x_zero = sem("x_zero")
        rows_stored = sem("rows_stored")
        ld_b1 = sem("ld_b1")
        counts_in = sem("counts_in")
        counts_full = sem("counts_full")
        b1_full = sem("b1_full")
        b1_ready = sem("b1_ready")
        gap_ready = sem("gap_ready")
        e_gap_ready = sem("e_gap_ready")
        blocks_ready = sem("blocks_ready")
        pos_ready = sem("pos_ready")
        scattered = sem("scattered")
        gathered = sem("gathered")
        fc_in = [sem("fc_in_0"), sem("fc_in_1")]
        pj_in = [sem("pj_in_0"), sem("pj_in_1")]
        fc_his = sem("fc_his")
        fc_ready = sem("fc_ready")
        pj_his = sem("pj_his")
        pj_ready = sem("pj_ready")
        x_in = sem("x_in")
        xt_full = sem("xt_full")
        xt_his = sem("xt_his")
        xt_ready = sem("xt_ready")
        b1_set = sem("b1_set")
        h_full = sem("h_full")
        h_act = sem("h_act")
        h_ready = sem("h_ready")
        y_full = sem("y_full")
        y_evac = sem("y_evac")
        z_out = [sem("z_out_0"), sem("z_out_1")]
        combined = sem("combined")
        out_done = sem("out_done")

        block = ctx.enter_context(nc.Block())

        M_AHEAD, M_BODY = 4, 12
        HI_AHEAD, HI_BODY = 4, 6
        DV_BODY = 12

        def m_use(base, u):
            uses, fulls, products = base
            return (u % 2, uses // 2 + u // 2 + 1, fulls + u + 1 - sum(u > v for v in products))

        def m_base(g, more):
            return (g * M_BODY + M_AHEAD, g * (M_BODY - 2) + M_AHEAD, (0, 6 if more else 2))

        ahead = (0, 0, ())

        def rows(c0, m):
            if CHROWS[c0 + m - 1] == CHROWS[c0]:
                return [(CHROWS[c0], c0, c0 + m)]
            return [(CHROWS[c0], c0, c0 + m - 1), (CHROWS[c0 + m - 1], c0 + m - 1, c0 + m)]

        H0 = PAIRS
        ATT_OVER = (GROUPS * M_BODY - 4 + M_AHEAD) // 2 + 1
        NBLOCKS = SHARED + BLOCKS

        def attention_over(eng):
            for bank in range(2):
                eng.wait_ge(m_free[bank], ATT_OVER)

        @block.sync
        def _(sp):
            with nc.allow_non_contiguous_dma(reason="small columns"):
                for i, w in enumerate((wq, wk, wv)):
                    sp.dma_start(w3[:, i], w.rearrange("(o p) i -> p o i", p=P)).then_inc(ld_w, 16)
                sp.dma_start(ctx_a[:, :, :], ctx_kv[:, 0:P, :].rearrange("b p d -> p b d")).then_inc(ld_c, 16)
                sp.dma_start(ctx_b[:, :, :], ctx_kv[:, P:KV, :].rearrange("b p d -> p b d")).then_inc(ld_c, 16)
                sp.dma_start(X[:, 0:GT], x[0, 0:GN].rearrange("(t p) d -> p t d", p=P)).then_inc(ld_x, 16)
                sp.dma_start(bq_col[:, :], bq.rearrange("(o p) -> p o", p=P)).then_inc(ld_small, 16)
                sp.dma_start(bk_col[:, :], bk.rearrange("(o p) -> p o", p=P)).then_inc(ld_small, 16)
                sp.dma_start(bv_row[:, :], bv.rearrange("(a n) -> a n", a=1).to_broadcast([P, D])).then_inc(ld_small, 16)
                sp.dma_start(gate_x[:, :], g_xattn.rearrange("(a n) -> a n", a=1).to_broadcast([P, 1])).then_inc(ld_small, 16)
                sp.dma_start(wr_raw[:, :, :], wr.rearrange("(k p) e -> p k e", p=P)).then_inc(ld_small, 16)
                sp.dma_start(gate_f[:, :], g_ffn.rearrange("(a n) -> a n", a=1).to_broadcast([P, 1])).then_inc(ld_small, 16)
                sp.dma_start(mask_i[:, :, :], mask.rearrange("b (t p) k -> p (b t) k", p=P)).then_inc(ld_m, 16)
                for g in range(1, GROUPS):
                    b, t0 = g * GN // T, g * GN % T
                    sp.dma_start(X[:, g * GT:(g + 1) * GT],
                                 x[b, t0:t0 + GN].rearrange("(t p) d -> p t d", p=P)).then_inc(ld_x, 16)
                sp.dma_start(b1_rows[0:NE * HC, :], bfc.rearrange("e (c p) -> (e c) p", p=P)).then_inc(ld_b1, 16)
                sp.dma_start(b1_rows[NE * HC:(NE + 1) * HC, :], bfc_s.rearrange("(c p) -> c p", p=P)).then_inc(ld_b1, 16)
                sp.dma_start(b2_all[:, 0:NE, :], bproj.rearrange("(a e) n -> a e n", a=1).to_broadcast([P, NE, D])).then_inc(ld_b1, 16)
                sp.dma_start(b2_all[:, NE, :], bproj_s.rearrange("(a n) -> a n", a=1).to_broadcast([P, D])).then_inc(ld_b1, 16)
                sp.wait_ge(consts, 1)
                for t in vx:
                    for b in range(B):
                        for h in range(HALVES):
                            sp.dma_start(t[b, h].rearrange("(p c) f -> p (c f)", p=P), zeros[:, :]).then_inc(vx_zero, 16)
                sp.wait_ge(vx_zero, 16 * 2 * B * HALVES)
                sp.wait_ge(prep_done, 9)
                for t, va, vb in zip(vx, (v_hi, v_lo), (vr_hi, vr_lo)):
                    for b in range(B):
                        for hf in range(HALVES):
                            for src, r0, n in ((va, 0, P), (vb, P, KVR)):
                                dst = bass.AP(t.tensor, t[b, hf].offset + r0 * P, [[P, n], [KV * P + HD, HH], [1, HD]])
                                sp.dma_start(dst, src[:, b, hf * P:(hf + 1) * P].rearrange("p (h f) -> p h f", h=HH).bitcast(FP32)).then_inc(vx_in, 16)
                sp.wait_ge(vx_in, 16 * 4 * B * HALVES)
                blank = x_sorted.rearrange("(p r) d -> p (r d)", p=P)
                for a in range(0, ROWS * D // P, NCH * P):
                    z = min(a + NCH * P, ROWS * D // P)
                    sp.dma_start(blank[:, a:z], zeros[:, 0:z - a]).then_inc(x_zero, 16)
                with sp.Fori(0, GROUPS) as g:
                    sp.wait_ge(pv_done, g * 2 + 1)
                    for n in range(2):
                        for hf in range(HALVES):
                            sp.dma_start(vs[n][:, hf].bitcast(FP32),
                                         vx[n][bass.ds(g // 2, 1), hf].rearrange("a (c p) f -> p (a c) f", p=P)).then_inc(ld_v, 16)
                    sp.wait_ge(y2_kept, g + 2)
                    sp.dma_start(x_rows[bass.ds(g * GN, GN), :].rearrange("(t p) d -> p t d", p=P),
                                 y2_all[:, bass.ds(g * GT, GT), :]).then_inc(rows_stored, 16)

                attention_over(sp)

                def load_fc(slot, w):
                    sp.dma_start(raw_fc[:, slot], w.rearrange("a (k p) n -> p (a k) n", p=P)).then_inc(fc_in[slot], 16)

                def load_pj(slot, w):
                    for half in range(2):
                        sp.dma_start(raw_pj[:, slot, half * HC // 2:(half + 1) * HC // 2],
                                     w[:, half * HID // 2:(half + 1) * HID // 2].rearrange("a (c p) n -> p (a c) n", p=P)).then_inc(pj_in[slot], 16)

                def load_x(rows, r):
                    sp.dma_start(xr[:, :, :], rows[bass.ds(r, BN), :].rearrange("(t p) d -> p t d", p=P)).then_inc(x_in, 16)

                def expert(t):
                    return sp.value_load(block_e[0:1, bass.ds(t, 1)], min_val=0, max_val=NE - 1)

                sp.wait_ge(rows_stored, 16 * GROUPS)
                load_x(x_rows, 0)
                load_fc(0, wfc_s.rearrange("(a k) n -> a k n", a=1))
                load_pj(0, wproj_s.rearrange("(a k) n -> a k n", a=1))
                with sp.Fori(1, SHARED) as n:
                    sp.wait_ge(xt_full, n)
                    load_x(x_rows, n * BN)
                sp.wait_ge(blocks_ready, 1)
                e = expert(0)
                load_fc(1, wfc[bass.ds(e, 1)])
                load_pj(1, wproj[bass.ds(e, 1)])
                sp.wait_ge(xt_full, SHARED)
                sp.wait_ge(scattered, 16 * TOPK * TILES)
                load_x(x_sorted, 0)
                e = expert(1)
                sp.wait_ge(fc_ready, PAIRS)
                load_fc(0, wfc[bass.ds(e, 1)])
                sp.wait_ge(pj_ready, PAIRS)
                load_pj(0, wproj[bass.ds(e, 1)])

                def store_z(t, par):
                    sp.wait_ge(y_evac, (t + SHARED + 2) * BT)
                    sp.dma_start(z_rows[bass.ds(t * BN, BN), :].rearrange("(t p) d -> p t d", p=P), y_sb[:, par]).then_inc(z_out[par], 16)

                def body(t, par, x_next, store, w_next):
                    if x_next:
                        sp.wait_ge(xt_full, t + SHARED + 1)
                        load_x(x_sorted, (t + 1) * BN)
                    if store:
                        store_z(t - 1, 1 - par)
                    if w_next:
                        e = expert(t + 2)
                        sp.wait_ge(fc_ready, (t + 2) * PAIRS)
                        load_fc(1 - par, wfc[bass.ds(e, 1)])
                        sp.wait_ge(pj_ready, (t + 2) * PAIRS)
                        load_pj(1 - par, wproj[bass.ds(e, 1)])

                body(0, 0, True, False, True)
                with sp.Fori(0, (BLOCKS - 3) // 2) as i:
                    body(i * 2 + 1, 1, True, True, True)
                    body(i * 2 + 2, 0, True, True, True)
                body(BLOCKS - 2, 1, True, True, False)
                body(BLOCKS - 1, 0, False, True, False)
                store_z(BLOCKS - 1, 0)
                for q in range(GROUPS):
                    b, t0 = q * GN // T, q * GN % T
                    sp.wait_ge(combined, q + 1)
                    sp.dma_start(out[b, t0:t0 + GN].rearrange("(t p) d -> p t d", p=P), X[:, q * GT:(q + 1) * GT]).then_inc(out_done, 16)
                sp.wait_ge(out_done, 16 * GROUPS)

        @block.gpsimd
        def _(pool):
            nc.gpsimd.memset(zeros[:, :], 0.0).then_inc(consts, 1)
            nc.gpsimd.memset(ident[:, :], 0.0).then_inc(c_pool, 1)
            nc.gpsimd.memset(head_rows[:, :], 1.0).then_inc(c_pool, 1)
            nc.gpsimd.memset(neg_half[:, :], -0.5).then_inc(c_pool, 1)
            pool.sem_inc(s_free, 4)
            pool.sem_inc(t_full, NB + 1)
            pool.sem_inc(t_free, 2)
            for one in (pv_done, m_free[0], m_free[1], y2_kept):
                pool.sem_inc(one, 1)
            pool.sem_inc(h_act, PAIRS)
            pool.sem_inc(h_ready, PAIRS)
            pool.sem_inc(y_evac, BT)
            pool.sem_inc(y_full, 1)
            pool.sem_inc(z_out[0], 16)
            pool.sem_inc(z_out[1], 16)
            nc.gpsimd.memset(wr_hi[:, :, :].bitcast(FP32), 0.0).then_inc(c_pool, 1)
            nc.gpsimd.memset(wr_lo[:, :, :].bitcast(FP32), 0.0).then_inc(c_pool, 1)
            pool.wait_ge(c_pool, 5)
            nc.gpsimd.affine_select(out=ident[:, :], in_=ident[:, :], compare_op=ALU.not_equal, fill=1.0,
                                    base=0, pattern=[[-1, P]], channel_multiplier=1).then_inc(consts, 1)
            nc.gpsimd.affine_select(out=head_rows[:, :], in_=head_rows[:, :], compare_op=ALU.is_ge, fill=0.0,
                                    base=0, pattern=[[-HD, HH]], channel_multiplier=1).then_inc(c_pool, 1)
            pool.wait_ge(c_pool, 6)
            nc.gpsimd.affine_select(out=head_rows[:, :], in_=head_rows[:, :], compare_op=ALU.is_ge, fill=0.0,
                                    base=HD - 1, pattern=[[HD, HH]], channel_multiplier=-1).then_inc(consts, 1)

            nc.gpsimd.memset(e_const[:, :], 2.718281828459045).then_inc(c_pool, 1)
            nc.gpsimd.memset(ones[:, :], 1.0).then_inc(c_pool, 1)
            nc.gpsimd.memset(before_p[:, :], 1.0).then_inc(c_pool, 1)
            nc.gpsimd.memset(before_e[:, :, :], 1.0).then_inc(c_pool, 1)
            nc.gpsimd.iota(iota_e[:, :], pattern=[[1, NE]], base=0, channel_multiplier=0, allow_small_or_imprecise_dtypes=True).then_inc(c_pool, 1)
            nc.gpsimd.iota(iota_b[:, :], pattern=[[1, BLOCKS]], base=0, channel_multiplier=0, allow_small_or_imprecise_dtypes=True).then_inc(c_pool, 1)
            pool.wait_ge(c_pool, 12)
            nc.gpsimd.affine_select(out=before_p[:, :], in_=before_p[:, :], compare_op=ALU.is_gt, fill=0.0,
                                    base=0, pattern=[[1, P]], channel_multiplier=-1).then_inc(c_pool, 1)
            nc.gpsimd.affine_select(out=before_e[:, :, :], in_=before_e[:, :, :], compare_op=ALU.is_gt, fill=0.0,
                                    base=0, pattern=[[1, NE], [-1, NE]], channel_multiplier=0).then_inc(c_pool, 1)

            def power(n):
                pool.wait_ge(veps_ready, n)
                nc.gpsimd.tensor_tensor(rstd[:, :], veps[:, :], neg_half[:, :], ALU.pow).then_inc(rstd_ready, 1)

            def body(g, more):
                if more:
                    power(g * 2 + 2)
                    power(g * 2 + 3)
                else:
                    power(g * 2 + 2)
                pool.wait_ge(y2_ready, g + 1)
                nc.gpsimd.tensor_copy(y2_all[:, bass.ds(g * GT, GT), :], y2[:, :, :]).then_inc(y2_kept, 1)

            power(1)
            with pool.Fori(0, GROUPS - 1) as g:
                body(g, True)
            body(GROUPS - 1, False)

            pool.wait_ge(gap_ready, 1)
            nc.gpsimd.tensor_tensor(e_gap[:, :], e_const[:, :], gap[:, :], ALU.pow).then_inc(e_gap_ready, 1)
            pool.wait_ge(x_zero, 16 * -(-ROWS * D // P // (NCH * P)))
            pool.wait_ge(pos_ready, 1)
            pool.wait_ge(y2_kept, GROUPS + 1)
            for t in range(TILES):
                for k in range(TOPK):
                    nc.gpsimd.indirect_dma_start(out=x_sorted, out_offset=bass.IndirectOffsetOnAxis(ap=pos[:, k, t:t + 1], axis=0),
                                                 in_=y2_all[:, t, :], in_offset=None, bounds_check=ROWS - 1, oob_is_err=False)\
                      .then_inc(scattered, 16)
            nc.gpsimd.memset(zg[:, :, :, :], 0.0).then_inc(c_pool, 1)
            pool.wait_ge(c_pool, 15)
            pool.wait_ge(z_out[0], 16 * ((BLOCKS + 1) // 2 + 1))
            pool.wait_ge(z_out[1], 16 * (BLOCKS // 2 + 1))
            for t in range(TILES):
                for k in range(TOPK):
                    nc.gpsimd.indirect_dma_start(out=zg[:, k, t, :], out_offset=None, in_=z_rows,
                                                 in_offset=bass.IndirectOffsetOnAxis(ap=pos[:, k, t:t + 1], axis=0),
                                                 bounds_check=ROWS - 1, oob_is_err=False).then_inc(gathered, 16)

        @block.tensor
        def _(pe):
            mm = nc.tensor.matmul
            pe.wait_ge(consts, 2)
            pe.wait_ge(ld_w, 48)
            for i in range(3):
                for k in range(KC):
                    for o in range(KC):
                        last = nc.tensor.transpose(s_bank[i][:, k * D + o * P:k * D + (o + 1) * P], w3[:, i, o, k * P:(k + 1) * P], ident[:, :])
                last.then_inc(prep_full, 1)
            pe.wait_ge(ld_c, 32)
            for k in range(KC):
                bank = (s_bank[3], t_bank[0])[k]
                for b in range(B):
                    nc.tensor.transpose(bank[:, b * KV:b * KV + P], ctx_a[:, b, k * P:(k + 1) * P], ident[:, :])
                    last = nc.tensor.transpose(bank[:, b * KV + P:(b + 1) * KV], ctx_b[:, b, k * P:(k + 1) * P], ident[0:KVR, 0:KVR])
                last.then_inc(prep_full, 1)
            pe.wait_ge(prep_done, 5)
            for hf in range(HALVES):
                bank = (t_bank[1], m_bank[0])[hf]
                for k in range(KC):
                    last = mm(bank[:, 0:B * KV], wk_t[:, k, hf * P:(hf + 1) * P], ctx_t[:, k].rearrange("p b k -> p (b k)"),
                              start=k == 0, stop=k == KC - 1)
                last.then_inc(prep_full, 1)
            for b in range(B):
                for k in range(KC):
                    last = mm(m_bank[1][:, b * D:(b + 1) * D], ctx_t[:, k, b, 0:P], wv_t[:, k, :], start=k == 0, stop=k == KC - 1)
            last.then_inc(prep_full, 1)
            for b in range(B):
                for k in range(KC):
                    last = mm(s_bank[0][0:KVR, b * D:(b + 1) * D], ctx_t[:, k, b, P:KV], wv_t[:, k, :], start=k == 0, stop=k == KC - 1)
            last.then_inc(prep_full, 1)
            pe.wait_ge(prep_done, 9)

            def y1_and_q(base, u, n):
                pe.wait_ge(y1_ready, n)
                for k in range(KC):
                    bank, free, _ = m_use(base, u + k)
                    pe.wait_ge(m_free[bank], free)
                    for j in range(GT):
                        last = nc.tensor.transpose(m_bank[bank][:, j * P:(j + 1) * P], y1[:, j, k * P:(k + 1) * P], ident[:, :])
                    last.then_inc(m_full, 1)
                for hf in range(HALVES):
                    bank, free, _ = m_use(base, u + 2 + hf)
                    pe.wait_ge(m_free[0], m_use(base, u + 2)[1])
                    pe.wait_ge(m_free[1], m_use(base, u + 3)[1] if hf == 0 else free)
                    out = m_bank[bank][:, :]
                    for k in range(KC):
                        for i, (w, y) in enumerate(((wq_hi, y1t_hi), (wq_lo, y1t_hi), (wq_hi, y1t_lo))):
                            last = mm(out, w[:, k, hf * P:(hf + 1) * P], y[:, k, :], start=k == 0 and i == 0, stop=k == KC - 1 and i == 2)
                    last.then_inc(m_full, 1)

            def scores(g, n):
                hf, j = divmod(n, GT)
                ql, qh = (q[:, hf, j * P:(j + 1) * P] for q in (q_lo, q_hi))
                for i, (h0, nh) in enumerate(HEADS):
                    u = n * NB + i
                    pe.wait_ge(s_free, g * (STEPS * NB) + u + 1)
                    out = s_bank[u % 4][:, 0:nh * KV]
                    cols = slice(h0 * KV, (h0 + nh) * KV)
                    kh = kb_hi[:, bass.ds(g // 2, 1), hf, cols]
                    kl = kb_lo[:, bass.ds(g // 2, 1), hf, cols]
                    mm(out, qh, kh, start=True, stop=False)
                    mm(out, qh, kl, start=False, stop=False)
                    mm(out, ql, kh, start=False, stop=False)
                    mm(out, ident_r[:, :], mask_big[:, bass.ds(g * GT + j, 1), :].to_broadcast([P, nh, KV]), start=False, stop=True)\
                        .then_inc(s_full, 1)

            def turn(g, n):
                for i, (c0, m) in enumerate(CHUNKS):
                    u = n * NB + i
                    pe.wait_ge(s_free, g * (STEPS * NB) + (n + 1) * NB + 4)
                    pe.wait_ge(t_free, g * (STEPS * NB) + u + 1)
                    for c in range(c0, c0 + m):
                        r = CHROWS[c]
                        last = nc.tensor.transpose(t_bank[u % 2][0:r, (c - c0) * P:(c - c0 + 1) * P],
                                                   prob[:, n % 2, c * P:c * P + r], ident[:, :])
                    last.then_inc(t_full, 1)

            def pv(g, hf, base, u):
                bank, free, _ = m_use(base, u)
                pe.wait_ge(m_free[bank], free)
                pe.wait_ge(ld_v, (g + 1) * 64)
                pe.wait_ge(t_free, g * (STEPS * NB) + (hf + 1) * GT * NB + 2)
                for c in range(NCH):
                    r = CHROWS[c]
                    for i, (v, p) in enumerate(((vs[0], pt_hi), (vs[1], pt_hi), (vs[0], pt_lo))):
                        last = mm(m_bank[bank][:, :], v[0:r, hf, c, :], p[0:r, c, :], start=c == 0 and i == 0, stop=c == NCH - 1 and i == 2)
                last.then_inc(pv_done, 1)

            def body(g, more):
                base = m_base(g, more)
                scores(g, 0)
                for n in range(1, STEPS):
                    scores(g, n)
                    if n == GT + 1:
                        pv(g, 0, base, 0)
                    turn(g, n - 1)
                    if n == GT + 1:
                        turn_out(base, 1, 0)
                u = 2
                if more:
                    y1_and_q(base, u, g + 2)
                    u += 4
                turn(g, STEPS - 1)
                pv(g, 1, base, u)
                turn_out(base, u + 1, 1)
                u += 2
                pe.wait_ge(y2_ready, g + 1)
                for k in range(KC):
                    bank, free, _ = m_use(base, u + k)
                    pe.wait_ge(m_free[bank], free)
                    for j in range(GT):
                        last = nc.tensor.transpose(m_bank[bank][:, j * P:(j + 1) * P], y2[:, j, k * P:(k + 1) * P], ident[:, :])
                    last.then_inc(m_full, 1)
                bank, free, _ = m_use(base, u + 2)
                pe.wait_ge(m_free[bank], free)
                pe.wait_ge(m_free[1 - bank], m_use(base, u + 3)[1])
                for k in range(KC):
                    for i, (w, y) in enumerate(((wr_hi, y2t_hi), (wr_lo, y2t_hi), (wr_hi, y2t_lo))):
                        last = mm(m_bank[bank][:, :], w[:, k, :], y[:, k, :], start=k == 0 and i == 0, stop=k == KC - 1 and i == 2)
                last.then_inc(m_full, 1)
                bank2, free, _ = m_use(base, u + 3)
                pe.wait_ge(m_free[bank], m_use(base, u + 4)[1])
                for j in range(GT):
                    last = nc.tensor.transpose(m_bank[bank2][:, j * P:(j + 1) * P], lt[:, j * P:(j + 1) * P], ident[:, :])
                last.then_inc(m_full, 1)
                if more:
                    for hf in range(HALVES):
                        pe.wait_ge(m_free[hf], m_use(base, 2 + 4 + hf)[1])

            def turn_out(base, u, hf):
                bank, free, _ = m_use(base, u)
                pe.wait_ge(m_free[bank], free)
                pe.wait_ge(m_free[1 - bank], m_use(base, u + 1)[1])
                for j in range(GT):
                    last = nc.tensor.transpose(m_bank[bank][:, j * P:(j + 1) * P], ot[:, hf, j * P:(j + 1) * P], ident[:, :])
                last.then_inc(m_full, 1)

            y1_and_q(ahead, 0, 1)
            for hf in range(HALVES):
                pe.wait_ge(m_free[hf], m_use(ahead, 4 + hf)[1])
            pe.wait_ge(kb_ready, 1)
            with pe.Fori(0, GROUPS - 1) as g:
                body(g, True)
            body(GROUPS - 1, False)

            pe.wait_ge(counts_in, 1)
            mm(t_bank[1][:, 0:P], before_p[:, :], both[:, :, :].rearrange("p t e -> p (t e)"), start=True, stop=True)
            mm(t_bank[1][:, P:2 * P], ones[:, :], both[:, :, :].rearrange("p t e -> p (t e)"), start=True, stop=True)\
                .then_inc(counts_full, 1)

            def turn_x(n):
                pe.wait_ge(x_in, (n + 1) * 16)
                pe.wait_ge(xt_ready, n)
                for k in range(KC):
                    for i in range(BT):
                        last = nc.tensor.transpose(t_bank[0][:, (k * BT + i) * P:(k * BT + i + 1) * P], xr[:, i, k * P:(k + 1) * P], ident[:, :])
                last.then_inc(xt_full, 1)

            def block_of(n, load, next_x):
                pe.wait_ge(xt_ready, n + 1)
                for p in range(PAIRS):
                    pe.wait_ge(fc_ready, load * PAIRS + p + 1)
                    pe.wait_ge(h_act, n * PAIRS + p + 1)
                    for c in (0, 1):
                        hid = slice((2 * p + c) * P, (2 * p + c + 1) * P)
                        for k in range(KC):
                            for i, (w, xx) in enumerate(((fc_hi, xt_hi), (fc_lo, xt_hi), (fc_hi, xt_lo))):
                                last = mm(s_bank[p][:, c * BN:(c + 1) * BN], w[:, k, hid], xx[:, k, :],
                                          start=k == 0 and i == 0, stop=k == KC - 1 and i == 2)
                    last.then_inc(h_full, 1)
                if next_x:
                    turn_x(n + 1)
                for i in range(BT):
                    pe.wait_ge(y_evac, n * BT + i + 1)
                    for c in range(HC):
                        if i == 0 and c % 2 == 0:
                            pe.wait_ge(pj_ready, load * PAIRS + c // 2 + 1)
                            pe.wait_ge(h_ready, n * PAIRS + c // 2 + 1 + H0)
                        for j, (h, w) in enumerate(((ht_hi, pj_hi), (ht_hi, pj_lo), (ht_lo, pj_hi))):
                            last = mm(m_bank[i][:, 0:D], h[:, c, i * P:(i + 1) * P], w[:, c, :], start=c == 0 and j == 0, stop=c == HC - 1 and j == 2)
                    last.then_inc(y_full, 1)

            nc_b1 = nc.tensor.transpose(t_bank[1][:, 2 * P:2 * P + (NE + 1) * HC], b1_rows[:, :], ident[0:(NE + 1) * HC, 0:(NE + 1) * HC])
            nc_b1.then_inc(b1_full, 1)
            turn_x(0)
            with pe.Fori(0, SHARED) as n:
                block_of(n, 0, True)
            with pe.Fori(0, BLOCKS - 1) as t:
                block_of(t + SHARED, t + 1, True)
            block_of(NBLOCKS - 1, BLOCKS, False)

        @block.scalar
        def _(act):
            A = nc.scalar.activation
            act.wait_ge(ld_small, 16 * 6)
            A(tg_x[:, :], gate_x[:, :], ACT.Tanh).then_inc(tanh_ready, 1)
            A(tg_f[:, :], gate_f[:, :], ACT.Tanh).then_inc(tanh_ready, 1)

            def split_hi(out, base, u, bias=0.0):
                bank, _, full = m_use(base, u)
                act.wait_ge(m_full, full)
                A(out, m_bank[bank][:, :], ACT.Identity, bias=bias).then_inc(m_hi, 1)

            def exps(g, n):
                hf, j = divmod(n, GT)
                act.wait_ge(t_full, g * (STEPS * NB) + n * NB + 1)
                for i, (h0, nh) in enumerate(HEADS):
                    u = n * NB + i
                    act.wait_ge(s_max, g * (STEPS * NB) + u + 1)
                    for h in range(h0, h0 + nh):
                        last = A(prob[:, n % 2, h * KV:(h + 1) * KV], s_bank[u % 4][:, (h - h0) * KV:(h - h0 + 1) * KV], ACT.Exp,
                                 bias=negmax[:, hf, j, h:h + 1], scale=-1.0, accum_out=psums[:, hf, j, h:h + 1])
                    last.then_inc(s_free, 1)

            def turned_hi(g, n):
                hf, j = divmod(n, GT)
                if j == 0:
                    act.wait_ge(pv_done, g * 2 + hf + 1)
                for i, (c0, m) in enumerate(CHUNKS):
                    u = n * NB + i
                    act.wait_ge(t_full, g * (STEPS * NB) + u + 1 + NB + 1)
                    for r, a, z in rows(c0, m):
                        last = A(pt_hi[0:r, a:z, j * P:(j + 1) * P],
                                 t_bank[u % 2][0:r, (a - c0) * P:(z - c0) * P].rearrange("p (c q) -> p c q", q=P), ACT.Copy)
                    last.then_inc(t_hi, 1)

            def pv_out(g, base, u, hf):
                bank, _, _ = m_use(base, u)
                act.wait_ge(pv_done, g * 2 + hf + 2)
                A(ot[:, hf, :], m_bank[bank][:, :], ACT.Copy).then_inc(m_free[bank], 1)

            def y1_and_q(base, u):
                for k in range(KC):
                    split_hi(y1t_hi[:, k, :], base, u + k)
                for hf in range(HALVES):
                    split_hi(q_hi[:, hf, :], base, u + 2 + hf, bias=bq_neg[:, hf:hf + 1])

            def body(g, more):
                base = m_base(g, more)
                exps(g, 0)
                for n in range(1, STEPS):
                    exps(g, n)
                    if n == GT + 1:
                        pv_out(g, base, 0, 0)
                    turned_hi(g, n - 1)
                u = 2
                if more:
                    y1_and_q(base, u)
                    u += 4
                turned_hi(g, STEPS - 1)
                pv_out(g, base, u, 1)
                u += 2
                for k in range(KC):
                    split_hi(y2t_hi[:, k, :], base, u + k)
                bank, _, full = m_use(base, u + 2)
                act.wait_ge(m_full, full)
                A(lt[:, :], m_bank[bank][:, :], ACT.Copy).then_inc(m_free[bank], 1)

            act.wait_ge(prep_done, 1)
            y1_and_q(ahead, 0)
            with act.Fori(0, GROUPS - 1) as g:
                body(g, True)
            body(GROUPS - 1, False)

            def split_fc(load, slot, arrivals):
                act.wait_ge(fc_in[slot], arrivals * 16)
                for p in range(PAIRS):
                    cols = slice(p * 2 * P, (p + 1) * 2 * P)
                    A(fc_hi[:, :, cols], raw_fc[:, slot, :, cols], ACT.Copy).then_inc(fc_his, 1)

            def split_pj(p, slot, arrivals):
                act.wait_ge(pj_in[slot], arrivals * 32)
                A(pj_hi[:, 2 * p:2 * p + 2, :], raw_pj[:, slot, 2 * p:2 * p + 2, :], ACT.Copy).then_inc(pj_his, 1)

            def split_x(n):
                act.wait_ge(xt_full, n + 1)
                A(xt_hi[:, :, :], t_bank[0][:, :].rearrange("p (k n) -> p k n", k=KC), ACT.Copy).then_inc(xt_his, 1)

            def block_of(n, par, pj, next_x, next_fc):
                act.wait_ge(b1_set, n + 1)
                for p in range(PAIRS):
                    act.wait_ge(h_full, n * PAIRS + p + 1)
                    act.wait_ge(h_ready, n * PAIRS + p + 1)
                    for c in (0, 1):
                        last = A(h_f[:, p, c, :], s_bank[p][:, c * BN:(c + 1) * BN], ACT.Gelu_apprx_tanh,
                                 bias=b1_now[:, par, 2 * p + c:2 * p + c + 1])
                    last.then_inc(h_act, 1)
                    if pj:
                        act.wait_ge(y_full, n * BT + 1)
                        split_pj(p, *pj)
                if next_x:
                    split_x(n + 1)
                if next_fc:
                    split_fc(None, *next_fc)

            attention_over(act)
            split_x(0)
            split_fc(0, 0, 1)
            block_of(0, 0, (0, 1), True, None)
            block_of(1, 1, None, True, None)
            with act.Fori(1, SHARED // 2 - 1) as i:
                block_of(i * 2, 0, None, True, None)
                block_of(i * 2 + 1, 1, None, True, None)
            block_of(SHARED - 2, 0, None, True, None)
            block_of(SHARED - 1, 1, None, True, (1, 1))

            with act.Fori(0, (BLOCKS - 1) // 2) as i:
                block_of(i * 2 + SHARED, 0, (1, i + 1), True, (0, i + 2))
                block_of(i * 2 + 1 + SHARED, 1, (0, i + 2), True, (1, i + 2))
            block_of(NBLOCKS - 1, 0, (1, (BLOCKS + 1) // 2), False, None)

        @block.vector
        def _(dve):
            V = nc.vector
            count = [0, 0]

            def link(ins):
                count[1] += 1
                ins.then_inc(dv, 1)
                dve.wait_ge(dv, count[0] + count[1])

            def norm_stats(tile):
                for j in range(GT):
                    last = V.bn_stats(stats[:, j, :], tile(j))
                link(last)
                V.memset(wait_taker[:, :], 0.0)
                for j in range(GT):
                    last = V.bn_aggr(mv[:, j, :], stats[:, j, :])
                link(last)
                V.tensor_scalar(veps[:, :], mv[:, :, 1], EPS, None, ALU.add).then_inc(veps_ready, 1)

            def norm(tile, n, out, ready):
                dve.wait_ge(rstd_ready, n)
                for j in range(GT):
                    last = V.tensor_scalar(out[:, j, :], tile(j), mv[:, j, 0:1], rstd[:, j:j + 1],
                                           ALU.subtract, ALU.mult)
                last.then_inc(ready, 1)

            def split_lo(out, hi, base, u, n, bias=None):
                bank, _, _ = m_use(base, u)
                dve.wait_ge(m_hi, n)
                if bias is None:
                    ins = V.tensor_tensor(out, m_bank[bank][:, :], hi.bitcast(FP32), ALU.subtract)
                else:
                    ins = V.scalar_tensor_tensor(out, m_bank[bank][:, :], bias, hi.bitcast(FP32), ALU.add, ALU.subtract)
                ins.then_inc(m_free[bank], 1)

            def y1_and_q(base, u, n):
                for k in range(KC):
                    split_lo(y1t_lo[:, k, :], y1t_hi[:, k, :], base, u + k, n + k + 1)
                for hf in range(HALVES):
                    split_lo(q_lo[:, hf, :], q_hi[:, hf, :], base, u + 2 + hf, n + 3 + hf, bias=bq_neg[:, hf:hf + 1])

            def maxima(g, n):
                hf, j = divmod(n, GT)
                for i, (h0, nh) in enumerate(HEADS):
                    u = n * NB + i
                    dve.wait_ge(s_full, g * (STEPS * NB) + u + 1)
                    V.tensor_reduce(negmax[:, hf, j, h0:h0 + nh], s_bank[u % 4][:, 0:nh * KV].rearrange("p (h k) -> p h k", k=KV),
                                    axis=AX.X, op=ALU.min).then_inc(s_max, 1)

            def turned_lo(g, n):
                hf, j = divmod(n, GT)
                for i, (c0, m) in enumerate(CHUNKS):
                    u = n * NB + i
                    dve.wait_ge(t_hi, g * (STEPS * NB) + u + 1)
                    for r, a, z in rows(c0, m):
                        cols = slice(j * P, (j + 1) * P)
                        last = V.tensor_tensor(pt_lo[0:r, a:z, cols],
                                               t_bank[u % 2][0:r, (a - c0) * P:(z - c0) * P].rearrange("p (c q) -> p c q", q=P),
                                               pt_hi[0:r, a:z, cols].bitcast(FP32), ALU.subtract)
                    last.then_inc(t_free, 1)

            def half_out(base, u, hf):
                if hf == 0:
                    link(V.tensor_scalar(some[:, :], negmax[:, 0, :, 0], MASKED / 10, None, ALU.is_lt))
                bank, _, full = m_use(base, u)
                dve.wait_ge(m_full, full)
                keep = some[:, :].unsqueeze(2).to_broadcast([P, GT, HH])
                link(V.tensor_tensor(rden[:, :, :], psums[:, hf], keep, ALU.mult))
                link(V.reciprocal(rden[:, :, :], rden[:, :, :]))
                link(V.tensor_tensor(rden[:, :, :], rden[:, :, :], keep, ALU.mult))
                V.tensor_tensor(att[:, :, hf * P:(hf + 1) * P].rearrange("p t (h d) -> p t h d", d=HD),
                                m_bank[bank][:, :].rearrange("p (t h d) -> p t h d", t=GT, d=HD),
                                rden[:, :, :].unsqueeze(3).to_broadcast([P, GT, HH, HD]), ALU.mult).then_inc(m_free[bank], 1)

            def body(g, more):
                base = m_base(g, more)
                hi = g * HI_BODY + HI_AHEAD
                maxima(g, 0)
                for n in range(1, STEPS):
                    maxima(g, n)
                    if n == GT and more:
                        norm_stats(lambda j: X[:, bass.ds((g + 1) * GT + j, 1), :])
                    turned_lo(g, n - 1)
                    if n == GT + 1:
                        if more:
                            dve.wait_ge(y2_kept, g + 1)
                            norm(lambda j: X[:, bass.ds((g + 1) * GT + j, 1), :], g * 2 + 2, y1, y1_ready)
                        half_out(base, 1, 0)
                u = 2
                if more:
                    y1_and_q(base, u, hi)
                    u += 4
                    hi = hi + 4
                turned_lo(g, STEPS - 1)
                half_out(base, u + 1, 1)
                u += 2
                dve.wait_ge(tanh_ready, 1)
                dve.wait_ge(m_free[(u - 1) % 2], m_use(base, u + 1)[1])
                xg = X[:, bass.ds(g * GT, GT), :]
                link(V.scalar_tensor_tensor(att[:, :, :], att[:, :, :], tg_x[:, 0:1], xg, ALU.mult, ALU.add))
                V.tensor_scalar(xg, att[:, :, :], 1.0, None, ALU.mult)
                norm_stats(lambda j: att[:, j, :])
                dve.wait_ge(y2_kept, g + 1)
                norm(lambda j: att[:, j, :], g * 2 + (3 if more else 2), y2, y2_ready)
                for k in range(KC):
                    split_lo(y2t_lo[:, k, :], y2t_hi[:, k, :], base, u + k, hi + k + 1)
                bank, _, full = m_use(base, u + 3)
                dve.wait_ge(m_full, full)
                V.tensor_scalar(logits[:, bass.ds(g * GT, GT), :], m_bank[bank][:, :].rearrange("p (t e) -> p t e", e=P)[:, :, 0:NE],
                                1.0, None, ALU.mult)\
                 .then_inc(m_free[bank], 1)

            dve.wait_ge(consts, 3)
            V.tensor_copy(ident_r[:, :], ident[:, :])
            dve.wait_ge(ld_small, 16 * 6)
            V.tensor_scalar(bq_neg[:, :], bq_col[:, :], SQ, None, ALU.mult)
            dve.wait_ge(c_pool, 5)
            link(V.tensor_copy(wr_hi[:, :, 0:NE], wr_raw[:, :, :]))
            V.tensor_tensor(wr_lo[:, :, 0:NE], wr_raw[:, :, :], wr_hi[:, :, 0:NE].bitcast(FP32), ALU.subtract)
            dve.wait_ge(prep_full, 1)
            link(V.tensor_scalar(wq_hi[:, :, :], s_bank[0][:, :], SQ, None, ALU.mult))
            V.scalar_tensor_tensor(wq_lo[:, :, :], s_bank[0][:, :], SQ, wq_hi[:, :, :].bitcast(FP32), ALU.mult, ALU.subtract).then_inc(prep_done, 1)
            for i, w in ((1, wk_t), (2, wv_t)):
                dve.wait_ge(prep_full, 1 + i)
                V.tensor_copy(w[:, :, :], s_bank[i][:, :]).then_inc(prep_done, 1)
            for k, bank in enumerate((s_bank[3], t_bank[0])):
                dve.wait_ge(prep_full, 4 + k)
                V.tensor_copy(ctx_t[:, k], bank[:, 0:B * KV].rearrange("p (b k) -> p b k", b=B)).then_inc(prep_done, 1)
            dve.wait_ge(ld_x, 16)
            norm_stats(lambda j: X[:, j, :])
            norm(lambda j: X[:, j, :], 1, y1, y1_ready)
            for hf, bank in enumerate((t_bank[1], m_bank[0])):
                dve.wait_ge(prep_full, 6 + hf)
                V.tensor_scalar(k_t[:, hf], bank[:, 0:B * KV].rearrange("p (b k) -> p b k", b=B), bk_col[:, hf:hf + 1], None, ALU.add)\
                 .then_inc(prep_done, 1)
            for i, (f, h, l, bank, r) in enumerate(((v_f, v_hi, v_lo, m_bank[1], P), (vr_f, vr_hi, vr_lo, s_bank[0], KVR))):
                dve.wait_ge(prep_full, 8 + i)
                for b in range(B):
                    last = V.tensor_tensor(f[:, b], bank[0:r, b * D:(b + 1) * D], bv_row[0:r, :], ALU.add)
                link(last)
                link(V.tensor_copy(h[:, :, :], f[:, :, :]))
                V.tensor_tensor(l[:, :, :], f[:, :, :], h[:, :, :].bitcast(FP32), ALU.subtract).then_inc(prep_done, 1)
            y1_and_q(ahead, 0, 0)
            dve.wait_ge(ld_m, 16)
            V.tensor_scalar(mask_big[:, :, :], mask_i[:, :, :], 1.0, MASKED, ALU.is_equal, ALU.mult)
            dve.wait_ge(prep_done, 7)
            for b in range(B):
                for hf in range(HALVES):
                    link(V.tensor_tensor(kb_f[:, :, :], k_t[:, hf, b:b + 1, :].to_broadcast([P, HH, KV]),
                                         head_rows[:, :].unsqueeze(2).to_broadcast([P, HH, KV]), ALU.mult))
                    link(V.tensor_copy(kb_hi[:, b, hf, :], kb_f[:, :, :].rearrange("p h k -> p (h k)")))
                    last = V.tensor_tensor(kb_lo[:, b, hf, :], kb_f[:, :, :].rearrange("p h k -> p (h k)"),
                                           kb_hi[:, b, hf, :].bitcast(FP32), ALU.subtract)
                    if b == B - 1 and hf == HALVES - 1:
                        last.then_inc(kb_ready, 1)
                    else:
                        link(last)
            dve.wait_ge(ld_x, 16 * GROUPS)
            count[0], count[1] = count[0] + count[1], 0
            first = count[0]
            with dve.Fori(0, GROUPS - 1) as g:
                count[0], count[1] = g * DV_BODY + first, 0
                body(g, True)
                assert count[1] == DV_BODY, count
            count[0], count[1] = first + (GROUPS - 1) * DV_BODY, 0
            body(GROUPS - 1, False)

            dve.wait_ge(c_pool, 14)
            attention_over(dve)
            for t in range(TILES):
                last = V.max(top[:, t, :], logits[:, t, :])
            link(last)
            for t in range(TILES):
                last = V.max_index(top_i[:, t, :], top[:, t, :], logits[:, t, :])
            V.tensor_tensor(gap[:, :], top[:, :, 1], top[:, :, 0], ALU.subtract).then_inc(gap_ready, 1)
            link(V.memset(cum[:, 0, :], 0.0))
            link(V.tensor_copy(top_f[:, :, :], top_i[:, :, 0:TOPK].rearrange("p t k -> p k t")))
            for k in range(TOPK):
                last = V.tensor_tensor(chosen[:, k], top_f[:, k, :].unsqueeze(2).to_broadcast([P, TILES, NE]),
                                       iota_e[:, :].unsqueeze(1).to_broadcast([P, TILES, NE]), ALU.is_equal)
            link(last)
            V.tensor_tensor(both[:, :, :], chosen[:, 0], chosen[:, 1], ALU.add).then_inc(counts_in, 1)
            dve.wait_ge(ld_b1, 64)
            dve.wait_ge(b1_full, 1)
            V.tensor_copy(b1_t[:, :], t_bank[1][:, 2 * P:2 * P + (NE + 1) * HC])
            dve.wait_ge(counts_full, 1)
            V.tensor_copy(in_tile[:, :, :], t_bank[1][:, 0:P])
            link(V.tensor_copy(totals[:, :, :], t_bank[1][:, P:2 * P]))
            for t in range(TILES):
                link(V.tensor_tensor(cum[:, t + 1, :], cum[:, t, :], totals[:, t, :], ALU.add))
            link(V.tensor_scalar(thresholds[:, :], iota_e[:, :], float(BN), None, ALU.mult))
            link(V.tensor_tensor(over[:, :, :], cum[:, TILES, :].unsqueeze(2).to_broadcast([P, NE, NE]),
                                 thresholds[:, :].unsqueeze(1).to_broadcast([P, NE, NE]), ALU.is_gt))
            link(V.tensor_reduce(blocks_of[:, :], over[:, :, :], axis=AX.X, op=ALU.add))
            link(V.tensor_tensor(over[:, :, :], before_e[:, :, :], blocks_of[:, :].unsqueeze(1).to_broadcast([P, NE, NE]), ALU.mult))
            link(V.tensor_reduce(start[:, :], over[:, :, :], axis=AX.X, op=ALU.add))
            link(V.tensor_tensor(end[:, :], start[:, :], blocks_of[:, :], ALU.add))
            link(V.tensor_tensor(passed[:, :, :], end[:, :].unsqueeze(1).to_broadcast([P, BLOCKS, NE]),
                                 iota_b[:, :].unsqueeze(2).to_broadcast([P, BLOCKS, NE]), ALU.is_le))
            link(V.tensor_reduce(block_f[:, :], passed[:, :, :], axis=AX.X, op=ALU.add))
            V.tensor_scalar(block_e[:, :], block_f[:, :], float(NE - 1), None, ALU.min).then_inc(blocks_ready, 1)
            link(V.tensor_scalar(start[:, :], start[:, :], float(BN), None, ALU.mult))
            link(V.tensor_tensor(slot[:, :, :], cum[:, 0:TILES, :], in_tile[:, :, :], ALU.add))
            link(V.tensor_tensor(slot[:, :, :], slot[:, :, :], start[:, :].unsqueeze(1).to_broadcast([P, TILES, NE]), ALU.add))
            for k in range(TOPK):
                last = V.tensor_tensor(work[:, k], chosen[:, k], slot[:, :, :], ALU.mult)
            link(last)
            for k in range(TOPK):
                V.tensor_reduce(pos_f[:, k, :], work[:, k], axis=AX.X, op=ALU.add)
                last = V.tensor_reduce(none_f[:, k, :], chosen[:, k], axis=AX.X, op=ALU.add)
            link(last)
            link(V.tensor_scalar(none_f[:, :, :], none_f[:, :, :], -float(ROWS), float(ROWS), ALU.mult, ALU.add))
            V.tensor_tensor(pos[:, :, :], pos_f[:, :, :], none_f[:, :, :], ALU.add).then_inc(pos_ready, 1)
            dve.wait_ge(e_gap_ready, 1)
            link(V.tensor_scalar(gap[:, :], e_gap[:, :], 1.0, None, ALU.add))
            link(V.reciprocal(gap[:, :], gap[:, :]))
            dve.wait_ge(tanh_ready, 2)
            link(V.tensor_scalar(gates[:, 0, :], gap[:, :], tg_f[:, 0:1], None, ALU.mult))
            V.tensor_tensor(gates[:, 1, :], gates[:, 0, :], e_gap[:, :], ALU.mult)

            def set_b1(n, par, e):
                V.tensor_scalar(b1_now[:, par, :], b1_t[:, bass.ds(e * HC, HC)], 1.0, None, ALU.mult).then_inc(b1_set, 1)

            def split_fc(load, slot):
                for p in range(PAIRS):
                    cols = slice(p * 2 * P, (p + 1) * 2 * P)
                    dve.wait_ge(fc_his, load * PAIRS + p + 1)
                    V.tensor_tensor(fc_lo[:, :, cols], raw_fc[:, slot, :, cols], fc_hi[:, :, cols].bitcast(FP32), ALU.subtract)\
                     .then_inc(fc_ready, 1)

            def split_pj(p, load, slot):
                dve.wait_ge(pj_his, load * PAIRS + p + 1)
                rows_ = slice(2 * p, 2 * p + 2)
                V.tensor_tensor(pj_lo[:, rows_, :], raw_pj[:, slot, rows_, :], pj_hi[:, rows_, :].bitcast(FP32), ALU.subtract)\
                 .then_inc(pj_ready, 1)

            def split_x(n):
                dve.wait_ge(xt_his, n + 1)
                V.tensor_tensor(xt_lo[:, :, :], t_bank[0][:, :].rearrange("p (k n) -> p k n", k=KC), xt_hi[:, :, :].bitcast(FP32),
                                ALU.subtract).then_inc(xt_ready, 1)

            def block_of(n, par, pj, next_x, next_fc, next_e, e, shared, stored=None):
                for p in range(PAIRS):
                    pair = slice(2 * p, 2 * p + 2)
                    dve.wait_ge(h_act, n * PAIRS + p + 1 + H0)
                    if p == 0:
                        dve.wait_ge(y_full, n * BT + 1)
                    link(V.tensor_copy(ht_hi[:, pair, :], h_f[:, p]))
                    V.tensor_tensor(ht_lo[:, pair, :], h_f[:, p], ht_hi[:, pair, :].bitcast(FP32), ALU.subtract).then_inc(h_ready, 1)
                    if pj:
                        split_pj(p, *pj)
                if next_x:
                    split_x(n + 1)
                    set_b1(n + 1, 1 - par, next_e())
                if next_fc:
                    split_fc(*next_fc)
                if not shared:
                    dve.wait_ge(z_out[par], stored * 16 + 16)
                for i in range(BT):
                    dve.wait_ge(y_full, n * BT + i + 2)
                    ins = V.tensor_tensor(y_sb[:, par, i, :], m_bank[i][:, 0:D], b2_all[:, bass.ds(e, 1), :], ALU.add)
                    if i == 1 and shared:
                        pass
                    ins.then_inc(y_evac, 1)
                if shared:
                    dve.wait_ge(y_evac, n * BT + BT + BT)
                    xs = X[:, bass.ds(n * BT, BT), :]
                    V.scalar_tensor_tensor(xs, y_sb[:, par], tg_f[:, 0:1], xs, ALU.mult, ALU.add)

            def expert(t):
                return dve.value_load(block_e[0:1, bass.ds(t, 1)], min_val=0, max_val=NE - 1)

            def same():
                return NE

            split_x(0)
            link(V.memset(wait_taker[:, :], 0.0))
            set_b1(0, 0, NE)
            split_fc(0, 0)
            EXP_LINKS = PAIRS
            base = count[0] + count[1]

            def at(n):
                count[0], count[1] = n * EXP_LINKS + base, 0

            at(0)
            block_of(0, 0, (0, 0), True, None, same, NE, True)
            at(1)
            block_of(1, 1, None, True, None, same, NE, True)
            with dve.Fori(1, SHARED // 2 - 1) as i:
                at(i * 2)
                block_of(i * 2, 0, None, True, None, same, NE, True)
                at(i * 2 + 1)
                block_of(i * 2 + 1, 1, None, True, None, same, NE, True)
            at(SHARED - 2)
            block_of(SHARED - 2, 0, None, True, None, same, NE, True)
            dve.wait_ge(blocks_ready, 1)
            at(SHARED - 1)
            block_of(SHARED - 1, 1, None, True, (1, 1), lambda: expert(0), NE, True)
            with dve.Fori(0, (BLOCKS - 1) // 2) as i:
                at(i * 2 + SHARED)
                block_of(i * 2 + SHARED, 0, (i * 2 + 1, 1), True, (i * 2 + 2, 0), lambda: expert(i * 2 + 1), expert(i * 2), False, i)
                at(i * 2 + SHARED + 1)
                block_of(i * 2 + SHARED + 1, 1, (i * 2 + 2, 0), True, (i * 2 + 3, 1), lambda: expert(i * 2 + 2), expert(i * 2 + 1), False, i)
            at(NBLOCKS - 1)
            block_of(NBLOCKS - 1, 0, (BLOCKS, 1), False, None, None, expert(BLOCKS - 1), False, BLOCKS // 2)
            at(NBLOCKS)
            dve.wait_ge(gathered, 16 * TOPK * TILES)
            for q in range(GROUPS):
                for k in range(TOPK):
                    for t in range(q * GT, (q + 1) * GT):
                        last = V.scalar_tensor_tensor(X[:, t, :], zg[:, k, t, :], gates[:, k, t:t + 1], X[:, t, :], ALU.mult, ALU.add)
                    if k == 0:
                        link(last)
                last.then_inc(combined, 1)

    return nc


_INS = ['x', 'ctx_1024', 'mask_BxSxS2_ik1', 'g_xattn', 'g_ffn', 'L0_xattn_Wq', 'L0_xattn_bq', 'L0_xattn_Wk', 'L0_xattn_bk',
        'L0_xattn_Wv', 'L0_xattn_bv', 'L0_ffn_Wfc_s', 'L0_ffn_bfc_s', 'L0_ffn_Wproj_s', 'L0_ffn_bproj_s', 'L0_ffn_Wr',
        'L0_ffn_Wfc', 'L0_ffn_bfc', 'L0_ffn_Wproj', 'L0_ffn_bproj']
_OUTS = [((B, T, D), 'float32')]


def kernel(**inputs):
    import numpy as _np
    import concourse.bacc as _bacc
    from concourse import mybir as _mybir
    from concourse.bass_utils import run_bass_kernel_spmd as _run

    nc = _bacc.Bacc("TRN2", target_bir_lowering=False, num_devices=1)
    arrays, args = {}, []
    for name in _INS:
        a = _np.ascontiguousarray(inputs[name])
        arrays[f"in_{name}_dram"] = a
        args.append(nc.dram_tensor(f"in_{name}_dram", a.shape, _mybir.dt.from_np(a.dtype), kind="ExternalInput").ap())
    for i, (shape, dtype) in enumerate(_OUTS):
        dt = _mybir.dt.from_np(_np.dtype(dtype))
        args.append(nc.dram_tensor(f"out_{i}_dram", shape, dt, kind="ExternalOutput").ap())
    build(nc, *args)
    r = _run(nc, [arrays], core_ids=[0])
    return r.results[0]["out_0_dram"]
```

```python
from contextlib import ExitStack

import concourse.bass as bass
from concourse import mybir

FP32 = mybir.dt.float32
FP32R = mybir.dt.float32r
INT32 = mybir.dt.int32
ALU = mybir.AluOpType
ACT = mybir.ActivationFunctionType
AX = mybir.AxisListType

P = 128
B, T, D = 2, 1024, 256
KV = 154
H, HD = 16, 16
NE = 8
TILES = B * T // P
GT = 2
GROUPS = TILES // GT
GN = GT * P
KC = D // P
HALVES = H * HD // P
HH = H // HALVES
HW = HH * KV
HEADS = [(0, 3), (3, 3), (6, 2)]
NCH = -(-HW // P)
CHROWS = [min(P, HW - P * c) for c in range(NCH)]
CHUNKS = [(0, 4), (4, 4), (8, 2)]
STEPS = HALVES * GT
NB = len(HEADS)
UNITS = STEPS * NB
BG = T // GN
LATE_T = 4
LATE_LO = 5
PV_FIRST = {0: (4, 7), 2: (7, 10)}
PV_SECOND = {6: (0, 4), 7: (4, 7), 8: (7, 10)}
KVR = KV - P
MASKED = 1e30
HID = 4 * D
HC = HID // P
PAIRS = HC // 2
TOPK = 2
BT = 2
BN = BT * P
SHARED = TILES // BT
BLOCKS = TILES * TOPK // BT + NE - 1
ROWS = BLOCKS * BN
EPS = 1e-5
SQ = -1.0 / 16.0


def build(nc, x, ctx_kv, mask, g_xattn, g_ffn, wq, bq, wk, bk, wv, bv,
          wfc_s, bfc_s, wproj_s, bproj_s, wr, wfc, bfc, wproj, bproj, out):
    ctx = ExitStack()
    with ctx:
        def sb(name, shape, dt=FP32):
            return ctx.enter_context(nc.sbuf_tensor(name, shape, dt))

        def ps(name):
            return ctx.enter_context(nc.psum_tensor(name, [P, 512], FP32))

        def sem(name):
            return ctx.enter_context(nc.semaphore(name))

        x_rows = nc.dram_tensor("x_rows", [TILES * P, D], FP32, kind="Internal").ap()
        x_sorted = nc.dram_tensor("x_sorted", [ROWS, D], FP32, kind="Internal").ap()
        z_rows = nc.dram_tensor("z_rows", [ROWS, D], FP32, kind="Internal").ap()
        vx = [nc.dram_tensor(f"v_blocks_{n}", [B, HALVES, NCH * P, P], FP32, kind="Internal").ap() for n in ("hi", "lo")]

        X = sb("X", [P, TILES, D])
        bq_col = sb("bq_col", [P, HALVES])
        bk_col = sb("bk_col", [P, HALVES])
        bv_row = sb("bv_row", [P, D])
        gate_x = sb("gate_x", [P, 1])
        tg_x = sb("tg_x", [P, 1])
        wr_raw = sb("wr_raw", [P, KC, NE])
        bq_neg = sb("bq_neg", [P, HALVES])
        wr_parts = sb("wr_parts", [P, KC, 2, NE], FP32R)
        ident = sb("ident", [P, P])
        ident_r = sb("ident_r", [P, P], FP32R)
        zeros = sb("zeros", [P, NCH * P])
        head_rows = sb("head_rows", [P, HH])
        neg_half = sb("neg_half", [P, GT])
        negmax = sb("negmax", [P, 2, GT, HALVES, HH])
        psums = sb("psums", [P, 2, GT, HALVES, HH])
        wait_taker = sb("wait_taker", [P, 1])
        stats = sb("stats", [P, GT, 6])
        mv = sb("mv", [P, GT, 2])
        veps = sb("veps", [P, GT])
        rstd = sb("rstd", [P, GT])
        logits = sb("logits", [P, TILES, NE])
        gate_f = sb("gate_f", [P, 1])
        tg_f = sb("tg_f", [P, 1])
        e_const = sb("e_const", [P, TILES])
        iota_e = sb("iota_e", [P, NE])
        iota_b = sb("iota_b", [P, BLOCKS])
        before_e = sb("before_e", [P, NE, NE])
        ones = sb("ones", [P, P])
        before_p = sb("before_p", [P, P])
        b1_rows = sb("b1_rows", [(NE + 1) * HC, P])
        b1_t = sb("b1_t", [P, (NE + 1) * HC])
        b2_all = sb("b2_all", [P, NE + 1, D])
        pos = sb("pos", [P, TOPK, TILES], mybir.dt.uint32)
        gates = sb("gates", [P, TOPK, TILES])
        block_e = sb("block_e", [P, BLOCKS], INT32)

        attention = ExitStack()

        def att_sb(name, shape, dt=FP32):
            return attention.enter_context(nc.sbuf_tensor(name, shape, dt))

        kb_hi = att_sb("kb_hi", [P, B, HALVES, HW], FP32R)
        kb_lo = att_sb("kb_lo", [P, B, HALVES, HW], FP32R)
        mask_big = att_sb("mask_big", [P, TILES, KV], FP32R)
        vs = [att_sb(f"vs_{n}", [P, HALVES, NCH, P], FP32R) for n in ("hi", "lo")]
        y1 = att_sb("y1", [P, GT, D])
        y1t_hi = att_sb("y1t_hi", [P, KC, GN], FP32R)
        y1t_lo = att_sb("y1t_lo", [P, KC, GN], FP32R)
        q_hi = att_sb("q_hi", [P, HALVES, GN], FP32R)
        q_lo = att_sb("q_lo", [P, HALVES, GN], FP32R)
        prob = att_sb("prob", [P, STEPS, HW])
        wq_hi = att_sb("wq_hi", [P, KC, D], FP32R)
        wq_lo = att_sb("wq_lo", [P, KC, D], FP32R)
        k_hi = att_sb("k_hi", [P, HALVES, B, KV], FP32R)
        k_lo = att_sb("k_lo", [P, HALVES, B, KV], FP32R)

        early = ExitStack()

        def tmp(name, shape, dt=FP32):
            return early.enter_context(nc.sbuf_tensor(name, shape, dt))

        v_hi = tmp("v_hi", [P, B, D], FP32R)
        v_lo = tmp("v_lo", [P, B, D], FP32R)
        vr_hi = tmp("vr_hi", [KVR, B, D], FP32R)
        vr_lo = tmp("vr_lo", [KVR, B, D], FP32R)
        v_f = tmp("v_f", [P, B, D])
        vr_f = tmp("vr_f", [KVR, B, D])
        w3 = tmp("w3", [P, 3, KC, D])
        ctx_a = tmp("ctx_a", [P, B, D])
        ctx_b = tmp("ctx_b", [KVR, B, D])
        mask_i = tmp("mask_i", [P, TILES, KV], INT32)
        wk_t = tmp("wk_t", [P, KC, D])
        wv_t = tmp("wv_t", [P, KC, D])
        ctx_t = tmp("ctx_t", [P, KC, B, KV])
        k_t = tmp("k_t", [P, HALVES, B, KV])
        early.close()
        y2 = att_sb("y2", [P, GT, D])
        y2t_hi = att_sb("y2t_hi", [P, KC, GN], FP32R)
        y2t_lo = att_sb("y2t_lo", [P, KC, GN], FP32R)
        ot = att_sb("ot", [P, HALVES, GN])
        rden = att_sb("rden", [P, GT, HALVES, HH])
        some = att_sb("some", [P, GT])
        att = att_sb("att", [P, GT, D])
        pt_hi = att_sb("pt_hi", [P, HALVES, NCH, GN], FP32R)
        pt_lo = att_sb("pt_lo", [P, HALVES, NCH, GN], FP32R)
        attention.close()

        y2_all = sb("y2_all", [P, TILES, D])
        raw_fc = sb("raw_fc", [P, 2, KC, HID])
        raw_pj = sb("raw_pj", [P, 2, HC, D])
        fc_hi = sb("fc_hi", [P, KC, HID], FP32R)
        fc_lo = sb("fc_lo", [P, KC, HID], FP32R)
        pj_hi = sb("pj_hi", [P, HC, D], FP32R)
        pj_lo = sb("pj_lo", [P, HC, D], FP32R)
        xr = sb("xr", [P, BT, D])
        xt_hi = sb("xt_hi", [P, KC, BN], FP32R)
        xt_lo = sb("xt_lo", [P, KC, BN], FP32R)
        h_f = sb("h_f", [P, PAIRS, 2, BN])
        b1_now = sb("b1_now", [P, 2, HC])
        ht_hi = sb("ht_hi", [P, HC, BN], FP32R)
        ht_lo = sb("ht_lo", [P, HC, BN], FP32R)
        y_sb = sb("y_sb", [P, 2, BT, D])
        top = sb("top", [P, TILES, NE])
        top_i = sb("top_i", [P, TILES, NE], mybir.dt.uint32)
        top_f = sb("top_f", [P, TOPK, TILES])
        chosen = sb("chosen", [P, TOPK, TILES, NE])
        both = sb("both", [P, TILES, NE])
        in_tile = sb("in_tile", [P, TILES, NE])
        totals = sb("totals", [P, TILES, NE])
        cum = sb("cum", [P, TILES + 1, NE])
        slot = sb("slot", [P, TILES, NE])
        work = sb("work", [P, TOPK, TILES, NE])
        over = sb("over", [P, NE, NE])
        thresholds = sb("thresholds", [P, NE])
        blocks_of = sb("blocks_of", [P, NE])
        start = sb("start", [P, NE])
        end = sb("end", [P, NE])
        passed = sb("passed", [P, BLOCKS, NE])
        block_f = sb("block_f", [P, BLOCKS])
        gap = sb("gap", [P, TILES])
        e_gap = sb("e_gap", [P, TILES])
        pos_f = sb("pos_f", [P, TOPK, TILES])
        none_f = sb("none_f", [P, TOPK, TILES])
        zg = sb("zg", [P, TOPK, TILES, D])


        s_bank = [ps(f"scores_{i}") for i in range(4)]
        t_bank = [ps(f"turned_{i}") for i in range(2)]
        m_bank = [ps(f"misc_{i}") for i in range(2)]

        ld_w = sem("ld_w")
        ld_c = sem("ld_c")
        ld_x = sem("ld_x")
        ld_m = sem("ld_m")
        ld_small = sem("ld_small")
        ld_v = [sem("ld_v_0"), sem("ld_v_1")]
        ld_x_rest = sem("ld_x_rest")
        y2_in = sem("y2_in")
        vx_zero = sem("vx_zero")
        vx_in = sem("vx_in")
        consts = sem("consts")
        c_pool = sem("c_pool")
        prep_full = sem("prep_full")
        wq_ready = sem("wq_ready")
        wkv_ready = sem("wkv_ready")
        ctx_ready = sem("ctx_ready")
        k_ready = sem("k_ready")
        k_hi_ready = sem("k_hi_ready")
        v_added = sem("v_added")
        v_hi_ready = sem("v_hi_ready")
        v_ready = sem("v_ready")
        mask_ready = sem("mask_ready")
        kb_ready = [sem("kb_ready_0"), sem("kb_ready_1")]
        tanh_ready = sem("tanh_ready")
        veps_ready = sem("veps_ready")
        rstd_ready = sem("rstd_ready")
        y1_ready = sem("y1_ready")
        y2_ready = sem("y2_ready")
        s_full = sem("s_full")
        s_max = sem("s_max")
        s_free = sem("s_free")
        t_full = sem("t_full")
        t_hi = sem("t_hi")
        t_free = sem("t_free")
        pv_done = sem("pv_done")
        m_full = sem("m_full")
        m_hi = sem("m_hi")
        m_free = sem("m_free")
        ot_done = sem("ot_done")
        dv = sem("dv")
        x_zero = sem("x_zero")
        rows_stored = sem("rows_stored")
        ld_b1 = sem("ld_b1")
        counts_in = sem("counts_in")
        counts_full = sem("counts_full")
        b1_full = sem("b1_full")
        gap_ready = sem("gap_ready")
        e_gap_ready = sem("e_gap_ready")
        blocks_ready = sem("blocks_ready")
        pos_ready = sem("pos_ready")
        scattered = sem("scattered")
        gathered = sem("gathered")
        fc_in = [sem("fc_in_0"), sem("fc_in_1")]
        pj_in = [sem("pj_in_0"), sem("pj_in_1")]
        fc_his = sem("fc_his")
        fc_ready = sem("fc_ready")
        pj_his = sem("pj_his")
        pj_ready = sem("pj_ready")
        x_in = sem("x_in")
        xt_full = sem("xt_full")
        xt_his = sem("xt_his")
        xt_ready = sem("xt_ready")
        b1_set = sem("b1_set")
        h_full = sem("h_full")
        h_act = sem("h_act")
        h_ready = sem("h_ready")
        y_full = sem("y_full")
        y_evac = sem("y_evac")
        z_out = [sem("z_out_0"), sem("z_out_1")]
        combined = sem("combined")
        out_done = sem("out_done")

        block = ctx.enter_context(nc.Block())

        pv_bank, misc_bank = m_bank
        M_ALL = 5 * GROUPS

        def m_base(g, before):
            return (2, 4, g * 5 - 3)[before]

        def hi_base(g, before):
            return (2, 4, g * 3)[before]

        def unit(v):
            n, i = divmod(v % UNITS, NB)
            return (n, i) + divmod(n, GT)

        def rows(c0, m):
            if CHROWS[c0 + m - 1] == CHROWS[c0]:
                return [(CHROWS[c0], c0, c0 + m)]
            return [(CHROWS[c0], c0, c0 + m - 1), (CHROWS[c0 + m - 1], c0 + m - 1, c0 + m)]

        H0 = PAIRS
        NBLOCKS = SHARED + BLOCKS

        def attention_over(eng):
            eng.wait_ge(m_free, M_ALL + 1)

        @block.sync
        def _(sp):
            with nc.allow_non_contiguous_dma(reason="small columns"):
                for i, w in enumerate((wq, wk, wv)):
                    sp.dma_start(w3[:, i], w.rearrange("(o p) i -> p o i", p=P)).then_inc(ld_w, 16)
                sp.dma_start(ctx_a[:, :, :], ctx_kv[:, 0:P, :].rearrange("b p d -> p b d")).then_inc(ld_c, 16)
                sp.dma_start(ctx_b[:, :, :], ctx_kv[:, P:KV, :].rearrange("b p d -> p b d")).then_inc(ld_c, 16)
                sp.dma_start(X[:, 0:GT], x[0, 0:GN].rearrange("(t p) d -> p t d", p=P)).then_inc(ld_x, 16)
                sp.dma_start(bq_col[:, :], bq.rearrange("(o p) -> p o", p=P)).then_inc(ld_small, 16)
                sp.dma_start(bk_col[:, :], bk.rearrange("(o p) -> p o", p=P)).then_inc(ld_small, 16)
                sp.dma_start(bv_row[:, :], bv.rearrange("(a n) -> a n", a=1).to_broadcast([P, D])).then_inc(ld_small, 16)
                sp.dma_start(gate_x[:, :], g_xattn.rearrange("(a n) -> a n", a=1).to_broadcast([P, 1])).then_inc(ld_small, 16)
                sp.dma_start(wr_raw[:, :, :], wr.rearrange("(k p) e -> p k e", p=P)).then_inc(ld_small, 16)
                sp.dma_start(gate_f[:, :], g_ffn.rearrange("(a n) -> a n", a=1).to_broadcast([P, 1])).then_inc(ld_small, 16)
                sp.dma_start(mask_i[:, :, :], mask.rearrange("b (t p) k -> p (b t) k", p=P)).then_inc(ld_m, 16)
                for g in range(1, GROUPS):
                    b, t0 = g * GN // T, g * GN % T
                    sp.dma_start(X[:, g * GT:(g + 1) * GT],
                                 x[b, t0:t0 + GN].rearrange("(t p) d -> p t d", p=P)).then_inc(ld_x_rest, 16)
                sp.dma_start(b1_rows[0:NE * HC, :], bfc.rearrange("e (c p) -> (e c) p", p=P)).then_inc(ld_b1, 16)
                sp.dma_start(b1_rows[NE * HC:(NE + 1) * HC, :], bfc_s.rearrange("(c p) -> c p", p=P)).then_inc(ld_b1, 16)
                sp.dma_start(b2_all[:, 0:NE, :], bproj.rearrange("(a e) n -> a e n", a=1).to_broadcast([P, NE, D])).then_inc(ld_b1, 16)
                sp.dma_start(b2_all[:, NE, :], bproj_s.rearrange("(a n) -> a n", a=1).to_broadcast([P, D])).then_inc(ld_b1, 16)
                sp.wait_ge(consts, 1)
                for t in vx:
                    for b in range(B):
                        for h in range(HALVES):
                            sp.dma_start(t[b, h].rearrange("(p c) f -> p (c f)", p=P), zeros[:, :]).then_inc(vx_zero, 16)
                sp.wait_ge(vx_zero, 16 * 2 * B * HALVES)
                sp.wait_ge(v_ready, 2)
                for t, va, vb in zip(vx, (v_hi, v_lo), (vr_hi, vr_lo)):
                    for b in range(B):
                        for hf in range(HALVES):
                            for src, r0, n in ((va, 0, P), (vb, P, KVR)):
                                dst = bass.AP(t.tensor, t[b, hf].offset + r0 * P, [[P, n], [KV * P + HD, HH], [1, HD]])
                                sp.dma_start(dst, src[:, b, hf * P:(hf + 1) * P].rearrange("p (h f) -> p h f", h=HH).bitcast(FP32)).then_inc(vx_in, 16)
                sp.wait_ge(vx_in, 16 * 4 * B * HALVES)
                def load_v(b, hf):
                    for n in range(2):
                        sp.dma_start(vs[n][:, hf].bitcast(FP32), vx[n][b, hf].rearrange("(c p) f -> p c f", p=P)).then_inc(ld_v[hf], 16)

                def store_y2(g0, g1):
                    with sp.Fori(g0, g1) as g:
                        sp.wait_ge(y2_ready, g + 1)
                        sp.dma_start(x_rows[bass.ds(g * GN, GN), :].rearrange("(t p) d -> p t d", p=P), y2[:, :, :]).then_inc(rows_stored, 16)

                for hf in range(HALVES):
                    load_v(0, hf)
                blank = x_sorted.rearrange("(p r) d -> p (r d)", p=P)
                for a in range(0, ROWS * D // P, NCH * P):
                    z = min(a + NCH * P, ROWS * D // P)
                    sp.dma_start(blank[:, a:z], zeros[:, 0:z - a]).then_inc(x_zero, 16)
                store_y2(0, BG - 1)
                for hf in range(HALVES):
                    sp.wait_ge(pv_done, (BG - 1) * 2 + hf + 3)
                    load_v(1, hf)
                store_y2(BG - 1, GROUPS)

                attention_over(sp)

                def load_fc(slot, w):
                    sp.dma_start(raw_fc[:, slot], w.rearrange("a (k p) n -> p (a k) n", p=P)).then_inc(fc_in[slot], 16)

                def load_pj(slot, w):
                    for half in range(2):
                        sp.dma_start(raw_pj[:, slot, half * HC // 2:(half + 1) * HC // 2],
                                     w[:, half * HID // 2:(half + 1) * HID // 2].rearrange("a (c p) n -> p (a c) n", p=P)).then_inc(pj_in[slot], 16)

                def load_x(rows, r):
                    sp.dma_start(xr[:, :, :], rows[bass.ds(r, BN), :].rearrange("(t p) d -> p t d", p=P)).then_inc(x_in, 16)

                def expert(t):
                    return sp.value_load(block_e[0:1, bass.ds(t, 1)], min_val=0, max_val=NE - 1)

                sp.wait_ge(rows_stored, 16 * GROUPS + 16)
                load_x(x_rows, 0)
                load_fc(0, wfc_s.rearrange("(a k) n -> a k n", a=1))
                load_pj(0, wproj_s.rearrange("(a k) n -> a k n", a=1))
                sp.dma_start(y2_all[:, :, :], x_rows.rearrange("(t p) d -> p t d", p=P)).then_inc(y2_in, 16)
                with sp.Fori(1, SHARED) as n:
                    sp.wait_ge(xt_full, n)
                    load_x(x_rows, n * BN)
                sp.wait_ge(blocks_ready, 1)
                e = expert(0)
                load_fc(1, wfc[bass.ds(e, 1)])
                load_pj(1, wproj[bass.ds(e, 1)])
                sp.wait_ge(xt_full, SHARED)
                sp.wait_ge(scattered, 16 * TOPK * TILES)
                load_x(x_sorted, 0)
                e = expert(1)
                sp.wait_ge(fc_ready, PAIRS)
                load_fc(0, wfc[bass.ds(e, 1)])
                sp.wait_ge(pj_ready, PAIRS)
                load_pj(0, wproj[bass.ds(e, 1)])

                def store_z(t, par):
                    sp.wait_ge(y_evac, (t + SHARED + 2) * BT)
                    sp.dma_start(z_rows[bass.ds(t * BN, BN), :].rearrange("(t p) d -> p t d", p=P), y_sb[:, par]).then_inc(z_out[par], 16)

                def body(t, par, x_next, store, w_next):
                    if x_next:
                        sp.wait_ge(xt_full, t + SHARED + 1)
                        load_x(x_sorted, (t + 1) * BN)
                    if store:
                        store_z(t - 1, 1 - par)
                    if w_next:
                        e = expert(t + 2)
                        sp.wait_ge(fc_ready, (t + 2) * PAIRS)
                        load_fc(1 - par, wfc[bass.ds(e, 1)])
                        sp.wait_ge(pj_ready, (t + 2) * PAIRS)
                        load_pj(1 - par, wproj[bass.ds(e, 1)])

                body(0, 0, True, False, True)
                with sp.Fori(0, (BLOCKS - 3) // 2) as i:
                    body(i * 2 + 1, 1, True, True, True)
                    body(i * 2 + 2, 0, True, True, True)
                body(BLOCKS - 2, 1, True, True, False)
                body(BLOCKS - 1, 0, False, True, False)
                store_z(BLOCKS - 1, 0)
                for q in range(GROUPS):
                    b, t0 = q * GN // T, q * GN % T
                    sp.wait_ge(combined, q + 1)
                    sp.dma_start(out[b, t0:t0 + GN].rearrange("(t p) d -> p t d", p=P), X[:, q * GT:(q + 1) * GT]).then_inc(out_done, 16)
                sp.wait_ge(out_done, 16 * GROUPS)

        @block.gpsimd
        def _(pool):
            nc.gpsimd.memset(zeros[:, :], 0.0).then_inc(consts, 1)
            nc.gpsimd.memset(ident[:, :], 0.0).then_inc(c_pool, 1)
            nc.gpsimd.memset(head_rows[:, :], 1.0).then_inc(c_pool, 1)
            nc.gpsimd.memset(neg_half[:, :], -0.5).then_inc(c_pool, 1)
            pool.sem_inc(s_free, 4)
            pool.sem_inc(t_full, UNITS - NB + 1)
            pool.sem_inc(t_free, 2)
            pool.sem_inc(pv_done, 2)
            pool.sem_inc(m_free, 1)
            pool.sem_inc(ot_done, 1)
            pool.sem_inc(rows_stored, 16)
            pool.sem_inc(h_act, PAIRS)
            pool.sem_inc(h_ready, PAIRS)
            pool.sem_inc(y_evac, BT)
            pool.sem_inc(y_full, 1)
            pool.sem_inc(z_out[0], 16)
            pool.sem_inc(z_out[1], 16)
            pool.wait_ge(c_pool, 3)
            nc.gpsimd.affine_select(out=ident[:, :], in_=ident[:, :], compare_op=ALU.not_equal, fill=1.0,
                                    base=0, pattern=[[-1, P]], channel_multiplier=1).then_inc(consts, 1)
            nc.gpsimd.affine_select(out=head_rows[:, :], in_=head_rows[:, :], compare_op=ALU.is_ge, fill=0.0,
                                    base=0, pattern=[[-HD, HH]], channel_multiplier=1).then_inc(c_pool, 1)
            pool.wait_ge(c_pool, 4)
            nc.gpsimd.affine_select(out=head_rows[:, :], in_=head_rows[:, :], compare_op=ALU.is_ge, fill=0.0,
                                    base=HD - 1, pattern=[[HD, HH]], channel_multiplier=-1).then_inc(consts, 1)

            nc.gpsimd.memset(e_const[:, :], 2.718281828459045).then_inc(c_pool, 1)
            nc.gpsimd.memset(ones[:, :], 1.0).then_inc(c_pool, 1)
            nc.gpsimd.memset(before_p[:, :], 1.0).then_inc(c_pool, 1)
            nc.gpsimd.memset(before_e[:, :, :], 1.0).then_inc(c_pool, 1)
            nc.gpsimd.iota(iota_e[:, :], pattern=[[1, NE]], base=0, channel_multiplier=0, allow_small_or_imprecise_dtypes=True).then_inc(c_pool, 1)
            nc.gpsimd.iota(iota_b[:, :], pattern=[[1, BLOCKS]], base=0, channel_multiplier=0, allow_small_or_imprecise_dtypes=True).then_inc(c_pool, 1)
            pool.wait_ge(c_pool, 10)
            nc.gpsimd.affine_select(out=before_p[:, :], in_=before_p[:, :], compare_op=ALU.is_gt, fill=0.0,
                                    base=0, pattern=[[1, P]], channel_multiplier=-1).then_inc(c_pool, 1)
            nc.gpsimd.affine_select(out=before_e[:, :, :], in_=before_e[:, :, :], compare_op=ALU.is_gt, fill=0.0,
                                    base=0, pattern=[[1, NE], [-1, NE]], channel_multiplier=0).then_inc(c_pool, 1)

            with pool.Fori(0, 2 * GROUPS) as n:
                pool.wait_ge(veps_ready, n + 1)
                nc.gpsimd.tensor_tensor(rstd[:, :], veps[:, :], neg_half[:, :], ALU.pow).then_inc(rstd_ready, 1)

            pool.wait_ge(gap_ready, 1)
            nc.gpsimd.tensor_tensor(e_gap[:, :], e_const[:, :], gap[:, :], ALU.pow).then_inc(e_gap_ready, 1)
            pool.wait_ge(x_zero, 16 * -(-ROWS * D // P // (NCH * P)))
            pool.wait_ge(pos_ready, 1)
            pool.wait_ge(y2_in, 16)
            for t in range(TILES):
                for k in range(TOPK):
                    nc.gpsimd.indirect_dma_start(out=x_sorted, out_offset=bass.IndirectOffsetOnAxis(ap=pos[:, k, t:t + 1], axis=0),
                                                 in_=y2_all[:, t, :], in_offset=None, bounds_check=ROWS - 1, oob_is_err=False)\
                      .then_inc(scattered, 16)
            nc.gpsimd.memset(zg[:, :, :, :], 0.0).then_inc(c_pool, 1)
            pool.wait_ge(c_pool, 13)
            pool.wait_ge(z_out[0], 16 * ((BLOCKS + 1) // 2 + 1))
            pool.wait_ge(z_out[1], 16 * (BLOCKS // 2 + 1))
            for t in range(TILES):
                for k in range(TOPK):
                    nc.gpsimd.indirect_dma_start(out=zg[:, k, t, :], out_offset=None, in_=z_rows,
                                                 in_offset=bass.IndirectOffsetOnAxis(ap=pos[:, k, t:t + 1], axis=0),
                                                 bounds_check=ROWS - 1, oob_is_err=False).then_inc(gathered, 16)

        @block.tensor
        def _(pe):
            mm = nc.tensor.matmul
            pe.wait_ge(consts, 2)
            pe.wait_ge(ld_w, 48)
            for i in range(3):
                for k in range(KC):
                    for o in range(KC):
                        last = nc.tensor.transpose(s_bank[i][:, k * D + o * P:k * D + (o + 1) * P], w3[:, i, o, k * P:(k + 1) * P], ident[:, :])
                last.then_inc(prep_full, 1)
            pe.wait_ge(ld_c, 32)
            for k in range(KC):
                bank = (s_bank[3], t_bank[0])[k]
                for b in range(B):
                    nc.tensor.transpose(bank[:, b * KV:b * KV + P], ctx_a[:, b, k * P:(k + 1) * P], ident[:, :])
                    last = nc.tensor.transpose(bank[:, b * KV + P:(b + 1) * KV], ctx_b[:, b, k * P:(k + 1) * P], ident[0:KVR, 0:KVR])
                last.then_inc(prep_full, 1)
            pe.wait_ge(wkv_ready, 2)
            pe.wait_ge(ctx_ready, 2)
            for hf in range(HALVES):
                bank = (t_bank[1], pv_bank)[hf]
                for k in range(KC):
                    last = mm(bank[:, 0:B * KV], wk_t[:, k, hf * P:(hf + 1) * P], ctx_t[:, k].rearrange("p b k -> p (b k)"),
                              start=k == 0, stop=k == KC - 1)
                last.then_inc(prep_full, 1)

            def y_turned(use, y):
                pe.wait_ge(m_free, use + 1)
                for k in range(KC):
                    for j in range(GT):
                        last = nc.tensor.transpose(misc_bank[:, (k * GT + j) * P:(k * GT + j + 1) * P], y[:, j, k * P:(k + 1) * P], ident[:, :])
                last.then_inc(m_full, 1)

            def q_product(use):
                pe.wait_ge(m_free, use + 1)
                for hf in range(HALVES):
                    for k in range(KC):
                        for i, (w, y) in enumerate(((wq_hi, y1t_hi), (wq_lo, y1t_hi), (wq_hi, y1t_lo))):
                            last = mm(misc_bank[:, hf * GN:(hf + 1) * GN], w[:, k, hf * P:(hf + 1) * P], y[:, k, :],
                                      start=k == 0 and i == 0, stop=k == KC - 1 and i == 2)
                last.then_inc(m_full, 1)

            pe.wait_ge(y1_ready, 1)
            y_turned(0, y1)
            pe.wait_ge(wq_ready, 1)
            q_product(1)
            pe.wait_ge(k_ready, 1)
            for bank, r0, n in ((t_bank[0], 0, P), (t_bank[1], P, KVR)):
                for b in range(B):
                    for k in range(KC):
                        last = mm(bank[0:n, b * D:(b + 1) * D], ctx_t[:, k, b, r0:r0 + n], wv_t[:, k, :], start=k == 0, stop=k == KC - 1)
                last.then_inc(prep_full, 1)

            def scores(g, b, u):
                n, i, hf, j = unit(u)
                h0, nh = HEADS[i]
                ql, qh = (q[:, hf, j * P:(j + 1) * P] for q in (q_lo, q_hi))
                pe.wait_ge(s_free, g * UNITS + u + 1)
                out = s_bank[u % 4][:, 0:nh * KV]
                cols = slice(h0 * KV, (h0 + nh) * KV)
                kh = kb_hi[:, bass.ds(b, 1), hf, cols]
                kl = kb_lo[:, bass.ds(b, 1), hf, cols]
                mm(out, qh, kh, start=True, stop=False)
                mm(out, qh, kl, start=False, stop=False)
                mm(out, ql, kh, start=False, stop=False)
                mm(out, ident_r[:, :], mask_big[:, bass.ds(g * GT + j, 1), :].to_broadcast([P, nh, KV]), start=False, stop=True)\
                    .then_inc(s_full, 1)

            def turn(g, v):
                n, i, hf, j = unit(v)
                c0, m = CHUNKS[i]
                pe.wait_ge(s_free, g * UNITS + v + (2 if i < NB - 1 else 1) + 4)
                pe.wait_ge(t_free, g * UNITS + v + 1)
                for c in range(c0, c0 + m):
                    r = CHROWS[c]
                    last = nc.tensor.transpose(t_bank[v % 2][0:r, (c - c0) * P:(c - c0 + 1) * P],
                                               prob[:, n, c * P:c * P + r], ident[:, :])
                last.then_inc(t_full, 1)

            def pv(hf, c0, c1):
                for c in range(c0, c1):
                    r = CHROWS[c]
                    for i, (v, p) in enumerate(((vs[0], pt_hi), (vs[1], pt_hi), (vs[0], pt_lo))):
                        last = mm(pv_bank[:, hf * GN:(hf + 1) * GN], v[0:r, hf, c, :], p[0:r, hf, c, :],
                                  start=c == 0 and i == 0, stop=c == NCH - 1 and i == 2)
                if c1 == NCH:
                    last.then_inc(pv_done, 1)

            def pv_inputs(b, hf, turned):
                pe.wait_ge(ld_v[hf], b * 32 + 32)
                pe.wait_ge(t_free, turned + 2)

            def out_turned(g, use):
                pe.wait_ge(ot_done, g + 1)
                pe.wait_ge(m_free, use + 1)
                for hf in range(HALVES):
                    for j in range(GT):
                        last = nc.tensor.transpose(misc_bank[:, j * D + hf * P:j * D + (hf + 1) * P], ot[:, hf, j * P:(j + 1) * P], ident[:, :])
                last.then_inc(m_full, 1)

            def router_logits(use):
                pe.wait_ge(m_free, use + 1)
                for j in range(GT):
                    for k in range(KC):
                        for i, y in enumerate((y2t_hi, y2t_lo)):
                            last = mm(misc_bank[:, j * 2 * NE:(j + 1) * 2 * NE], y[:, k, j * P:(j + 1) * P],
                                      wr_parts[:, k].rearrange("p a e -> p (a e)"), start=k == 0 and i == 0, stop=k == KC - 1 and i == 1)
                last.then_inc(m_full, 1)

            def body(g, b, b_before, before, more):
                base = m_base(g, before)
                pe.wait_ge(m_free, base + 1)
                for u in range(UNITS):
                    scores(g, b, u)
                    if u == 1 and before == 2:
                        pe.wait_ge(y2_ready, g - 1)
                        y_turned(base, y2)
                    if u == 3 and before == 2:
                        router_logits(base + 1)
                        base += 2
                    if u in PV_FIRST and before:
                        pv(0, *PV_FIRST[u])
                    if u in PV_SECOND and before:
                        if PV_SECOND[u][0] == 0:
                            pv_inputs(b_before, 1, g * UNITS)
                        pv(1, *PV_SECOND[u])
                    if u == 6 and more:
                        pe.wait_ge(y1_ready, g + 2)
                        y_turned(base, y1)
                        base += 1
                    if u == 10 and before:
                        out_turned(g, base)
                        base += 1
                    if u == 11 and more:
                        q_product(base)
                    if u == LATE_T and not before:
                        pe.wait_ge(v_added, 2)
                    if u >= LATE_T or before:
                        turn(g, u - LATE_T)
                pe.wait_ge(ot_done, g + 1)
                pv_inputs(b, 0, g * UNITS + UNITS // 2)
                pv(0, 0, PV_FIRST[0][0])

            pe.wait_ge(kb_ready[0], 2 * HALVES)
            pe.wait_ge(mask_ready, 1)
            body(0, 0, 0, 0, True)
            pe.wait_ge(kb_ready[1], 2 * HALVES)
            body(1, 0, 0, 1, True)
            with pe.Fori(1, GROUPS // 2 - 1) as i:
                body(i * 2, (i * 2) // BG, (i * 2 - 1) // BG, 2, True)
                body(i * 2 + 1, (i * 2 + 1) // BG, (i * 2) // BG, 2, True)
            body(GROUPS - 2, B - 1, B - 1, 2, True)
            body(GROUPS - 1, B - 1, B - 1, 2, False)
            for u in PV_FIRST:
                pv(0, *PV_FIRST[u])
            pe.wait_ge(y2_ready, GROUPS - 1)
            y_turned(M_ALL - 5, y2)
            for u in range(LATE_T):
                turn(GROUPS, u - LATE_T)
            router_logits(M_ALL - 4)
            pv_inputs(B - 1, 1, GROUPS * UNITS)
            pv(1, 0, NCH)
            out_turned(GROUPS, M_ALL - 3)
            pe.wait_ge(y2_ready, GROUPS)
            y_turned(M_ALL - 2, y2)
            router_logits(M_ALL - 1)

            pe.wait_ge(counts_in, 1)
            mm(t_bank[1][:, 0:P], before_p[:, :], both[:, :, :].rearrange("p t e -> p (t e)"), start=True, stop=True)
            mm(t_bank[1][:, P:2 * P], ones[:, :], both[:, :, :].rearrange("p t e -> p (t e)"), start=True, stop=True)\
                .then_inc(counts_full, 1)

            def turn_x(n):
                pe.wait_ge(x_in, (n + 1) * 16)
                pe.wait_ge(xt_ready, n)
                for k in range(KC):
                    for i in range(BT):
                        last = nc.tensor.transpose(t_bank[0][:, (k * BT + i) * P:(k * BT + i + 1) * P], xr[:, i, k * P:(k + 1) * P], ident[:, :])
                last.then_inc(xt_full, 1)

            def block_of(n, load, next_x):
                pe.wait_ge(xt_ready, n + 1)
                for p in range(PAIRS):
                    pe.wait_ge(fc_ready, load * PAIRS + p + 1)
                    pe.wait_ge(h_act, n * PAIRS + p + 1)
                    for c in (0, 1):
                        hid = slice((2 * p + c) * P, (2 * p + c + 1) * P)
                        for k in range(KC):
                            for i, (w, xx) in enumerate(((fc_hi, xt_hi), (fc_lo, xt_hi), (fc_hi, xt_lo))):
                                last = mm(s_bank[p][:, c * BN:(c + 1) * BN], w[:, k, hid], xx[:, k, :],
                                          start=k == 0 and i == 0, stop=k == KC - 1 and i == 2)
                    last.then_inc(h_full, 1)
                if next_x:
                    turn_x(n + 1)
                for i in range(BT):
                    pe.wait_ge(y_evac, n * BT + i + 1)
                    for c in range(HC):
                        if i == 0 and c % 2 == 0:
                            pe.wait_ge(pj_ready, load * PAIRS + c // 2 + 1)
                            pe.wait_ge(h_ready, n * PAIRS + c // 2 + 1 + H0)
                        for j, (h, w) in enumerate(((ht_hi, pj_hi), (ht_hi, pj_lo), (ht_lo, pj_hi))):
                            last = mm(m_bank[i][:, 0:D], h[:, c, i * P:(i + 1) * P], w[:, c, :], start=c == 0 and j == 0, stop=c == HC - 1 and j == 2)
                    last.then_inc(y_full, 1)

            nc_b1 = nc.tensor.transpose(t_bank[1][:, 2 * P:2 * P + (NE + 1) * HC], b1_rows[:, :], ident[0:(NE + 1) * HC, 0:(NE + 1) * HC])
            nc_b1.then_inc(b1_full, 1)
            turn_x(0)
            with pe.Fori(0, SHARED) as n:
                block_of(n, 0, True)
            with pe.Fori(0, BLOCKS - 1) as t:
                block_of(t + SHARED, t + 1, True)
            block_of(NBLOCKS - 1, BLOCKS, False)

        @block.scalar
        def _(act):
            A = nc.scalar.activation
            act.wait_ge(ld_small, 16 * 6)
            A(tg_x[:, :], gate_x[:, :], ACT.Tanh).then_inc(tanh_ready, 1)
            A(tg_f[:, :], gate_f[:, :], ACT.Tanh).then_inc(tanh_ready, 1)

            def hi_of(out, use):
                act.wait_ge(m_full, use + 1)
                A(out, misc_bank[:, :], ACT.Copy).then_inc(m_hi, 1)

            def q_hi_of(use):
                act.wait_ge(m_full, use + 1)
                for hf in range(HALVES):
                    last = A(q_hi[:, hf, :], misc_bank[:, hf * GN:(hf + 1) * GN], ACT.Identity, bias=bq_neg[:, hf:hf + 1])
                last.then_inc(m_hi, 1)

            def kb_low(b, hf):
                for h in range(HH):
                    last = A(kb_lo[:, b, hf, h * KV:(h + 1) * KV], k_lo[:, hf, b, :], ACT.Copy, scale=head_rows[:, h:h + 1])
                last.then_inc(kb_ready[b], 1)

            def exps(g, par, u):
                n, i, hf, j = unit(u)
                h0, nh = HEADS[i]
                if i == 0:
                    act.wait_ge(t_full, g * UNITS + u + 1)
                act.wait_ge(s_max, g * UNITS + u + 1)
                for h in range(h0, h0 + nh):
                    last = A(prob[:, n, h * KV:(h + 1) * KV], s_bank[u % 4][:, (h - h0) * KV:(h - h0 + 1) * KV], ACT.Exp,
                             bias=negmax[:, par, j, hf, h:h + 1], scale=-1.0, accum_out=psums[:, par, j, hf, h:h + 1])
                last.then_inc(s_free, 1)

            def turned_hi(g, v):
                n, i, hf, j = unit(v)
                c0, m = CHUNKS[i]
                if j == 0 and i == 0:
                    act.wait_ge(pv_done, g * 2 + hf + 1)
                act.wait_ge(t_full, g * UNITS + v + 1 + UNITS - NB + 1)
                for r, a, z in rows(c0, m):
                    last = A(pt_hi[0:r, hf, a:z, j * P:(j + 1) * P],
                             t_bank[v % 2][0:r, (a - c0) * P:(z - c0) * P].rearrange("p (c q) -> p c q", q=P), ACT.Copy)
                last.then_inc(t_hi, 1)

            def out_copied(g):
                act.wait_ge(pv_done, g * 2 + 2)
                A(ot[:, :, :], pv_bank[:, :], ACT.Copy).then_inc(ot_done, 1)

            def body(g, par, before, more):
                base = m_base(g, before)
                for u in range(UNITS):
                    exps(g, par, u)
                    if u == 1 and before == 2:
                        hi_of(y2t_hi[:, :, :], base)
                        base += 2
                    if u == 7 and more:
                        hi_of(y1t_hi[:, :, :], base)
                        base += 1
                    if u == 9 and before:
                        out_copied(g)
                        base += 1
                    if u == 11 and more:
                        q_hi_of(base)
                    if u in (6, 9) and not before:
                        kb_low(1, (u - 6) // 3)
                    if u >= LATE_T or before:
                        turned_hi(g, u - LATE_T)

            for i, w in ((1, wk_t), (2, wv_t)):
                act.wait_ge(prep_full, 1 + i)
                A(w[:, :, :], s_bank[i][:, :], ACT.Copy).then_inc(wkv_ready, 1)
            act.wait_ge(prep_full, 4)
            A(ctx_t[:, 0], s_bank[3][:, 0:B * KV], ACT.Copy).then_inc(ctx_ready, 1)
            act.wait_ge(k_ready, 1)
            A(k_hi[:, :, :, :], k_t[:, :, :, :], ACT.Copy).then_inc(k_hi_ready, 1)
            hi_of(y1t_hi[:, :, :], 0)
            act.wait_ge(k_ready, 2)
            act.wait_ge(consts, 3)
            kb_low(0, 0)
            q_hi_of(1)
            kb_low(0, 1)
            for i, (f, h) in enumerate(((v_f, v_hi), (vr_f, vr_hi))):
                act.wait_ge(v_added, i + 1)
                A(h[:, :, :], f[:, :, :], ACT.Copy).then_inc(v_hi_ready, 1)
            body(0, 0, 0, True)
            body(1, 1, 1, True)
            with act.Fori(1, GROUPS // 2 - 1) as i:
                body(i * 2, 0, 2, True)
                body(i * 2 + 1, 1, 2, True)
            body(GROUPS - 2, 0, 2, True)
            body(GROUPS - 1, 1, 2, False)
            hi_of(y2t_hi[:, :, :], M_ALL - 5)
            for u in range(LATE_T):
                turned_hi(GROUPS, u - LATE_T)
            out_copied(GROUPS)
            hi_of(y2t_hi[:, :, :], M_ALL - 2)

            def split_fc(load, slot, arrivals):
                act.wait_ge(fc_in[slot], arrivals * 16)
                for p in range(PAIRS):
                    cols = slice(p * 2 * P, (p + 1) * 2 * P)
                    A(fc_hi[:, :, cols], raw_fc[:, slot, :, cols], ACT.Copy).then_inc(fc_his, 1)

            def split_pj(p, slot, arrivals):
                act.wait_ge(pj_in[slot], arrivals * 32)
                A(pj_hi[:, 2 * p:2 * p + 2, :], raw_pj[:, slot, 2 * p:2 * p + 2, :], ACT.Copy).then_inc(pj_his, 1)

            def split_x(n):
                act.wait_ge(xt_full, n + 1)
                A(xt_hi[:, :, :], t_bank[0][:, :].rearrange("p (k n) -> p k n", k=KC), ACT.Copy).then_inc(xt_his, 1)

            def block_of(n, par, pj, next_x, next_fc):
                act.wait_ge(b1_set, n + 1)
                for p in range(PAIRS):
                    act.wait_ge(h_full, n * PAIRS + p + 1)
                    act.wait_ge(h_ready, n * PAIRS + p + 1)
                    for c in (0, 1):
                        last = A(h_f[:, p, c, :], s_bank[p][:, c * BN:(c + 1) * BN], ACT.Gelu_apprx_tanh,
                                 bias=b1_now[:, par, 2 * p + c:2 * p + c + 1])
                    last.then_inc(h_act, 1)
                    if pj:
                        act.wait_ge(y_full, n * BT + 1)
                        split_pj(p, *pj)
                if next_x:
                    split_x(n + 1)
                if next_fc:
                    split_fc(None, *next_fc)

            attention_over(act)
            split_x(0)
            split_fc(0, 0, 1)
            block_of(0, 0, (0, 1), True, None)
            block_of(1, 1, None, True, None)
            with act.Fori(1, SHARED // 2 - 1) as i:
                block_of(i * 2, 0, None, True, None)
                block_of(i * 2 + 1, 1, None, True, None)
            block_of(SHARED - 2, 0, None, True, None)
            block_of(SHARED - 1, 1, None, True, (1, 1))

            with act.Fori(0, (BLOCKS - 1) // 2) as i:
                block_of(i * 2 + SHARED, 0, (1, i + 1), True, (0, i + 2))
                block_of(i * 2 + 1 + SHARED, 1, (0, i + 2), True, (1, i + 2))
            block_of(NBLOCKS - 1, 0, (1, (BLOCKS + 1) // 2), False, None)

        @block.vector
        def _(dve):
            V = nc.vector
            count = [0, 0]

            def link(ins):
                count[1] += 1
                ins.then_inc(dv, 1)
                dve.wait_ge(dv, count[0] + count[1])

            def norm_stats(tile):
                V.memset(wait_taker[:, :], 0.0)
                for j in range(GT):
                    last = V.bn_stats(stats[:, j, :], tile(j))
                link(last)
                V.memset(wait_taker[:, :], 0.0)
                for j in range(GT):
                    last = V.bn_aggr(mv[:, j, :], stats[:, j, :])
                link(last)
                V.tensor_scalar(veps[:, :], mv[:, :, 1], EPS, None, ALU.add).then_inc(veps_ready, 1)

            def norm(tile, n, out, ready):
                dve.wait_ge(rstd_ready, n)
                for j in range(GT):
                    last = V.tensor_scalar(out[:, j, :], tile(j), mv[:, j, 0:1], rstd[:, j:j + 1],
                                           ALU.subtract, ALU.mult)
                last.then_inc(ready, 1)

            def lo_of(out, hi, n):
                dve.wait_ge(m_hi, n)
                V.tensor_tensor(out, misc_bank[:, :], hi.bitcast(FP32), ALU.subtract).then_inc(m_free, 1)

            def q_lo_of(n):
                dve.wait_ge(m_hi, n)
                for hf in range(HALVES):
                    last = V.scalar_tensor_tensor(q_lo[:, hf, :], misc_bank[:, hf * GN:(hf + 1) * GN], bq_neg[:, hf:hf + 1],
                                                  q_hi[:, hf, :].bitcast(FP32), ALU.add, ALU.subtract)
                last.then_inc(m_free, 1)

            def kb_high(b, hf):
                V.tensor_tensor(kb_hi[:, b, hf, :].rearrange("p (h k) -> p h k", k=KV),
                                k_hi[:, hf, b:b + 1, :].bitcast(FP32).to_broadcast([P, HH, KV]),
                                head_rows[:, :].unsqueeze(2).to_broadcast([P, HH, KV]), ALU.mult).then_inc(kb_ready[b], 1)

            def maxima(g, par, u):
                n, i, hf, j = unit(u)
                h0, nh = HEADS[i]
                dve.wait_ge(s_full, g * UNITS + u + 1)
                V.tensor_reduce(negmax[:, par, j, hf, h0:h0 + nh], s_bank[u % 4][:, 0:nh * KV].rearrange("p (h k) -> p h k", k=KV),
                                axis=AX.X, op=ALU.min).then_inc(s_max, 1)

            def turned_lo(g, v):
                n, i, hf, j = unit(v)
                c0, m = CHUNKS[i]
                dve.wait_ge(t_hi, g * UNITS + v + 1)
                for r, a, z in rows(c0, m):
                    cols = slice(j * P, (j + 1) * P)
                    last = V.tensor_tensor(pt_lo[0:r, hf, a:z, cols],
                                           t_bank[v % 2][0:r, (a - c0) * P:(z - c0) * P].rearrange("p (c q) -> p c q", q=P),
                                           pt_hi[0:r, hf, a:z, cols].bitcast(FP32), ALU.subtract)
                last.then_inc(t_free, 1)

            rden_all = rden[:, :, :, :].rearrange("p t a h -> p t (a h)")

            def denominators(par):
                link(V.tensor_scalar(some[:, :], negmax[:, par, :, 0, 0], MASKED / 10, None, ALU.is_lt))
                keep = some[:, :].unsqueeze(2).to_broadcast([P, GT, H])
                link(V.tensor_tensor(rden_all, psums[:, par].rearrange("p t a h -> p t (a h)"), keep, ALU.mult))
                link(V.reciprocal(rden_all, rden_all))
                link(V.tensor_tensor(rden_all, rden_all, keep, ALU.mult))

            def group_out(g, use):
                dve.wait_ge(m_full, use + 1)
                V.tensor_tensor(att[:, :, :].rearrange("p t (h d) -> p t h d", d=HD),
                                misc_bank[:, :].rearrange("p (t h d) -> p t h d", t=GT, d=HD),
                                rden_all.unsqueeze(3).to_broadcast([P, GT, H, HD]), ALU.mult).then_inc(m_free, 1)
                dve.wait_ge(m_free, use + 2)
                xg = X[:, bass.ds(g * GT, GT), :]
                link(V.scalar_tensor_tensor(xg, att[:, :, :], tg_x[:, 0:1], xg, ALU.mult, ALU.add))

            def tiles_of(g):
                return lambda j: X[:, bass.ds(g * GT + j, 1), :]

            def second_norm(g, power):
                dve.wait_ge(rows_stored, g * 16 + 16)
                norm(tiles_of(g), power, y2, y2_ready)

            def body(g, par, before, more):
                base, hi = m_base(g, before), hi_base(g, before)
                for u in range(UNITS):
                    maxima(g, par, u)
                    if u == 0 and before == 2:
                        second_norm(g - 2, g * 2)
                    if u == 2 and before == 2:
                        lo_of(y2t_lo[:, :, :], y2t_hi[:, :, :], hi + 1)
                        hi += 1
                    if u == 4 and before == 2:
                        logits_of(g - 2, base + 1)
                        base += 2
                    if u == 3 and more:
                        norm_stats(tiles_of(g + 1))
                    if u == 5 and more:
                        norm(tiles_of(g + 1), g * 2 + 1 if before else 2, y1, y1_ready)
                    if u == 6 and before:
                        denominators(1 - par)
                    if u == 8 and more:
                        lo_of(y1t_lo[:, :, :], y1t_hi[:, :, :], hi + 1)
                        base += 1
                        hi += 1
                    if u == 10 and before:
                        group_out(g - 1, base)
                    if u == 11 and more:
                        q_lo_of(hi + 1)
                    if u in (6, 9) and not before:
                        kb_high(1, (u - 6) // 3)
                    if u >= LATE_LO or before:
                        turned_lo(g, u - LATE_LO)
                    if u == 11 and before:
                        norm_stats(tiles_of(g - 1))

            def logits_of(g, use):
                dve.wait_ge(m_full, use + 1)
                sums = misc_bank[:, 0:GT * 2 * NE].rearrange("p (t a e) -> p t e a", t=GT, a=2)
                V.tensor_reduce(logits[:, bass.ds(g * GT, GT), :], sums, axis=AX.X, op=ALU.add).then_inc(m_free, 1)

            dve.wait_ge(ld_x, 16)
            norm_stats(lambda j: X[:, j, :])
            dve.wait_ge(consts, 2)
            V.tensor_copy(ident_r[:, :], ident[:, :])
            dve.wait_ge(ld_small, 16 * 6)
            V.tensor_scalar(bq_neg[:, :], bq_col[:, :], SQ, None, ALU.mult)
            norm(lambda j: X[:, j, :], 1, y1, y1_ready)
            dve.wait_ge(prep_full, 1)
            link(V.tensor_scalar(wq_hi[:, :, :], s_bank[0][:, :], SQ, None, ALU.mult))
            V.scalar_tensor_tensor(wq_lo[:, :, :], s_bank[0][:, :], SQ, wq_hi[:, :, :].bitcast(FP32), ALU.mult, ALU.subtract).then_inc(wq_ready, 1)
            dve.wait_ge(prep_full, 5)
            V.tensor_copy(ctx_t[:, 1], t_bank[0][:, 0:B * KV]).then_inc(ctx_ready, 1)
            for hf, bank in enumerate((t_bank[1], pv_bank)):
                dve.wait_ge(prep_full, 6 + hf)
                last = V.tensor_scalar(k_t[:, hf], bank[:, 0:B * KV].rearrange("p (b k) -> p b k", b=B), bk_col[:, hf:hf + 1], None, ALU.add)
            last.then_inc(k_ready, 1)
            lo_of(y1t_lo[:, :, :], y1t_hi[:, :, :], 1)
            dve.wait_ge(k_hi_ready, 1)
            V.tensor_tensor(k_lo[:, :, :, :], k_t[:, :, :, :], k_hi[:, :, :, :].bitcast(FP32), ALU.subtract).then_inc(k_ready, 1)
            dve.wait_ge(consts, 3)
            kb_high(0, 0)
            q_lo_of(2)
            kb_high(0, 1)
            dve.wait_ge(ld_m, 16)
            V.tensor_scalar(mask_big[:, :, :], mask_i[:, :, :], 1.0, MASKED, ALU.is_equal, ALU.mult).then_inc(mask_ready, 1)
            for i, (f, bank, r) in enumerate(((v_f, t_bank[0], P), (vr_f, t_bank[1], KVR))):
                dve.wait_ge(prep_full, 8 + i)
                for b in range(B):
                    last = V.tensor_tensor(f[:, b], bank[0:r, b * D:(b + 1) * D], bv_row[0:r, :], ALU.add)
                if i == 0:
                    last.then_inc(v_added, 1)
            last.then_inc(v_added, 1)
            link(V.tensor_copy(wr_parts[:, :, 0, :], wr_raw[:, :, :]))
            V.tensor_tensor(wr_parts[:, :, 1, :], wr_raw[:, :, :], wr_parts[:, :, 0, :].bitcast(FP32), ALU.subtract)
            for i, (f, h, l) in enumerate(((v_f, v_hi, v_lo), (vr_f, vr_hi, vr_lo))):
                dve.wait_ge(v_hi_ready, i + 1)
                V.tensor_tensor(l[:, :, :], f[:, :, :], h[:, :, :].bitcast(FP32), ALU.subtract).then_inc(v_ready, 1)
            dve.wait_ge(ld_x_rest, 16 * (GROUPS - 1))
            dve.wait_ge(tanh_ready, 1)
            NORM, LINKS = 2, 9
            ahead = count[1]
            body(0, 0, 0, True)
            assert count[1] == ahead + NORM, count

            def at(g):
                count[0], count[1] = g * LINKS + (ahead + NORM - LINKS), 0

            body(1, 1, 1, True)
            with dve.Fori(1, GROUPS // 2 - 1) as i:
                for par in range(2):
                    at(i * 2 + par)
                    body(i * 2 + par, par, 2, True)
                    assert count[1] == LINKS, count
            at(GROUPS - 2)
            body(GROUPS - 2, 0, 2, True)
            body(GROUPS - 1, 1, 2, False)
            second_norm(GROUPS - 2, 2 * GROUPS - 1)
            for u in range(LATE_LO):
                turned_lo(GROUPS, u - LATE_LO)
            lo_of(y2t_lo[:, :, :], y2t_hi[:, :, :], 3 * GROUPS - 1)
            denominators(1)
            logits_of(GROUPS - 2, M_ALL - 4)
            group_out(GROUPS - 1, M_ALL - 3)
            norm_stats(tiles_of(GROUPS - 1))
            second_norm(GROUPS - 1, 2 * GROUPS)
            lo_of(y2t_lo[:, :, :], y2t_hi[:, :, :], 3 * GROUPS)
            logits_of(GROUPS - 1, M_ALL - 1)

            dve.wait_ge(c_pool, 12)
            attention_over(dve)
            for t in range(TILES):
                last = V.max(top[:, t, :], logits[:, t, :])
            link(last)
            for t in range(TILES):
                last = V.max_index(top_i[:, t, :], top[:, t, :], logits[:, t, :])
            V.tensor_tensor(gap[:, :], top[:, :, 1], top[:, :, 0], ALU.subtract).then_inc(gap_ready, 1)
            link(V.memset(cum[:, 0, :], 0.0))
            link(V.tensor_copy(top_f[:, :, :], top_i[:, :, 0:TOPK].rearrange("p t k -> p k t")))
            for k in range(TOPK):
                last = V.tensor_tensor(chosen[:, k], top_f[:, k, :].unsqueeze(2).to_broadcast([P, TILES, NE]),
                                       iota_e[:, :].unsqueeze(1).to_broadcast([P, TILES, NE]), ALU.is_equal)
            link(last)
            V.tensor_tensor(both[:, :, :], chosen[:, 0], chosen[:, 1], ALU.add).then_inc(counts_in, 1)
            dve.wait_ge(ld_b1, 64)
            dve.wait_ge(b1_full, 1)
            V.tensor_copy(b1_t[:, :], t_bank[1][:, 2 * P:2 * P + (NE + 1) * HC])
            dve.wait_ge(counts_full, 1)
            V.tensor_copy(in_tile[:, :, :], t_bank[1][:, 0:P])
            link(V.tensor_copy(totals[:, :, :], t_bank[1][:, P:2 * P]))
            for t in range(TILES):
                link(V.tensor_tensor(cum[:, t + 1, :], cum[:, t, :], totals[:, t, :], ALU.add))
            link(V.tensor_scalar(thresholds[:, :], iota_e[:, :], float(BN), None, ALU.mult))
            link(V.tensor_tensor(over[:, :, :], cum[:, TILES, :].unsqueeze(2).to_broadcast([P, NE, NE]),
                                 thresholds[:, :].unsqueeze(1).to_broadcast([P, NE, NE]), ALU.is_gt))
            link(V.tensor_reduce(blocks_of[:, :], over[:, :, :], axis=AX.X, op=ALU.add))
            link(V.tensor_tensor(over[:, :, :], before_e[:, :, :], blocks_of[:, :].unsqueeze(1).to_broadcast([P, NE, NE]), ALU.mult))
            link(V.tensor_reduce(start[:, :], over[:, :, :], axis=AX.X, op=ALU.add))
            link(V.tensor_tensor(end[:, :], start[:, :], blocks_of[:, :], ALU.add))
            link(V.tensor_tensor(passed[:, :, :], end[:, :].unsqueeze(1).to_broadcast([P, BLOCKS, NE]),
                                 iota_b[:, :].unsqueeze(2).to_broadcast([P, BLOCKS, NE]), ALU.is_le))
            link(V.tensor_reduce(block_f[:, :], passed[:, :, :], axis=AX.X, op=ALU.add))
            V.tensor_scalar(block_e[:, :], block_f[:, :], float(NE - 1), None, ALU.min).then_inc(blocks_ready, 1)
            link(V.tensor_scalar(start[:, :], start[:, :], float(BN), None, ALU.mult))
            link(V.tensor_tensor(slot[:, :, :], cum[:, 0:TILES, :], in_tile[:, :, :], ALU.add))
            link(V.tensor_tensor(slot[:, :, :], slot[:, :, :], start[:, :].unsqueeze(1).to_broadcast([P, TILES, NE]), ALU.add))
            for k in range(TOPK):
                last = V.tensor_tensor(work[:, k], chosen[:, k], slot[:, :, :], ALU.mult)
            link(last)
            for k in range(TOPK):
                V.tensor_reduce(pos_f[:, k, :], work[:, k], axis=AX.X, op=ALU.add)
                last = V.tensor_reduce(none_f[:, k, :], chosen[:, k], axis=AX.X, op=ALU.add)
            link(last)
            link(V.tensor_scalar(none_f[:, :, :], none_f[:, :, :], -float(ROWS), float(ROWS), ALU.mult, ALU.add))
            V.tensor_tensor(pos[:, :, :], pos_f[:, :, :], none_f[:, :, :], ALU.add).then_inc(pos_ready, 1)
            dve.wait_ge(e_gap_ready, 1)
            link(V.tensor_scalar(gap[:, :], e_gap[:, :], 1.0, None, ALU.add))
            link(V.reciprocal(gap[:, :], gap[:, :]))
            dve.wait_ge(tanh_ready, 2)
            link(V.tensor_scalar(gates[:, 0, :], gap[:, :], tg_f[:, 0:1], None, ALU.mult))
            V.tensor_tensor(gates[:, 1, :], gates[:, 0, :], e_gap[:, :], ALU.mult)

            def set_b1(n, par, e):
                V.tensor_scalar(b1_now[:, par, :], b1_t[:, bass.ds(e * HC, HC)], 1.0, None, ALU.mult).then_inc(b1_set, 1)

            def split_fc(load, slot):
                for p in range(PAIRS):
                    cols = slice(p * 2 * P, (p + 1) * 2 * P)
                    dve.wait_ge(fc_his, load * PAIRS + p + 1)
                    V.tensor_tensor(fc_lo[:, :, cols], raw_fc[:, slot, :, cols], fc_hi[:, :, cols].bitcast(FP32), ALU.subtract)\
                     .then_inc(fc_ready, 1)

            def split_pj(p, load, slot):
                dve.wait_ge(pj_his, load * PAIRS + p + 1)
                rows_ = slice(2 * p, 2 * p + 2)
                V.tensor_tensor(pj_lo[:, rows_, :], raw_pj[:, slot, rows_, :], pj_hi[:, rows_, :].bitcast(FP32), ALU.subtract)\
                 .then_inc(pj_ready, 1)

            def split_x(n):
                dve.wait_ge(xt_his, n + 1)
                V.tensor_tensor(xt_lo[:, :, :], t_bank[0][:, :].rearrange("p (k n) -> p k n", k=KC), xt_hi[:, :, :].bitcast(FP32),
                                ALU.subtract).then_inc(xt_ready, 1)

            def block_of(n, par, pj, next_x, next_fc, next_e, e, shared, stored=None):
                for p in range(PAIRS):
                    pair = slice(2 * p, 2 * p + 2)
                    dve.wait_ge(h_act, n * PAIRS + p + 1 + H0)
                    if p == 0:
                        dve.wait_ge(y_full, n * BT + 1)
                    link(V.tensor_copy(ht_hi[:, pair, :], h_f[:, p]))
                    V.tensor_tensor(ht_lo[:, pair, :], h_f[:, p], ht_hi[:, pair, :].bitcast(FP32), ALU.subtract).then_inc(h_ready, 1)
                    if pj:
                        split_pj(p, *pj)
                if next_x:
                    split_x(n + 1)
                    set_b1(n + 1, 1 - par, next_e())
                if next_fc:
                    split_fc(*next_fc)
                if not shared:
                    dve.wait_ge(z_out[par], stored * 16 + 16)
                for i in range(BT):
                    dve.wait_ge(y_full, n * BT + i + 2)
                    ins = V.tensor_tensor(y_sb[:, par, i, :], m_bank[i][:, 0:D], b2_all[:, bass.ds(e, 1), :], ALU.add)
                    if i == 1 and shared:
                        pass
                    ins.then_inc(y_evac, 1)
                if shared:
                    dve.wait_ge(y_evac, n * BT + BT + BT)
                    xs = X[:, bass.ds(n * BT, BT), :]
                    V.scalar_tensor_tensor(xs, y_sb[:, par], tg_f[:, 0:1], xs, ALU.mult, ALU.add)

            def expert(t):
                return dve.value_load(block_e[0:1, bass.ds(t, 1)], min_val=0, max_val=NE - 1)

            def same():
                return NE

            split_x(0)
            link(V.memset(wait_taker[:, :], 0.0))
            set_b1(0, 0, NE)
            split_fc(0, 0)
            EXP_LINKS = PAIRS
            base = count[0] + count[1]

            def at(n):
                count[0], count[1] = n * EXP_LINKS + base, 0

            at(0)
            block_of(0, 0, (0, 0), True, None, same, NE, True)
            at(1)
            block_of(1, 1, None, True, None, same, NE, True)
            with dve.Fori(1, SHARED // 2 - 1) as i:
                at(i * 2)
                block_of(i * 2, 0, None, True, None, same, NE, True)
                at(i * 2 + 1)
                block_of(i * 2 + 1, 1, None, True, None, same, NE, True)
            at(SHARED - 2)
            block_of(SHARED - 2, 0, None, True, None, same, NE, True)
            dve.wait_ge(blocks_ready, 1)
            at(SHARED - 1)
            block_of(SHARED - 1, 1, None, True, (1, 1), lambda: expert(0), NE, True)
            with dve.Fori(0, (BLOCKS - 1) // 2) as i:
                at(i * 2 + SHARED)
                block_of(i * 2 + SHARED, 0, (i * 2 + 1, 1), True, (i * 2 + 2, 0), lambda: expert(i * 2 + 1), expert(i * 2), False, i)
                at(i * 2 + SHARED + 1)
                block_of(i * 2 + SHARED + 1, 1, (i * 2 + 2, 0), True, (i * 2 + 3, 1), lambda: expert(i * 2 + 2), expert(i * 2 + 1), False, i)
            at(NBLOCKS - 1)
            block_of(NBLOCKS - 1, 0, (BLOCKS, 1), False, None, None, expert(BLOCKS - 1), False, BLOCKS // 2)
            at(NBLOCKS)
            dve.wait_ge(gathered, 16 * TOPK * TILES)
            for q in range(GROUPS):
                for k in range(TOPK):
                    for t in range(q * GT, (q + 1) * GT):
                        last = V.scalar_tensor_tensor(X[:, t, :], zg[:, k, t, :], gates[:, k, t:t + 1], X[:, t, :], ALU.mult, ALU.add)
                    if k == 0:
                        link(last)
                last.then_inc(combined, 1)

    return nc


_INS = ['x', 'ctx_1024', 'mask_BxSxS2_ik1', 'g_xattn', 'g_ffn', 'L0_xattn_Wq', 'L0_xattn_bq', 'L0_xattn_Wk', 'L0_xattn_bk',
        'L0_xattn_Wv', 'L0_xattn_bv', 'L0_ffn_Wfc_s', 'L0_ffn_bfc_s', 'L0_ffn_Wproj_s', 'L0_ffn_bproj_s', 'L0_ffn_Wr',
        'L0_ffn_Wfc', 'L0_ffn_bfc', 'L0_ffn_Wproj', 'L0_ffn_bproj']
_OUTS = [((B, T, D), 'float32')]


def kernel(**inputs):
    import numpy as _np
    import concourse.bacc as _bacc
    from concourse import mybir as _mybir
    from concourse.bass_utils import run_bass_kernel_spmd as _run

    nc = _bacc.Bacc("TRN2", target_bir_lowering=False, num_devices=1)
    arrays, args = {}, []
    for name in _INS:
        a = _np.ascontiguousarray(inputs[name])
        arrays[f"in_{name}_dram"] = a
        args.append(nc.dram_tensor(f"in_{name}_dram", a.shape, _mybir.dt.from_np(a.dtype), kind="ExternalInput").ap())
    for i, (shape, dtype) in enumerate(_OUTS):
        dt = _mybir.dt.from_np(_np.dtype(dtype))
        args.append(nc.dram_tensor(f"out_{i}_dram", shape, dt, kind="ExternalOutput").ap())
    build(nc, *args)
    r = _run(nc, [arrays], core_ids=[0])
    return r.results[0]["out_0_dram"]
```

```python
from contextlib import ExitStack

import concourse.bass as bass
from concourse import mybir

FP32 = mybir.dt.float32
FP32R = mybir.dt.float32r
INT32 = mybir.dt.int32
ALU = mybir.AluOpType
ACT = mybir.ActivationFunctionType
AX = mybir.AxisListType

P = 128
B, T, D = 2, 1024, 256
KV = 154
H, HD = 16, 16
NE = 8
TILES = B * T // P
GT = 2
GROUPS = TILES // GT
GN = GT * P
KC = D // P
HALVES = H * HD // P
HH = H // HALVES
HW = HH * KV
HEADS = [(0, 3), (3, 3), (6, 2)]
NCH = -(-HW // P)
CHROWS = [min(P, HW - P * c) for c in range(NCH)]
CHUNKS = [(0, 4), (4, 4), (8, 2)]
STEPS = HALVES * GT
NB = len(HEADS)
UNITS = STEPS * NB
BG = T // GN
LATE_T = 3
LATE_LO = 4
PV_FIRST = {0: (4, 7), 2: (7, 10)}
PV_SECOND = {6: (0, 4), 7: (4, 7), 8: (7, 10)}
Q_UNIT = UNITS - 1
FC_UNITS = (2, 3, 4, 5)
S_BANKS, T_BANKS = 3, 3
KVR = KV - P
MASKED = 1e30
HID = 4 * D
HC = HID // P
PAIRS = HC // 2
TOPK = 2
BT = 2
BN = BT * P
SHARED = TILES // BT
FIRST = 5
BLOCKS = TILES * TOPK // BT + NE - 1
ROWS = BLOCKS * BN
NBLOCKS = SHARED + BLOCKS
LOADS = BLOCKS + 2
ODD = FIRST % 2
OUT_PARTS = [(0, 5), (5, 10), (10, 13), (13, 15), (15, 16)]
EPS = 1e-5
SQ = -1.0 / 16.0


def build(nc, x, ctx_kv, mask, g_xattn, g_ffn, wq, bq, wk, bk, wv, bv,
          wfc_s, bfc_s, wproj_s, bproj_s, wr, wfc, bfc, wproj, bproj, out):
    ctx = ExitStack()
    with ctx:
        def sb(name, shape, dt=FP32):
            return ctx.enter_context(nc.sbuf_tensor(name, shape, dt))

        def ps(name):
            return ctx.enter_context(nc.psum_tensor(name, [P, 512], FP32))

        def sem(name):
            return ctx.enter_context(nc.semaphore(name))

        x_rows = nc.dram_tensor("x_rows", [TILES * P, D], FP32, kind="Internal").ap()
        x_sorted = nc.dram_tensor("x_sorted", [ROWS, D], FP32, kind="Internal").ap()
        z_rows = nc.dram_tensor("z_rows", [ROWS, D], FP32, kind="Internal").ap()
        vx = [nc.dram_tensor(f"v_blocks_{n}", [B, HALVES, NCH * P, P], FP32, kind="Internal").ap() for n in ("hi", "lo")]

        X = sb("X", [P, TILES, D])
        bq_col = sb("bq_col", [P, HALVES])
        bk_col = sb("bk_col", [P, HALVES])
        gate_x = sb("gate_x", [P, 1])
        tg_x = sb("tg_x", [P, 1])
        wr_raw = sb("wr_raw", [P, KC, NE])
        bq_neg = sb("bq_neg", [P, HALVES])
        wr_parts = sb("wr_parts", [P, KC, 2, NE], FP32R)
        ident = sb("ident", [P, P])
        ident_r = sb("ident_r", [P, P], FP32R)
        zeros = sb("zeros", [P, D])
        head_rows = sb("head_rows", [P, HH])
        neg_half = sb("neg_half", [P, GT])
        negmax = sb("negmax", [P, 2, GT, HALVES, HH])
        psums = sb("psums", [P, 2, GT, HALVES, HH])
        wait_taker = sb("wait_taker", [P, 1])
        stats = sb("stats", [P, GT, 6])
        mv = sb("mv", [P, GT, 2])
        veps = sb("veps", [P, GT])
        rstd = sb("rstd", [P, GT])
        logits = sb("logits", [P, TILES, NE])
        gate_f = sb("gate_f", [P, 1])
        tg_f = sb("tg_f", [P, 1])
        e_const = sb("e_const", [P, TILES])
        iota_e = sb("iota_e", [P, NE])
        iota_b = sb("iota_b", [P, BLOCKS])
        before_e = sb("before_e", [P, NE, NE])
        ones = sb("ones", [P, P])
        before_p = sb("before_p", [P, P])
        b1_rows = sb("b1_rows", [(NE + 1) * HC, P])
        b1_t = sb("b1_t", [P, (NE + 1) * HC])
        b2_all = sb("b2_all", [P, NE + 1, D])
        pos = sb("pos", [P, TOPK, TILES], mybir.dt.uint32)
        gates = sb("gates", [P, TOPK, TILES])
        block_e = sb("block_e", [P, BLOCKS], INT32)

        raw_fc, raw_pj = [sb("raw_fc_0", [P, KC, HID])], [sb("raw_pj_0", [P, HC, D])]
        y1 = xr = sb("rows", [P, BT, D])
        y1t_hi = xt_hi = sb("rows_turned_hi", [P, KC, BN], FP32R)
        y1t_lo = xt_lo = sb("rows_turned_lo", [P, KC, BN], FP32R)
        b1_now = sb("b1_now", [P, 2, HC])

        attention = ExitStack()

        def att_sb(name, shape, dt=FP32):
            return attention.enter_context(nc.sbuf_tensor(name, shape, dt))

        kb = att_sb("kb", [P, B, 2, HALVES, HW], FP32R)
        mask_big = att_sb("mask_big", [P, TILES, KV], FP32R)
        vs = [att_sb(f"vs_{n}", [P, HALVES, NCH, P], FP32R) for n in ("hi", "lo")]
        q_hi = att_sb("q_hi", [P, 2, HALVES, GN], FP32R)
        q_lo = att_sb("q_lo", [P, 2, HALVES, GN], FP32R)
        prob = att_sb("prob", [P, STEPS, HW])
        wq_hi = att_sb("wq_hi", [P, KC, D], FP32R)
        wq_lo = att_sb("wq_lo", [P, KC, D], FP32R)
        k_hi = att_sb("k_hi", [P, HALVES, B, KV], FP32R)
        k_lo = att_sb("k_lo", [P, HALVES, B, KV], FP32R)

        early = ExitStack()

        def tmp(name, shape, dt=FP32):
            return early.enter_context(nc.sbuf_tensor(name, shape, dt))

        v_hi = tmp("v_hi", [P, B, D], FP32R)
        v_lo = tmp("v_lo", [P, B, D], FP32R)
        vr_hi = tmp("vr_hi", [KVR, B, D], FP32R)
        vr_lo = tmp("vr_lo", [KVR, B, D], FP32R)
        v_f = tmp("v_f", [P, B, D])
        vr_f = tmp("vr_f", [KVR, B, D])
        bv_row = tmp("bv_row", [P, D])
        w3 = tmp("w3", [P, 3, KC, D])
        ctx_a = tmp("ctx_a", [P, B, D])
        ctx_b = tmp("ctx_b", [KVR, B, D])
        mask_i = tmp("mask_i", [P, TILES, KV], INT32)
        wk_t = tmp("wk_t", [P, KC, D])
        wv_t = tmp("wv_t", [P, KC, D])
        ctx_t = tmp("ctx_t", [P, KC, B, KV])
        k_t = tmp("k_t", [P, HALVES, B, KV])
        early.close()
        y2 = att_sb("y2", [P, GT, D])
        y2t_hi = att_sb("y2t_hi", [P, KC, GN], FP32R)
        y2t_lo = att_sb("y2t_lo", [P, KC, GN], FP32R)
        ot = att_sb("ot", [P, HALVES, GN])
        rden = att_sb("rden", [P, GT, HALVES, HH])
        some = att_sb("some", [P, GT])
        att = att_sb("att", [P, GT, D])
        pt_hi = att_sb("pt_hi", [P, HALVES, NCH, GN], FP32R)
        pt_lo = att_sb("pt_lo", [P, HALVES, NCH, GN], FP32R)
        attention.close()

        fc_hi = sb("fc_hi", [P, KC, HID], FP32R)
        fc_lo = sb("fc_lo", [P, KC, HID], FP32R)
        top = sb("top", [P, TILES, NE])
        top_i = sb("top_i", [P, TILES, NE], mybir.dt.uint32)
        top_f = sb("top_f", [P, TOPK, TILES])
        chosen = sb("chosen", [P, TOPK, TILES, NE])
        pj_hi, pj_lo = [sb("pj_hi_0", [P, HC, D], FP32R)], [sb("pj_lo_0", [P, HC, D], FP32R)]
        raw_fc.append(sb("raw_fc_1", [P, KC, HID]))
        raw_pj.append(sb("raw_pj_1", [P, HC, D]))
        h_f = sb("h_f", [P, PAIRS, 2, BN])
        ht_hi = sb("ht_hi", [P, HC, BN], FP32R)
        ht_lo = sb("ht_lo", [P, HC, BN], FP32R)
        both = sb("both", [P, TILES, NE])
        cum = [sb(f"cum_{i}", [P, TILES + 1, NE]) for i in range(2)]
        slot = sb("slot", [P, TILES, NE])
        work = sb("work", [P, TOPK, TILES, NE])
        over = sb("over", [P, NE, NE])
        thresholds = sb("thresholds", [P, NE])
        blocks_of = sb("blocks_of", [P, NE])
        start = sb("start", [P, NE])
        end = sb("end", [P, NE])
        passed = sb("passed", [P, BLOCKS, NE])
        block_f = sb("block_f", [P, BLOCKS])
        gap = sb("gap", [P, TILES])
        e_gap = sb("e_gap", [P, TILES])
        pos_f = sb("pos_f", [P, TOPK, TILES])
        none_f = sb("none_f", [P, TOPK, TILES])
        y_sb = sb("y_sb", [P, 2, BT, D])
        b2_now = sb("b2_now", [P, 2, D])
        pj_hi.append(sb("pj_hi_1", [P, HC, D], FP32R))
        pj_lo.append(sb("pj_lo_1", [P, HC, D], FP32R))
        z_second = sb("z_second", [P, TILES, D])
        y2_all = sb("y2_all", [P, TILES, D])
        zg = [y2_all, z_second]

        s_bank = [ps(f"scores_{i}") for i in range(S_BANKS)]
        t_bank = [ps(f"turned_{i}") for i in range(T_BANKS)]
        pv_bank, misc_bank = ps("products_pv"), ps("misc")

        ld_w = sem("ld_w")
        ld_c = sem("ld_c")
        ld_x = sem("ld_x")
        ld_m = sem("ld_m")
        ld_small = sem("ld_small")
        ld_v = [sem("ld_v_0"), sem("ld_v_1")]
        ld_x_next = sem("ld_x_next")
        ld_x_rest = sem("ld_x_rest")
        y2_in = sem("y2_in")
        vx_zero = [sem("vx_zero_0"), sem("vx_zero_1")]
        vx_in = [sem("vx_in_0"), sem("vx_in_1")]
        VX_WRITES = 16 * 4 * HALVES
        consts = sem("consts")
        c_pool = sem("c_pool")
        prep_full = sem("prep_full")
        wq_ready = sem("wq_ready")
        wkv_ready = sem("wkv_ready")
        ctx_ready = sem("ctx_ready")
        k_ready = sem("k_ready")
        k_hi_ready = sem("k_hi_ready")
        v_added = sem("v_added")
        v_hi_ready = sem("v_hi_ready")
        v_ready = sem("v_ready")
        mask_ready = sem("mask_ready")
        kb_ready = [[sem(f"kb_ready_{b}{hf}") for hf in range(HALVES)] for b in range(B)]
        tanh_ready = sem("tanh_ready")
        veps_ready = sem("veps_ready")
        rstd_ready = sem("rstd_ready")
        y1_ready = sem("y1_ready")
        y2_ready = sem("y2_ready")
        s_full = sem("s_full")
        s_max = sem("s_max")
        s_free = sem("s_free")
        t_full = sem("t_full")
        t_hi = sem("t_hi")
        t_free = sem("t_free")
        pv_done = sem("pv_done")
        m_full = sem("m_full")
        m_hi = sem("m_hi")
        q_his = sem("q_his")
        q_first = sem("q_first")
        m_free = sem("m_free")
        ot_done = sem("ot_done")
        dv = sem("dv")
        x_zero = sem("x_zero")
        rows_stored = sem("rows_stored")
        ld_b1 = sem("ld_b1")
        ld_b2 = sem("ld_b2")
        counts_in = sem("counts_in")
        counts_full = sem("counts_full")
        b1_full = sem("b1_full")
        gap_ready = sem("gap_ready")
        e_gap_ready = sem("e_gap_ready")
        blocks_ready = sem("blocks_ready")
        pos_ready = sem("pos_ready")
        scattered = sem("scattered")
        gathered = [sem(f"gathered_{j}") for j in range(len(OUT_PARTS))]
        fc_in = [sem("fc_in_0"), sem("fc_in_1")]
        pj_in = [sem("pj_in_0"), sem("pj_in_1")]
        fc_his = sem("fc_his")
        fc_ready = sem("fc_ready")
        pj_his = sem("pj_his")
        pj_ready = sem("pj_ready")
        x_in = sem("x_in")
        xt_full = sem("xt_full")
        xt_his = sem("xt_his")
        xt_ready = sem("xt_ready")
        biases_set = sem("biases_set")
        h_full = sem("h_full")
        h_act = sem("h_act")
        h_ready = sem("h_ready")
        y_full = sem("y_full")
        y_evac = sem("y_evac")
        z_out = [sem("z_out_0"), sem("z_out_1")]
        combined = sem("combined")
        out_done = sem("out_done")

        block = ctx.enter_context(nc.Block())

        x_bank, y_bank, h_bank = t_bank[0], (pv_bank, t_bank[1]), (*s_bank, t_bank[2])
        M_ALL = 5 * GROUPS

        def m_base(g, before):
            return (2, 4, g * 5 - 3)[before]

        def hi_base(g, before):
            return (1, 2, g * 2 - 1)[before]

        def unit(v):
            n, i = divmod(v % UNITS, NB)
            return (n, i) + divmod(n, GT)

        def rows(c0, m):
            if CHROWS[c0 + m - 1] == CHROWS[c0]:
                return [(CHROWS[c0], c0, c0 + m)]
            return [(CHROWS[c0], c0, c0 + m - 1), (CHROWS[c0 + m - 1], c0 + m - 1, c0 + m)]

        H0 = PAIRS

        def biases_of(n):
            return 2 if n < FIRST else min(n - FIRST + 3, BLOCKS + 4)

        @block.sync
        def _(sp):
            with nc.allow_non_contiguous_dma(reason="small columns"):
                for i, w in enumerate((wq, wk, wv)):
                    sp.dma_start(w3[:, i], w.rearrange("(o p) i -> p o i", p=P)).then_inc(ld_w, 16)
                sp.dma_start(ctx_a[:, :, :], ctx_kv[:, 0:P, :].rearrange("b p d -> p b d")).then_inc(ld_c, 16)
                sp.dma_start(ctx_b[:, :, :], ctx_kv[:, P:KV, :].rearrange("b p d -> p b d")).then_inc(ld_c, 16)
                sp.dma_start(X[:, 0:GT], x[0, 0:GN].rearrange("(t p) d -> p t d", p=P)).then_inc(ld_x, 16)
                sp.dma_start(bq_col[:, :], bq.rearrange("(o p) -> p o", p=P)).then_inc(ld_small, 16)
                sp.dma_start(bk_col[:, :], bk.rearrange("(o p) -> p o", p=P)).then_inc(ld_small, 16)
                sp.dma_start(bv_row[:, :], bv.rearrange("(a n) -> a n", a=1).to_broadcast([P, D])).then_inc(ld_small, 16)
                sp.dma_start(gate_x[:, :], g_xattn.rearrange("(a n) -> a n", a=1).to_broadcast([P, 1])).then_inc(ld_small, 16)
                sp.dma_start(wr_raw[:, :, :], wr.rearrange("(k p) e -> p k e", p=P)).then_inc(ld_small, 16)
                sp.dma_start(gate_f[:, :], g_ffn.rearrange("(a n) -> a n", a=1).to_broadcast([P, 1])).then_inc(ld_small, 16)
                sp.dma_start(b1_rows[0:NE * HC, :], bfc.rearrange("e (c p) -> (e c) p", p=P)).then_inc(ld_b1, 16)
                sp.dma_start(b1_rows[NE * HC:(NE + 1) * HC, :], bfc_s.rearrange("(c p) -> c p", p=P)).then_inc(ld_b1, 16)
                sp.dma_start(mask_i[:, :, :], mask.rearrange("b (t p) k -> p (b t) k", p=P)).then_inc(ld_m, 16)

                def zero_v(b):
                    for t in vx:
                        for h in range(HALVES):
                            sp.dma_start(t[b, h].rearrange("(p c a) f -> p c (a f)", p=P, a=D // P),
                                         zeros[:, :].unsqueeze(1).to_broadcast([P, NCH * P // D, D])).then_inc(vx_zero[b], 16)

                def blocks_of_v(b):
                    sp.wait_ge(vx_zero[b], 16 * 2 * HALVES)
                    for t, va, vb in zip(vx, (v_hi, v_lo), (vr_hi, vr_lo)):
                        for hf in range(HALVES):
                            for src, r0, n in ((va, 0, P), (vb, P, KVR)):
                                dst = bass.AP(t.tensor, t[b, hf].offset + r0 * P, [[P, n], [KV * P + HD, HH], [1, HD]])
                                sp.dma_start(dst, src[:, b, hf * P:(hf + 1) * P].rearrange("p (h f) -> p h f", h=HH).bitcast(FP32)).then_inc(vx_in[b], 16)
                    sp.wait_ge(vx_in[b], VX_WRITES)

                sp.wait_ge(consts, 1)
                zero_v(0)
                for g in range(1, GROUPS):
                    b, t0 = g * GN // T, g * GN % T
                    sp.dma_start(X[:, g * GT:(g + 1) * GT],
                                 x[b, t0:t0 + GN].rearrange("(t p) d -> p t d", p=P)).then_inc(ld_x_next if g == 1 else ld_x_rest, 16)
                sp.wait_ge(v_ready, 2)
                blocks_of_v(0)

                def load_v(b, hf):
                    for n in range(2):
                        sp.dma_start(vs[n][:, hf].bitcast(FP32), vx[n][b, hf].rearrange("(c p) f -> p c f", p=P)).then_inc(ld_v[hf], 16)

                def store_y2(g0, g1):
                    with sp.Fori(g0, g1) as g:
                        sp.wait_ge(y2_ready, g + 1)
                        sp.dma_start(x_rows[bass.ds(g * GN, GN), :].rearrange("(t p) d -> p t d", p=P), y2[:, :, :]).then_inc(rows_stored, 16)

                for hf in range(HALVES):
                    load_v(0, hf)
                zero_v(1)
                blocks_of_v(1)
                sp.dma_start(b2_all[:, 0:NE, :], bproj.rearrange("(a e) n -> a e n", a=1).to_broadcast([P, NE, D])).then_inc(ld_b2, 16)
                sp.dma_start(b2_all[:, NE, :], bproj_s.rearrange("(a n) -> a n", a=1).to_broadcast([P, D])).then_inc(ld_b2, 16)
                blank = x_sorted.rearrange("(p r) d -> p r d", p=P)
                for a in range(0, ROWS // P, 8):
                    z = min(a + 8, ROWS // P)
                    sp.dma_start(blank[:, a:z], zeros[:, :].unsqueeze(1).to_broadcast([P, z - a, D])).then_inc(x_zero, 16)
                store_y2(0, BG - 1)
                for hf in range(HALVES):
                    sp.wait_ge(pv_done, (BG - 1) * 2 + hf + 3)
                    load_v(1, hf)

                def load_fc(slot, w):
                    sp.dma_start(raw_fc[slot][:, :, :], w.rearrange("a (k p) n -> p (a k) n", p=P)).then_inc(fc_in[slot], 16)

                def load_pj(slot, w):
                    for half in range(2):
                        sp.dma_start(raw_pj[slot][:, half * HC // 2:(half + 1) * HC // 2],
                                     w[:, half * HID // 2:(half + 1) * HID // 2].rearrange("a (c p) n -> p (a c) n", p=P)).then_inc(pj_in[slot], 16)

                def load_x(rows, r):
                    sp.dma_start(xr[:, :, :], rows[bass.ds(r, BN), :].rearrange("(t p) d -> p t d", p=P)).then_inc(x_in, 16)

                def expert(t):
                    return sp.value_load(block_e[0:1, bass.ds(t, 1)], min_val=0, max_val=NE - 1)

                shared_fc = wfc_s.rearrange("(a k) n -> a k n", a=1)
                shared_pj = wproj_s.rearrange("(a k) n -> a k n", a=1)
                load_fc(0, shared_fc)
                load_pj(0, shared_pj)
                store_y2(BG - 1, GROUPS - 2)
                sp.wait_ge(rows_stored, 16 * (GROUPS - 1))
                load_x(x_rows, 0)
                store_y2(GROUPS - 2, GROUPS - 1)
                sp.wait_ge(xt_full, 1)
                load_x(x_rows, BN)
                store_y2(GROUPS - 1, GROUPS)
                sp.wait_ge(rows_stored, 16 * GROUPS + 16)
                sp.dma_start(y2_all[:, :, :], x_rows.rearrange("(t p) d -> p t d", p=P)).then_inc(y2_in, 16)
                with sp.Fori(2, FIRST) as n:
                    sp.wait_ge(xt_full, n)
                    load_x(x_rows, n * BN)
                sp.wait_ge(blocks_ready, 1)
                e = expert(0)
                load_pj(1, wproj[bass.ds(e, 1)])
                load_fc(1, wfc[bass.ds(e, 1)])
                e = expert(1)
                sp.wait_ge(pj_ready, PAIRS)
                load_pj(0, wproj[bass.ds(e, 1)])
                sp.wait_ge(fc_ready, PAIRS)
                load_fc(0, wfc[bass.ds(e, 1)])
                sp.wait_ge(xt_full, FIRST)
                sp.wait_ge(scattered, 16 * TOPK * TILES)
                load_x(x_sorted, 0)

                def store_z(t, par):
                    par = (par + ODD) % 2
                    sp.wait_ge(y_evac, (t + FIRST + 2) * BT)
                    sp.dma_start(z_rows[bass.ds(t * BN, BN), :].rearrange("(t p) d -> p t d", p=P), y_sb[:, par]).then_inc(z_out[par], 16)

                def body(t, par, store=True, weights=None):
                    sp.wait_ge(xt_full, t + FIRST + 1)
                    load_x(x_sorted, (t + 1) * BN)
                    pj, fc = weights() if weights else (shared_pj, shared_fc)
                    sp.wait_ge(pj_ready, (t + 2) * PAIRS)
                    load_pj(1 - par, pj)
                    if store:
                        store_z(t - 1, 1 - par)
                    sp.wait_ge(fc_ready, (t + 2) * PAIRS)
                    load_fc(1 - par, fc)

                def routed(t):
                    def weights():
                        e = expert(t)
                        return wproj[bass.ds(e, 1)], wfc[bass.ds(e, 1)]
                    return weights

                body(0, 0, False, routed(2))
                with sp.Fori(0, (BLOCKS - 3) // 2) as i:
                    body(i * 2 + 1, 1, True, routed(i * 2 + 3))
                    body(i * 2 + 2, 0, True, routed(i * 2 + 4))
                body(BLOCKS - 2, 1)
                for n in range(FIRST + BLOCKS, NBLOCKS):
                    sp.wait_ge(xt_full, n)
                    load_x(x_rows, (n - BLOCKS) * BN)
                    if n < FIRST + BLOCKS + 2:
                        t = n - FIRST - 2
                        store_z(t, t % 2)
                for q, (t0, t1) in enumerate(OUT_PARTS):
                    sp.wait_ge(combined, q + 1)
                    sp.dma_start(out.rearrange("b (t p) d -> p (b t) d", p=P)[:, t0:t1], X[:, t0:t1]).then_inc(out_done, 16)
                sp.wait_ge(out_done, 16 * len(OUT_PARTS))

        @block.gpsimd
        def _(pool):
            nc.gpsimd.memset(zeros[:, :], 0.0).then_inc(consts, 1)
            nc.gpsimd.memset(ident[:, :], 0.0).then_inc(c_pool, 1)
            nc.gpsimd.memset(head_rows[:, :], 1.0).then_inc(c_pool, 1)
            nc.gpsimd.memset(neg_half[:, :], -0.5).then_inc(c_pool, 1)
            pool.sem_inc(s_free, S_BANKS)
            pool.sem_inc(t_full, UNITS - NB + 1)
            pool.sem_inc(t_free, T_BANKS)
            pool.sem_inc(pv_done, 2)
            pool.sem_inc(m_free, 1)
            pool.sem_inc(ot_done, 1)
            pool.sem_inc(rows_stored, 16)
            pool.sem_inc(h_act, PAIRS)
            pool.sem_inc(h_ready, PAIRS)
            pool.sem_inc(y_evac, BT)
            pool.sem_inc(y_full, 1)
            pool.sem_inc(z_out[0], 16)
            pool.sem_inc(z_out[1], 16)
            pool.wait_ge(c_pool, 3)
            nc.gpsimd.affine_select(out=ident[:, :], in_=ident[:, :], compare_op=ALU.not_equal, fill=1.0,
                                    base=0, pattern=[[-1, P]], channel_multiplier=1).then_inc(consts, 1)
            nc.gpsimd.affine_select(out=head_rows[:, :], in_=head_rows[:, :], compare_op=ALU.is_ge, fill=0.0,
                                    base=0, pattern=[[-HD, HH]], channel_multiplier=1).then_inc(c_pool, 1)
            pool.wait_ge(c_pool, 4)
            nc.gpsimd.affine_select(out=head_rows[:, :], in_=head_rows[:, :], compare_op=ALU.is_ge, fill=0.0,
                                    base=HD - 1, pattern=[[HD, HH]], channel_multiplier=-1).then_inc(consts, 1)

            nc.gpsimd.memset(e_const[:, :], 2.718281828459045).then_inc(c_pool, 1)
            nc.gpsimd.memset(ones[:, :], 1.0).then_inc(c_pool, 1)
            nc.gpsimd.memset(before_p[:, :], 1.0).then_inc(c_pool, 1)
            nc.gpsimd.memset(before_e[:, :, :], 1.0).then_inc(c_pool, 1)
            nc.gpsimd.iota(iota_e[:, :], pattern=[[1, NE]], base=0, channel_multiplier=0, allow_small_or_imprecise_dtypes=True).then_inc(c_pool, 1)
            nc.gpsimd.iota(iota_b[:, :], pattern=[[1, BLOCKS]], base=0, channel_multiplier=0, allow_small_or_imprecise_dtypes=True).then_inc(c_pool, 1)
            pool.wait_ge(c_pool, 10)
            nc.gpsimd.affine_select(out=before_p[:, :], in_=before_p[:, :], compare_op=ALU.is_gt, fill=0.0,
                                    base=0, pattern=[[1, P]], channel_multiplier=-1).then_inc(c_pool, 1)
            nc.gpsimd.affine_select(out=before_e[:, :, :], in_=before_e[:, :, :], compare_op=ALU.is_gt, fill=0.0,
                                    base=0, pattern=[[1, NE], [-1, NE]], channel_multiplier=0).then_inc(c_pool, 1)

            def power(n):
                pool.wait_ge(veps_ready, n + 1)
                nc.gpsimd.tensor_tensor(rstd[:, :], veps[:, :], neg_half[:, :], ALU.pow).then_inc(rstd_ready, 1)

            low_later = [(0, 1), (1, 0), (1, 1)]
            for n, (b, hf) in enumerate(low_later):
                power(n)
                if n == 0:
                    pool.wait_ge(k_ready, 2)
                nc.gpsimd.tensor_tensor(kb[:, b, 1, hf, :].rearrange("p (h k) -> p h k", k=KV),
                                        k_lo[:, hf, b:b + 1, :].bitcast(FP32).to_broadcast([P, HH, KV]),
                                        head_rows[:, :].unsqueeze(2).to_broadcast([P, HH, KV]), ALU.mult).then_inc(kb_ready[b][hf], 1)
            with pool.Fori(len(low_later), 2 * GROUPS) as n:
                power(n)

            def set_biases(par, e, first=False):
                if not first:
                    nc.gpsimd.tensor_copy(b1_now[:, par, :], b1_t[:, bass.ds(e * HC, HC)])
                nc.gpsimd.tensor_copy(b2_now[:, par, :], b2_all[:, bass.ds(e, 1), :]).then_inc(biases_set, 1)

            pool.wait_ge(ld_b2, 32)
            for par in range(2):
                set_biases(par, NE, True)

            pool.wait_ge(gap_ready, 1)
            nc.gpsimd.tensor_tensor(e_gap[:, :], e_const[:, :], gap[:, :], ALU.pow).then_inc(e_gap_ready, 1)
            pool.wait_ge(x_zero, 16 * -(-ROWS // P // 8))
            pool.wait_ge(pos_ready, 1)
            pool.wait_ge(y2_in, 16)
            for t in range(TILES):
                for k in range(TOPK):
                    nc.gpsimd.indirect_dma_start(out=x_sorted, out_offset=bass.IndirectOffsetOnAxis(ap=pos[:, k, t:t + 1], axis=0),
                                                 in_=y2_all[:, t, :], in_offset=None, bounds_check=ROWS - 1, oob_is_err=False)\
                      .then_inc(scattered, 16)
            def routed_biases(t, par):
                pool.wait_ge(y_evac, (t + FIRST) * BT)
                e = pool.value_load(block_e[0:1, bass.ds(t, 1)], min_val=0, max_val=NE - 1)
                set_biases(par, e)

            pool.wait_ge(blocks_ready, 1)
            with pool.Fori(0, (BLOCKS - 1) // 2) as i:
                for par in range(2):
                    routed_biases(i * 2 + par, (par + ODD) % 2)
            routed_biases(BLOCKS - 1, ODD)
            for n in (FIRST + BLOCKS, FIRST + BLOCKS + 1):
                pool.wait_ge(y_evac, n * BT)
                set_biases(n % 2, NE)
            nc.gpsimd.memset(zg[1][:, :, :], 0.0).then_inc(c_pool, 1)
            pool.wait_ge(c_pool, 13)
            pool.wait_ge(scattered, 16 * TOPK * TILES)
            pool.wait_ge(z_out[ODD], 16 * ((BLOCKS + 1) // 2 + 1))
            pool.wait_ge(z_out[1 - ODD], 16 * (BLOCKS // 2 + 1))
            for j, (t0, t1) in enumerate(OUT_PARTS):
                for t, k in [(t, k) for t in range(t0, t1) for k in range(TOPK)]:
                    nc.gpsimd.indirect_dma_start(out=zg[k][:, t, :], out_offset=None, in_=z_rows,
                                                 in_offset=bass.IndirectOffsetOnAxis(ap=pos[:, k, t:t + 1], axis=0),
                                                 bounds_check=ROWS - 1, oob_is_err=False).then_inc(gathered[j], 16)

        @block.tensor
        def _(pe):
            mm = nc.tensor.matmul
            pe.wait_ge(consts, 2)
            pe.wait_ge(ld_w, 48)
            for i in range(3):
                for k in range(KC):
                    for o in range(KC):
                        last = nc.tensor.transpose(s_bank[i][:, k * D + o * P:k * D + (o + 1) * P], w3[:, i, o, k * P:(k + 1) * P], ident[:, :])
                last.then_inc(prep_full, 1)
            pe.wait_ge(ld_c, 32)
            for k in range(KC):
                bank = (t_bank[2], t_bank[0])[k]
                for b in range(B):
                    nc.tensor.transpose(bank[:, b * KV:b * KV + P], ctx_a[:, b, k * P:(k + 1) * P], ident[:, :])
                    last = nc.tensor.transpose(bank[:, b * KV + P:(b + 1) * KV], ctx_b[:, b, k * P:(k + 1) * P], ident[0:KVR, 0:KVR])
                last.then_inc(prep_full, 1)
            def y_turned(use, y):
                pe.wait_ge(m_free, use + 1)
                for k in range(KC):
                    for j in range(GT):
                        last = nc.tensor.transpose(misc_bank[:, (k * GT + j) * P:(k * GT + j + 1) * P], y[:, j, k * P:(k + 1) * P], ident[:, :])
                last.then_inc(m_full, 1)

            def q_product(use):
                pe.wait_ge(m_free, use + 1)
                for hf in range(HALVES):
                    for k in range(KC):
                        for i, (w, y) in enumerate(((wq_hi, y1t_hi), (wq_lo, y1t_hi), (wq_hi, y1t_lo))):
                            last = mm(misc_bank[:, hf * GN:(hf + 1) * GN], w[:, k, hf * P:(hf + 1) * P], y[:, k, :],
                                      start=k == 0 and i == 0, stop=k == KC - 1 and i == 2)
                last.then_inc(m_full, 1)

            pe.wait_ge(y1_ready, 1)
            y_turned(0, y1)
            pe.wait_ge(wkv_ready, 2)
            pe.wait_ge(ctx_ready, 2)
            for hf in range(HALVES):
                bank = (t_bank[1], pv_bank)[hf]
                for k in range(KC):
                    last = mm(bank[:, 0:B * KV], wk_t[:, k, hf * P:(hf + 1) * P], ctx_t[:, k].rearrange("p b k -> p (b k)"),
                              start=k == 0, stop=k == KC - 1)
                last.then_inc(prep_full, 1)

            pe.wait_ge(wq_ready, 1)
            q_product(1)
            pe.wait_ge(k_ready, 1)
            for bank, r0, n in ((t_bank[0], 0, P), (t_bank[1], P, KVR)):
                for b in range(B):
                    for k in range(KC):
                        last = mm(bank[0:n, b * D:(b + 1) * D], ctx_t[:, k, b, r0:r0 + n], wv_t[:, k, :], start=k == 0, stop=k == KC - 1)
                last.then_inc(prep_full, 1)

            pe.wait_ge(ld_b1, 32)
            nc.tensor.transpose(pv_bank[:, 0:(NE + 1) * HC], b1_rows[:, :], ident[0:(NE + 1) * HC, 0:(NE + 1) * HC]).then_inc(b1_full, 1)

            def scores(g, b, par, u):
                n, i, hf, j = unit(u)
                h0, nh = HEADS[i]
                ql, qh = (q[:, par, hf, j * P:(j + 1) * P] for q in (q_lo, q_hi))
                pe.wait_ge(s_free, g * UNITS + u + 1)
                out = s_bank[u % S_BANKS][:, 0:nh * KV]
                cols = slice(h0 * KV, (h0 + nh) * KV)
                kh = kb[:, bass.ds(b, 1), 0, hf, cols]
                kl = kb[:, bass.ds(b, 1), 1, hf, cols]
                mm(out, qh, kh, start=True, stop=False)
                mm(out, qh, kl, start=False, stop=False)
                mm(out, ql, kh, start=False, stop=False)
                mm(out, ident_r[:, :], mask_big[:, bass.ds(g * GT + j, 1), :].to_broadcast([P, nh, KV]), start=False, stop=True)\
                    .then_inc(s_full, 1)

            def turn(g, v):
                n, i, hf, j = unit(v)
                c0, m = CHUNKS[i]
                pe.wait_ge(s_free, g * UNITS + v + (2 if i < NB - 1 else 1) + S_BANKS)
                pe.wait_ge(t_free, g * UNITS + v + 1)
                for c in range(c0, c0 + m):
                    r = CHROWS[c]
                    last = nc.tensor.transpose(t_bank[v % T_BANKS][0:r, (c - c0) * P:(c - c0 + 1) * P],
                                               prob[:, n, c * P:c * P + r], ident[:, :])
                last.then_inc(t_full, 1)

            def pv(hf, c0, c1):
                for c in range(c0, c1):
                    r = CHROWS[c]
                    for i, (v, p) in enumerate(((vs[0], pt_hi), (vs[1], pt_hi), (vs[0], pt_lo))):
                        last = mm(pv_bank[:, hf * GN:(hf + 1) * GN], v[0:r, hf, c, :], p[0:r, hf, c, :],
                                  start=c == 0 and i == 0, stop=c == NCH - 1 and i == 2)
                if c1 == NCH:
                    last.then_inc(pv_done, 1)

            def pv_inputs(b, hf, turned):
                pe.wait_ge(ld_v[hf], b * 32 + 32)
                pe.wait_ge(t_free, turned + T_BANKS)

            def out_turned(g, use):
                pe.wait_ge(ot_done, g + 1)
                pe.wait_ge(m_free, use + 1)
                for hf in range(HALVES):
                    for j in range(GT):
                        last = nc.tensor.transpose(misc_bank[:, j * D + hf * P:j * D + (hf + 1) * P], ot[:, hf, j * P:(j + 1) * P], ident[:, :])
                last.then_inc(m_full, 1)

            def router_logits(use):
                pe.wait_ge(m_free, use + 1)
                for j in range(GT):
                    for k in range(KC):
                        for i, y in enumerate((y2t_hi, y2t_lo)):
                            last = mm(misc_bank[:, j * 2 * NE:(j + 1) * 2 * NE], y[:, k, j * P:(j + 1) * P],
                                      wr_parts[:, k].rearrange("p a e -> p (a e)"), start=k == 0 and i == 0, stop=k == KC - 1 and i == 1)
                last.then_inc(m_full, 1)

            def body(g, b, b_before, par, before, more):
                base = m_base(g, before)
                pe.wait_ge(q_first, g + 1)
                for u in range(UNITS):
                    if u == UNITS // 2 and not before:
                        pe.wait_ge(kb_ready[0][1], 2)
                    if u == UNITS // 2 and before < 2:
                        pe.wait_ge(m_free, base + 1)
                    if u == Q_UNIT and more:
                        q_product(base)
                    scores(g, b, par, u)
                    if u == 1 and before == 2:
                        pe.wait_ge(y2_ready, g - 1)
                        y_turned(base, y2)
                    if u == 3 and before == 2:
                        router_logits(base + 1)
                        base += 2
                    if u in PV_FIRST and before:
                        pv(0, *PV_FIRST[u])
                    if u in PV_SECOND and before:
                        if PV_SECOND[u][0] == 0:
                            pv_inputs(b_before, 1, g * UNITS)
                        pv(1, *PV_SECOND[u])
                    if u == 6 and more:
                        pe.wait_ge(y1_ready, g + 2)
                        y_turned(base, y1)
                        base += 1
                    if u == 10 and before:
                        out_turned(g, base)
                        base += 1
                    if u == LATE_T and not before:
                        pe.wait_ge(v_added, 2)
                    if u >= LATE_T or before:
                        turn(g, u - LATE_T)
                pe.wait_ge(ot_done, g + 1)
                pv_inputs(b, 0, g * UNITS + UNITS // 2)
                pv(0, 0, PV_FIRST[0][0])

            pe.wait_ge(kb_ready[0][0], 2)
            pe.wait_ge(mask_ready, 1)
            body(0, 0, 0, 0, 0, True)
            body(1, 0, 0, 1, 1, True)
            for hf in range(HALVES):
                pe.wait_ge(kb_ready[1][hf], 2)
            with pe.Fori(1, GROUPS // 2 - 1) as i:
                body(i * 2, (i * 2) // BG, (i * 2 - 1) // BG, 0, 2, True)
                body(i * 2 + 1, (i * 2 + 1) // BG, (i * 2) // BG, 1, 2, True)
            body(GROUPS - 2, B - 1, B - 1, 0, 2, True)
            body(GROUPS - 1, B - 1, B - 1, 1, 2, False)

            def turn_x(n):
                pe.wait_ge(x_in, (n + 1) * 16)
                if not (isinstance(n, int) and n == 0):
                    pe.wait_ge(xt_ready, n)
                for k in range(KC):
                    for i in range(BT):
                        last = nc.tensor.transpose(x_bank[:, (k * BT + i) * P:(k * BT + i + 1) * P], xr[:, i, k * P:(k + 1) * P], ident[:, :])
                last.then_inc(xt_full, 1)

            def first_layer(n, load, pairs):
                pe.wait_ge(xt_ready, n + 1)
                for p in pairs:
                    pe.wait_ge(fc_ready, load * PAIRS + p + 1)
                    pe.wait_ge(h_act, n * PAIRS + p + 1)
                    for c in (0, 1):
                        hid = slice((2 * p + c) * P, (2 * p + c + 1) * P)
                        for k in range(KC):
                            for i, (w, xx) in enumerate(((fc_hi, xt_hi), (fc_lo, xt_hi), (fc_hi, xt_lo))):
                                last = mm(h_bank[p][:, c * BN:(c + 1) * BN], w[:, k, hid], xx[:, k, :],
                                          start=k == 0 and i == 0, stop=k == KC - 1 and i == 2)
                    last.then_inc(h_full, 1)

            def second_layer(n, load, slot, tiles):
                for i in tiles:
                    pe.wait_ge(y_evac, n * BT + i + 1)
                    for c in range(HC):
                        if i == 0 and c % 2 == 0:
                            pe.wait_ge(pj_ready, load * PAIRS + c // 2 + 1)
                            pe.wait_ge(h_ready, n * PAIRS + c // 2 + 1 + H0)
                        for j, (h, w) in enumerate(((ht_hi, pj_hi), (ht_hi, pj_lo), (ht_lo, pj_hi))):
                            last = mm(y_bank[i][:, 0:D], h[:, c, i * P:(i + 1) * P], w[slot][:, c, :], start=c == 0 and j == 0, stop=c == HC - 1 and j == 2)
                    last.then_inc(y_full, 1)

            def block_of(n, load, slot, next_x=True):
                first_layer(n, load, range(PAIRS))
                if next_x:
                    turn_x(n + 1)
                second_layer(n, load, slot, range(BT))

            for u in PV_FIRST:
                pv(0, *PV_FIRST[u])
            for u in range(LATE_T):
                turn(GROUPS, u - LATE_T)
            pe.wait_ge(y2_ready, GROUPS - 1)
            y_turned(M_ALL - 5, y2)
            pv_inputs(B - 1, 1, GROUPS * UNITS)
            turn_x(0)
            pv(1, 0, NCH)
            router_logits(M_ALL - 4)
            first_layer(0, 0, range(0, PAIRS // 2))
            out_turned(GROUPS, M_ALL - 3)
            first_layer(0, 0, range(PAIRS // 2, PAIRS))
            turn_x(1)
            pe.wait_ge(y2_ready, GROUPS)
            y_turned(M_ALL - 2, y2)
            second_layer(0, 0, 0, (0,))
            router_logits(M_ALL - 1)

            def counts():
                pe.wait_ge(counts_in, 1)
                mm(misc_bank[:, 0:P], before_p[:, :], both[:, :, :].rearrange("p t e -> p (t e)"), start=True, stop=True)
                mm(misc_bank[:, P:2 * P], ones[:, :], both[:, :, :].rearrange("p t e -> p (t e)"), start=True, stop=True)\
                    .then_inc(counts_full, 1)

            second_layer(0, 0, 0, (1,))
            counts()
            first_layer(1, 0, range(PAIRS))
            turn_x(2)
            second_layer(1, 0, 0, range(BT))
            with pe.Fori(2, FIRST) as n:
                block_of(n, 0, 0)
            with pe.Fori(0, (BLOCKS - 1) // 2) as i:
                block_of(i * 2 + FIRST, i * 2 + 1, 1)
                block_of(i * 2 + FIRST + 1, i * 2 + 2, 0)
            block_of(FIRST + BLOCKS - 1, BLOCKS, 1)
            with pe.Fori(FIRST + BLOCKS, NBLOCKS - 1) as n:
                block_of(n, LOADS - 1, 0)
            block_of(NBLOCKS - 1, LOADS - 1, 0, False)

        @block.scalar
        def _(act):
            A = nc.scalar.activation
            act.wait_ge(ld_small, 16 * 6)
            A(tg_x[:, :], gate_x[:, :], ACT.Tanh).then_inc(tanh_ready, 1)
            A(tg_f[:, :], gate_f[:, :], ACT.Tanh).then_inc(tanh_ready, 1)

            def hi_of(out, use):
                act.wait_ge(m_full, use + 1)
                A(out, misc_bank[:, :], ACT.Copy).then_inc(m_hi, 1)

            def q_hi_of(use, par):
                act.wait_ge(m_full, use + 1)
                for hf in range(HALVES):
                    last = A(q_hi[:, par, hf, :], misc_bank[:, hf * GN:(hf + 1) * GN], ACT.Identity, bias=bq_neg[:, hf:hf + 1])
                last.then_inc(q_his, 1)

            def kb_low(b, hf):
                for h in range(HH):
                    last = A(kb[:, b, 1, hf, h * KV:(h + 1) * KV], k_lo[:, hf, b, :], ACT.Copy, scale=head_rows[:, h:h + 1])
                last.then_inc(kb_ready[b][hf], 1)

            def exps(g, par, u):
                n, i, hf, j = unit(u)
                h0, nh = HEADS[i]
                if i == 0:
                    act.wait_ge(t_full, g * UNITS + u + 1)
                act.wait_ge(s_max, g * UNITS + u + 1)
                for h in range(h0, h0 + nh):
                    last = A(prob[:, n, h * KV:(h + 1) * KV], s_bank[u % S_BANKS][:, (h - h0) * KV:(h - h0 + 1) * KV], ACT.Exp,
                             bias=negmax[:, par, j, hf, h:h + 1], scale=-1.0, accum_out=psums[:, par, j, hf, h:h + 1])
                last.then_inc(s_free, 1)

            def turned_hi(g, v):
                n, i, hf, j = unit(v)
                c0, m = CHUNKS[i]
                if j == 0 and i == 0:
                    act.wait_ge(pv_done, g * 2 + hf + 1)
                act.wait_ge(t_full, g * UNITS + v + 1 + UNITS - NB + 1)
                for r, a, z in rows(c0, m):
                    last = A(pt_hi[0:r, hf, a:z, j * P:(j + 1) * P],
                             t_bank[v % T_BANKS][0:r, (a - c0) * P:(z - c0) * P].rearrange("p (c q) -> p c q", q=P), ACT.Copy)
                last.then_inc(t_hi, 1)

            def out_copied(g):
                act.wait_ge(pv_done, g * 2 + 2)
                A(ot[:, :, :], pv_bank[:, :], ACT.Copy).then_inc(ot_done, 1)

            def fc_high(p, slot, arrivals):
                act.wait_ge(fc_in[slot], arrivals * 16)
                cols = slice(p * 2 * P, (p + 1) * 2 * P)
                A(fc_hi[:, :, cols], raw_fc[slot][:, :, cols], ACT.Copy).then_inc(fc_his, 1)

            def pj_high(p, slot, arrivals):
                act.wait_ge(pj_in[slot], arrivals * 32)
                A(pj_hi[slot][:, 2 * p:2 * p + 2, :], raw_pj[slot][:, 2 * p:2 * p + 2, :], ACT.Copy).then_inc(pj_his, 1)

            def work_ahead(u):
                if u == 1:
                    for i, (f, h) in enumerate(((v_f, v_hi), (vr_f, vr_hi))):
                        act.wait_ge(v_added, i + 1)
                        A(h[:, :, :], f[:, :, :], ACT.Copy).then_inc(v_hi_ready, 1)

            def body(g, par, before, more, shared_fc=False):
                base = m_base(g, before)
                for u in range(UNITS):
                    if u == 9 and before == 1:
                        act.wait_ge(vx_in[1], VX_WRITES)
                    if u == 9 and before:
                        out_copied(g)
                        base += 1
                    if u == Q_UNIT and more:
                        q_hi_of(base, 1 - par)
                    exps(g, par, u)
                    if shared_fc and u in FC_UNITS:
                        fc_high(u - FC_UNITS[0], 0, 1)
                    if u == 1 and before == 2:
                        hi_of(y2t_hi[:, :, :], base)
                        base += 2
                    if u == 7 and more:
                        hi_of(y1t_hi[:, :, :], base)
                        base += 1
                    if not before:
                        work_ahead(u)
                    if u >= LATE_T or before:
                        turned_hi(g, u - LATE_T)

            for i, w in ((1, wk_t), (2, wv_t)):
                act.wait_ge(prep_full, 1 + i)
                A(w[:, :, :], s_bank[i][:, :], ACT.Copy).then_inc(wkv_ready, 1)
            act.wait_ge(prep_full, 4)
            A(ctx_t[:, 0], t_bank[2][:, 0:B * KV], ACT.Copy).then_inc(ctx_ready, 1)
            hi_of(y1t_hi[:, :, :], 0)
            act.wait_ge(k_ready, 1)
            A(k_hi[:, :, :, :], k_t[:, :, :, :], ACT.Copy).then_inc(k_hi_ready, 1)
            q_hi_of(1, 0)
            act.wait_ge(k_ready, 2)
            act.wait_ge(consts, 3)
            kb_low(0, 0)
            body(0, 0, 0, True)
            body(1, 1, 1, True)
            with act.Fori(1, GROUPS // 2 - 1) as i:
                body(i * 2, 0, 2, True)
                body(i * 2 + 1, 1, 2, True)
            body(GROUPS - 2, 0, 2, True, True)
            body(GROUPS - 1, 1, 2, False)
            def split_x(n):
                act.wait_ge(xt_full, n + 1)
                A(xt_hi[:, :, :], x_bank[:, :].rearrange("p (k n) -> p k n", k=KC), ACT.Copy).then_inc(xt_his, 1)

            def hidden(n, par, p, biases):
                if p == 0 and biases is not None:
                    act.wait_ge(biases_set, biases)
                act.wait_ge(h_full, n * PAIRS + p + 1)
                act.wait_ge(h_ready, n * PAIRS + p + 1)
                for c in (0, 1):
                    last = A(h_f[:, p, c, :], h_bank[p][:, c * BN:(c + 1) * BN], ACT.Gelu_apprx_tanh,
                             bias=b1_now[:, par, 2 * p + c:2 * p + c + 1])
                last.then_inc(h_act, 1)

            def block_of(n, par, biases, following=None, next_x=True):
                if following:
                    act.wait_ge(y_full, n * BT + 1)
                    pj_high(0, *following)
                    pj_high(1, *following)
                for p in range(PAIRS):
                    hidden(n, par, p, biases)
                    if following and p < 2:
                        pj_high(p + 2, *following)
                if next_x:
                    split_x(n + 1)
                if following:
                    for p in range(PAIRS):
                        fc_high(p, *following)

            for u in range(LATE_T):
                turned_hi(GROUPS, u - LATE_T)
            hi_of(y2t_hi[:, :, :], M_ALL - 5)
            split_x(0)
            for p in range(PAIRS):
                pj_high(p, 0, 1)
            out_copied(GROUPS)
            for p in range(PAIRS):
                hidden(0, 0, p, None)
            hi_of(y2t_hi[:, :, :], M_ALL - 2)
            split_x(1)
            for n in range(1, FIRST):
                block_of(n, n % 2, None, (1, 1) if n == FIRST - 1 else None)
            with act.Fori(0, (BLOCKS - 1) // 2) as i:
                block_of(i * 2 + FIRST, ODD, i * 2 + 3, (0, i + 2))
                block_of(i * 2 + 1 + FIRST, 1 - ODD, i * 2 + 4, (1, i + 2))
            block_of(FIRST + BLOCKS - 1, ODD, BLOCKS + 2, (0, (LOADS + 1) // 2))
            for n in range(FIRST + BLOCKS, NBLOCKS):
                block_of(n, n % 2, biases_of(n), None, n < NBLOCKS - 1)

        @block.vector
        def _(dve):
            V = nc.vector
            count = [0, 0]

            def link(ins):
                count[1] += 1
                ins.then_inc(dv, 1)
                dve.wait_ge(dv, count[0] + count[1])

            def norm_stats(tile):
                V.memset(wait_taker[:, :], 0.0)
                for j in range(GT):
                    last = V.bn_stats(stats[:, j, :], tile(j))
                link(last)
                V.memset(wait_taker[:, :], 0.0)
                for j in range(GT):
                    last = V.bn_aggr(mv[:, j, :], stats[:, j, :])
                link(last)
                V.tensor_scalar(veps[:, :], mv[:, :, 1], EPS, None, ALU.add).then_inc(veps_ready, 1)

            def norm(tile, n, out, ready):
                dve.wait_ge(rstd_ready, n)
                for j in range(GT):
                    last = V.tensor_scalar(out[:, j, :], tile(j), mv[:, j, 0:1], rstd[:, j:j + 1],
                                           ALU.subtract, ALU.mult)
                last.then_inc(ready, 1)

            def lo_of(out, hi, n):
                dve.wait_ge(m_hi, n)
                V.tensor_tensor(out, misc_bank[:, :], hi.bitcast(FP32), ALU.subtract).then_inc(m_free, 1)

            def q_lo_of(g, par):
                dve.wait_ge(q_his, g + 1)
                for hf in range(HALVES):
                    last = V.scalar_tensor_tensor(q_lo[:, par, hf, :], misc_bank[:, hf * GN:(hf + 1) * GN], bq_neg[:, hf:hf + 1],
                                                  q_hi[:, par, hf, :].bitcast(FP32), ALU.add, ALU.subtract)
                    if hf == 0:
                        last.then_inc(q_first, 1)
                last.then_inc(m_free, 1)

            def kb_high(b, hf):
                V.tensor_tensor(kb[:, b, 0, hf, :].rearrange("p (h k) -> p h k", k=KV),
                                k_hi[:, hf, b:b + 1, :].bitcast(FP32).to_broadcast([P, HH, KV]),
                                head_rows[:, :].unsqueeze(2).to_broadcast([P, HH, KV]), ALU.mult).then_inc(kb_ready[b][hf], 1)

            def maxima(g, par, u):
                n, i, hf, j = unit(u)
                h0, nh = HEADS[i]
                dve.wait_ge(s_full, g * UNITS + u + 1)
                V.tensor_reduce(negmax[:, par, j, hf, h0:h0 + nh], s_bank[u % S_BANKS][:, 0:nh * KV].rearrange("p (h k) -> p h k", k=KV),
                                axis=AX.X, op=ALU.min).then_inc(s_max, 1)

            def turned_lo(g, v):
                n, i, hf, j = unit(v)
                c0, m = CHUNKS[i]
                dve.wait_ge(t_hi, g * UNITS + v + 1)
                for r, a, z in rows(c0, m):
                    cols = slice(j * P, (j + 1) * P)
                    last = V.tensor_tensor(pt_lo[0:r, hf, a:z, cols],
                                           t_bank[v % T_BANKS][0:r, (a - c0) * P:(z - c0) * P].rearrange("p (c q) -> p c q", q=P),
                                           pt_hi[0:r, hf, a:z, cols].bitcast(FP32), ALU.subtract)
                last.then_inc(t_free, 1)

            rden_all = rden[:, :, :, :].rearrange("p t a h -> p t (a h)")

            def denominators(par):
                link(V.tensor_scalar(some[:, :], negmax[:, par, :, 0, 0], MASKED / 10, None, ALU.is_lt))
                keep = some[:, :].unsqueeze(2).to_broadcast([P, GT, H])
                link(V.tensor_tensor(rden_all, psums[:, par].rearrange("p t a h -> p t (a h)"), keep, ALU.mult))
                link(V.reciprocal(rden_all, rden_all))
                link(V.tensor_tensor(rden_all, rden_all, keep, ALU.mult))

            def group_out(g, use):
                dve.wait_ge(m_full, use + 1)
                V.tensor_tensor(att[:, :, :].rearrange("p t (h d) -> p t h d", d=HD),
                                misc_bank[:, :].rearrange("p (t h d) -> p t h d", t=GT, d=HD),
                                rden_all.unsqueeze(3).to_broadcast([P, GT, H, HD]), ALU.mult).then_inc(m_free, 1)
                dve.wait_ge(m_free, use + 2)
                xg = X[:, bass.ds(g * GT, GT), :]
                link(V.scalar_tensor_tensor(xg, att[:, :, :], tg_x[:, 0:1], xg, ALU.mult, ALU.add))

            def tiles_of(g):
                return lambda j: X[:, bass.ds(g * GT + j, 1), :]

            def second_norm(g, power):
                dve.wait_ge(rows_stored, g * 16 + 16)
                norm(tiles_of(g), power, y2, y2_ready)

            def fc_low(p, load, slot):
                cols = slice(p * 2 * P, (p + 1) * 2 * P)
                dve.wait_ge(fc_his, load * PAIRS + p + 1)
                V.tensor_tensor(fc_lo[:, :, cols], raw_fc[slot][:, :, cols], fc_hi[:, :, cols].bitcast(FP32), ALU.subtract)\
                 .then_inc(fc_ready, 1)

            def body(g, par, before, more, shared_fc=False):
                base, hi = m_base(g, before), hi_base(g, before)
                for u in range(UNITS):
                    if u == Q_UNIT and more:
                        q_lo_of(g + 1, 1 - par)
                    maxima(g, par, u)
                    if u == 0 and before == 2:
                        second_norm(g - 2, g * 2)
                    if u == 2 and before == 2:
                        lo_of(y2t_lo[:, :, :], y2t_hi[:, :, :], hi + 1)
                        hi += 1
                    if u == 5 and before == 2:
                        logits_of(g - 2, base + 1)
                        base += 2
                    if u == 3 and before == 1:
                        dve.wait_ge(ld_x_rest, 16 * (GROUPS - 2))
                    if u == 10 and before == 1:
                        dve.wait_ge(tanh_ready, 1)
                        dve.wait_ge(vx_in[1], VX_WRITES)
                    if u == (3 if before else 4) and more:
                        norm_stats(tiles_of(g + 1))
                    if u == 5 and more:
                        norm(tiles_of(g + 1), g * 2 + 1 if before else 2, y1, y1_ready)
                    if u == 7 and before:
                        denominators(1 - par)
                    if u == 8 and more:
                        lo_of(y1t_lo[:, :, :], y1t_hi[:, :, :], hi + 1)
                        base += 1
                        hi += 1
                    if u == 10 and before:
                        group_out(g - 1, base)
                    if not before:
                        work_ahead(u)
                    if u >= LATE_LO or before:
                        turned_lo(g, u - LATE_LO)
                    if shared_fc and u - 1 in FC_UNITS:
                        fc_low(u - 1 - FC_UNITS[0], 0, 0)
                    if u == 11 and before:
                        norm_stats(tiles_of(g - 1))

            def logits_of(g, use):
                dve.wait_ge(m_full, use + 1)
                sums = misc_bank[:, 0:GT * 2 * NE].rearrange("p (t a e) -> p t e a", t=GT, a=2)
                V.tensor_reduce(logits[:, bass.ds(g * GT, GT), :], sums, axis=AX.X, op=ALU.add).then_inc(m_free, 1)

            dve.wait_ge(ld_x, 16)
            norm_stats(lambda j: X[:, j, :])
            dve.wait_ge(consts, 2)
            V.tensor_copy(ident_r[:, :], ident[:, :])
            dve.wait_ge(ld_small, 16 * 6)
            V.tensor_scalar(bq_neg[:, :], bq_col[:, :], SQ, None, ALU.mult)
            norm(lambda j: X[:, j, :], 1, y1, y1_ready)
            dve.wait_ge(prep_full, 1)
            link(V.tensor_scalar(wq_hi[:, :, :], s_bank[0][:, :], SQ, None, ALU.mult))
            V.scalar_tensor_tensor(wq_lo[:, :, :], s_bank[0][:, :], SQ, wq_hi[:, :, :].bitcast(FP32), ALU.mult, ALU.subtract).then_inc(wq_ready, 1)
            dve.wait_ge(prep_full, 5)
            V.tensor_copy(ctx_t[:, 1], t_bank[0][:, 0:B * KV]).then_inc(ctx_ready, 1)
            lo_of(y1t_lo[:, :, :], y1t_hi[:, :, :], 1)
            dve.wait_ge(ld_m, 16)
            V.tensor_scalar(mask_big[:, :, :], mask_i[:, :, :], 1.0, MASKED, ALU.is_equal, ALU.mult).then_inc(mask_ready, 1)
            for hf, bank in enumerate((t_bank[1], pv_bank)):
                dve.wait_ge(prep_full, 6 + hf)
                last = V.tensor_scalar(k_t[:, hf], bank[:, 0:B * KV].rearrange("p (b k) -> p b k", b=B), bk_col[:, hf:hf + 1], None, ALU.add)
            last.then_inc(k_ready, 1)
            dve.wait_ge(k_hi_ready, 1)
            V.tensor_tensor(k_lo[:, :, :, :], k_t[:, :, :, :], k_hi[:, :, :, :].bitcast(FP32), ALU.subtract).then_inc(k_ready, 1)
            dve.wait_ge(consts, 3)
            kb_high(0, 0)
            q_lo_of(0, 0)

            def work_ahead(u):
                if u == 0:
                    for i, (f, bank, r) in enumerate(((v_f, t_bank[0], P), (vr_f, t_bank[1], KVR))):
                        dve.wait_ge(prep_full, 8 + i)
                        for b in range(B):
                            last = V.tensor_tensor(f[:, b], bank[0:r, b * D:(b + 1) * D], bv_row[0:r, :], ALU.add)
                        last.then_inc(v_added, 1)
                if u == 1:
                    for i, (f, h, l) in enumerate(((v_f, v_hi, v_lo), (vr_f, vr_hi, vr_lo))):
                        dve.wait_ge(v_hi_ready, i + 1)
                        V.tensor_tensor(l[:, :, :], f[:, :, :], h[:, :, :].bitcast(FP32), ALU.subtract).then_inc(v_ready, 1)
                    link(V.tensor_copy(wr_parts[:, :, 0, :], wr_raw[:, :, :]))
                    V.tensor_tensor(wr_parts[:, :, 1, :], wr_raw[:, :, :], wr_parts[:, :, 0, :].bitcast(FP32), ALU.subtract)
                if u == 2:
                    dve.wait_ge(b1_full, 1)
                    link(V.tensor_copy(b1_t[:, :], pv_bank[:, 0:(NE + 1) * HC]))
                    for par in range(2):
                        V.tensor_copy(b1_now[:, par, :], b1_t[:, NE * HC:])
                    kb_high(0, 1)
                if u == 3:
                    dve.wait_ge(ld_x_next, 16)
                if u in (6, 9):
                    kb_high(1, (u - 6) // 3)

            NORM, LINKS = 4, 9
            ahead = count[1]
            body(0, 0, 0, True)
            assert count[1] == ahead + NORM, count

            def at(g):
                count[0], count[1] = g * LINKS + (ahead + NORM - LINKS), 0

            body(1, 1, 1, True)
            with dve.Fori(1, GROUPS // 2 - 1) as i:
                for par in range(2):
                    at(i * 2 + par)
                    body(i * 2 + par, par, 2, True)
                    assert count[1] == LINKS, count
            at(GROUPS - 2)
            body(GROUPS - 2, 0, 2, True, True)
            body(GROUPS - 1, 1, 2, False)
            def pj_low(p, load, slot):
                dve.wait_ge(pj_his, load * PAIRS + p + 1)
                chunks = slice(2 * p, 2 * p + 2)
                V.tensor_tensor(pj_lo[slot][:, chunks, :], raw_pj[slot][:, chunks, :], pj_hi[slot][:, chunks, :].bitcast(FP32), ALU.subtract)\
                 .then_inc(pj_ready, 1)

            def split_x(n):
                dve.wait_ge(xt_his, n + 1)
                V.tensor_tensor(xt_lo[:, :, :], x_bank[:, :].rearrange("p (k n) -> p k n", k=KC), xt_hi[:, :, :].bitcast(FP32),
                                ALU.subtract).then_inc(xt_ready, 1)

            def hidden(n, p, between=None):
                pair = slice(2 * p, 2 * p + 2)
                dve.wait_ge(h_act, n * PAIRS + p + 1 + H0)
                if p == 0:
                    dve.wait_ge(y_full, n * BT + 1)
                V.tensor_copy(ht_hi[:, pair, :], h_f[:, p]).then_inc(dv, 1)
                count[1] += 1
                if between:
                    between()
                dve.wait_ge(dv, count[0] + count[1])
                V.tensor_tensor(ht_lo[:, pair, :], h_f[:, p], ht_hi[:, pair, :].bitcast(FP32), ALU.subtract).then_inc(h_ready, 1)

            def outputs(n, par, i):
                dve.wait_ge(y_full, n * BT + i + 2)
                V.tensor_tensor(y_sb[:, par, i, :], y_bank[i][:, 0:D], b2_now[:, par, :], ALU.add).then_inc(y_evac, 1)

            def add_shared(n, par):
                dve.wait_ge(y_evac, n * BT + BT + BT)
                t = (n if n < FIRST else n - BLOCKS) * BT
                return V.scalar_tensor_tensor(X[:, t:t + BT, :], y_sb[:, par], tg_f[:, 0:1], X[:, t:t + BT, :], ALU.mult, ALU.add)

            def block_of(n, par, biases, own=None, following=None, next_x=True, stored=None, job=None, job_last=None):
                def pj(p):
                    if following:
                        pj_low(p, *following)

                if own:
                    fc_low(PAIRS - 1, *own)
                pj(0)
                pj(1)
                hidden(n, 0, lambda: pj(2))
                hidden(n, 1)
                hidden(n, 2)
                hidden(n, 3)
                pj(3)
                if next_x:
                    split_x(n + 1)
                if job:
                    job()
                if following:
                    fc_low(0, *following)
                    fc_low(1, *following)
                if stored is not None:
                    dve.wait_ge(z_out[par], stored * 16 + 16)
                if job_last:
                    job_last()
                dve.wait_ge(biases_set, biases)
                outputs(n, par, 0)
                if following:
                    fc_low(2, *following)
                outputs(n, par, 1)

            def best(t0, t1):
                for t in range(t0, t1):
                    last = V.max(top[:, t, :], logits[:, t, :])
                link(last)
                for t in range(t0, t1):
                    last = V.max_index(top_i[:, t, :], top[:, t, :], logits[:, t, :])
                return last

            def choices():
                link(best(TILES - GT, TILES))
                V.tensor_tensor(gap[:, :], top[:, :, 1], top[:, :, 0], ALU.subtract).then_inc(gap_ready, 1)
                link(V.tensor_copy(top_f[:, :, :], top_i[:, :, 0:TOPK].rearrange("p t k -> p k t")))
                for k in range(TOPK):
                    last = V.tensor_tensor(chosen[:, k], top_f[:, k, :].unsqueeze(2).to_broadcast([P, TILES, NE]),
                                           iota_e[:, :].unsqueeze(1).to_broadcast([P, TILES, NE]), ALU.is_equal)
                link(last)
                V.tensor_tensor(both[:, :, :], chosen[:, 0], chosen[:, 1], ALU.add).then_inc(counts_in, 1)

            def places():
                V.memset(cum[0][:, 0, :], 0.0)
                V.memset(cum[1][:, 0, :], 0.0)
                V.tensor_scalar(thresholds[:, :], iota_e[:, :], float(BN), None, ALU.mult)
                link(V.tensor_reduce(none_f[:, :, :], chosen[:, :, :, :], axis=AX.X, op=ALU.add))
                V.tensor_scalar(none_f[:, :, :], none_f[:, :, :], -float(ROWS), float(ROWS), ALU.mult, ALU.add)
                dve.wait_ge(counts_full, 1)
                link(V.tensor_copy(cum[0][:, 1:, :], misc_bank[:, P:2 * P]))
                a, z = cum
                for s in (1, 2, 4, 8):
                    V.tensor_copy(z[:, 1:1 + s, :], a[:, 1:1 + s, :])
                    link(V.tensor_tensor(z[:, 1 + s:, :], a[:, 1 + s:, :], a[:, 1:TILES + 1 - s, :], ALU.add))
                    a, z = z, a
                link(V.tensor_tensor(over[:, :, :], a[:, TILES, :].unsqueeze(2).to_broadcast([P, NE, NE]),
                                     thresholds[:, :].unsqueeze(1).to_broadcast([P, NE, NE]), ALU.is_gt))
                link(V.tensor_reduce(blocks_of[:, :], over[:, :, :], axis=AX.X, op=ALU.add))
                link(V.tensor_tensor(over[:, :, :], before_e[:, :, :], blocks_of[:, :].unsqueeze(1).to_broadcast([P, NE, NE]), ALU.mult))
                link(V.tensor_reduce(start[:, :], over[:, :, :], axis=AX.X, op=ALU.add))
                V.tensor_tensor(end[:, :], start[:, :], blocks_of[:, :], ALU.add)
                V.tensor_tensor(slot[:, :, :], misc_bank[:, 0:P].rearrange("p (t e) -> p t e", e=NE), a[:, 0:TILES, :], ALU.add)
                link(V.tensor_scalar(thresholds[:, :], start[:, :], float(BN), None, ALU.mult))
                link(V.tensor_tensor(slot[:, :, :], slot[:, :, :], thresholds[:, :].unsqueeze(1).to_broadcast([P, TILES, NE]), ALU.add))
                for k in range(TOPK):
                    last = V.tensor_tensor(work[:, k], chosen[:, k], slot[:, :, :], ALU.mult)
                link(last)
                link(V.tensor_reduce(pos_f[:, :, :], work[:, :, :, :], axis=AX.X, op=ALU.add))
                V.tensor_tensor(pos[:, :, :], pos_f[:, :, :], none_f[:, :, :], ALU.add).then_inc(pos_ready, 1)
                link(V.tensor_tensor(passed[:, :, :], end[:, :].unsqueeze(1).to_broadcast([P, BLOCKS, NE]),
                                     iota_b[:, :].unsqueeze(2).to_broadcast([P, BLOCKS, NE]), ALU.is_le))
                link(V.tensor_reduce(block_f[:, :], passed[:, :, :], axis=AX.X, op=ALU.add))
                V.tensor_scalar(block_e[:, :], block_f[:, :], float(NE - 1), None, ALU.min).then_inc(blocks_ready, 1)

            def gates_of():
                dve.wait_ge(e_gap_ready, 1)
                link(V.tensor_scalar(gap[:, :], e_gap[:, :], 1.0, None, ALU.add))
                link(V.reciprocal(gap[:, :], gap[:, :]))
                link(V.tensor_scalar(gates[:, 0, :], gap[:, :], tg_f[:, 0:1], None, ALU.mult))
                link(V.tensor_tensor(gates[:, 1, :], gates[:, 0, :], e_gap[:, :], ALU.mult))

            dve.wait_ge(c_pool, 12)
            second_norm(GROUPS - 2, 2 * GROUPS - 1)
            for u in range(LATE_LO):
                turned_lo(GROUPS, u - LATE_LO)
            lo_of(y2t_lo[:, :, :], y2t_hi[:, :, :], 2 * GROUPS - 1)
            split_x(0)
            denominators(1)
            for p in range(PAIRS):
                pj_low(p, 0, 0)
            logits_of(GROUPS - 2, M_ALL - 4)
            dve.wait_ge(m_free, M_ALL - 2)
            best(0, TILES - GT)
            group_out(GROUPS - 1, M_ALL - 3)
            norm_stats(tiles_of(GROUPS - 1))
            hidden(0, 0)
            second_norm(GROUPS - 1, 2 * GROUPS)
            for p in range(1, PAIRS):
                hidden(0, p)
            lo_of(y2t_lo[:, :, :], y2t_hi[:, :, :], 2 * GROUPS)
            split_x(1)
            dve.wait_ge(biases_set, biases_of(0))
            outputs(0, 0, 0)
            logits_of(GROUPS - 1, M_ALL - 1)
            dve.wait_ge(m_free, M_ALL + 1)
            choices()
            outputs(0, 0, 1)
            places()
            add_shared(0, 0)
            block_of(1, 1, biases_of(1))
            add_shared(1, 1)
            for n in range(2, FIRST - 1):
                block_of(n, n % 2, biases_of(n), job=gates_of if n == 2 else None)
                add_shared(n, n % 2)
            block_of(FIRST - 1, 1 - ODD, biases_of(FIRST - 1), None, (1, 1))
            link(add_shared(FIRST - 1, 1 - ODD))
            links = sum(count)
            with dve.Fori(0, (BLOCKS - 1) // 2) as i:
                for par in range(2):
                    t = i * 2 + par
                    count[0], count[1] = t * PAIRS + links, 0
                    block_of(t + FIRST, (par + ODD) % 2, t + 3, (t + 1, 1 - par), (t + 2, par), True, i)
            count[0], count[1] = (BLOCKS - 1) * PAIRS + links, 0
            block_of(FIRST + BLOCKS - 1, ODD, BLOCKS + 2, (BLOCKS, 1), (LOADS - 1, 0), True, BLOCKS // 2)

            def combine(j):
                t0, t1 = OUT_PARTS[j]
                dve.wait_ge(gathered[j], 16 * TOPK * (t1 - t0))
                for k in range(TOPK):
                    for t in range(t0, t1):
                        last = V.scalar_tensor_tensor(X[:, t, :], zg[k][:, t, :], gates[:, k, t:t + 1], X[:, t, :], ALU.mult, ALU.add)
                    if k == 0:
                        link(last)
                last.then_inc(combined, 1)

            for n in range(FIRST + BLOCKS, NBLOCKS):
                m = n - FIRST - BLOCKS
                par = n % 2
                block_of(n, par, biases_of(n), (LOADS - 1, 0) if m == 0 else None, None, n < NBLOCKS - 1,
                         (BLOCKS + 1 - (par + ODD) % 2) // 2, job=(lambda: combine(m - 1)) if m > 0 else None)
                link(add_shared(n, par))
            for j in range(NBLOCKS - FIRST - BLOCKS - 1, len(OUT_PARTS)):
                combine(j)

    return nc


_INS = ['x', 'ctx_1024', 'mask_BxSxS2_ik1', 'g_xattn', 'g_ffn', 'L0_xattn_Wq', 'L0_xattn_bq', 'L0_xattn_Wk', 'L0_xattn_bk',
        'L0_xattn_Wv', 'L0_xattn_bv', 'L0_ffn_Wfc_s', 'L0_ffn_bfc_s', 'L0_ffn_Wproj_s', 'L0_ffn_bproj_s', 'L0_ffn_Wr',
        'L0_ffn_Wfc', 'L0_ffn_bfc', 'L0_ffn_Wproj', 'L0_ffn_bproj']
_OUTS = [((B, T, D), 'float32')]


def kernel(**inputs):
    import numpy as _np
    import concourse.bacc as _bacc
    from concourse import mybir as _mybir
    from concourse.bass_utils import run_bass_kernel_spmd as _run

    nc = _bacc.Bacc("TRN2", target_bir_lowering=False, num_devices=1)
    arrays, args = {}, []
    for name in _INS:
        a = _np.ascontiguousarray(inputs[name])
        arrays[f"in_{name}_dram"] = a
        args.append(nc.dram_tensor(f"in_{name}_dram", a.shape, _mybir.dt.from_np(a.dtype), kind="ExternalInput").ap())
    for i, (shape, dtype) in enumerate(_OUTS):
        dt = _mybir.dt.from_np(_np.dtype(dtype))
        args.append(nc.dram_tensor(f"out_{i}_dram", shape, dt, kind="ExternalOutput").ap())
    build(nc, *args)
    r = _run(nc, [arrays], core_ids=[0])
    return r.results[0]["out_0_dram"]
```
